# Optimizing a Trainium2 kernel written in Bass

```python
import numpy as np
import jax
import jax.numpy as jnp

def _softmax(x, axis=-1):
    return jax.nn.softmax(x, axis=axis)

def _gelu(x):
    return jax.nn.gelu(x, approximate=True)

def _silu(x):
    return jax.nn.silu(x)

def _sigmoid(x):
    return jax.nn.sigmoid(x)

def _layernorm(x, axis=-1, eps=1e-05):
    m = jnp.mean(x, axis=axis, keepdims=True)
    v = jnp.var(x, axis=axis, keepdims=True)
    return (x - m) / jnp.sqrt(v + eps)

def _scatter_add(tgt, idx, src, axis=0):
    return tgt.at[idx].add(src)

def _segment_sum(src, seg, n):
    return jax.ops.segment_sum(src, seg, n)
kernel_name = 'mk_lm_tower_d1_tok_ids4096_r4_14cf9e'

def setup_inputs(seed: int=0):
    np.random.seed(seed)
    _w = jnp.asarray

    def _rec_inputs():
        import jax
        import jax.numpy as jnp
        _rk = jax.random.key(seed)
        x = jax.random.randint(jax.random.fold_in(_rk, 1), (8, 512), 0, 31999, jnp.int32)
        return x
    x = _rec_inputs()

    def _L0_tok_setup():
        import jax, jax.numpy as jnp
        import numpy as np
        VOCAB, D, N_IDS, INNER = (8000, 1024, 64, 16)
        N, L = (4, 1024)
        key = jax.random.key(seed)
        ks = jax.random.split(key, 8)
        inp = {'input_ids': jax.random.randint(ks[0], (N, L), 0, VOCAB, dtype=jnp.int32), 'ids': jnp.arange(N_IDS, dtype=jnp.int32), 'orig_W': jax.random.normal(ks[1], (VOCAB, D), dtype=jnp.float32) * 0.02, 'trainable_W': jax.random.normal(ks[2], (N_IDS, D), dtype=jnp.float32) * 0.02, 'A_w': jax.random.normal(ks[3], (INNER, D), dtype=jnp.float32) * 0.02, 'A_b': jax.random.normal(ks[4], (INNER,), dtype=jnp.float32) * 0.02, 'B_w': jax.random.normal(ks[5], (D, INNER), dtype=jnp.float32) * 0.02, 'B_b': jax.random.normal(ks[6], (D,), dtype=jnp.float32) * 0.02}
        return inp
    _L0_tok_all = _L0_tok_setup()
    _L0_tok_in = {k: v for k, v in _L0_tok_all.items() if k in ('ids', 'orig_W', 'trainable_W', 'A_w', 'A_b', 'B_w', 'B_b')}
    del _L0_tok_all

    def _L0_attn_setup():
        import jax, jax.numpy as jnp
        import numpy as np
        H = 1024
        D = 2048
        N = 16
        K = 4
        R = 64
        BATCH = 1
        L = 512
        EPS = 1e-06

        def _rmsnorm(x, w):
            return x * jax.lax.rsqrt(jnp.mean(x * x, axis=-1, keepdims=True) + EPS) * w
        key = jax.random.key(seed)
        ks = jax.random.split(key, 10)
        s = 0.02
        return {'hidden_states': jax.random.normal(ks[0], (BATCH, L, H), jnp.float32), 'W_in': jax.random.normal(ks[1], (2 * D, H), jnp.float32) * s, 'conv_w': jax.random.normal(ks[2], (D, K), jnp.float32) * s, 'conv_b': jax.random.normal(ks[3], (D,), jnp.float32) * s, 'Wx': jax.random.normal(ks[4], (R + 2 * N, D), jnp.float32) * s, 'dt_ln_w': jnp.ones((R,), jnp.float32), 'b_ln_w': jnp.ones((N,), jnp.float32), 'c_ln_w': jnp.ones((N,), jnp.float32), 'Wdt': jax.random.normal(ks[5], (D, R), jnp.float32) * s, 'dt_bias': jax.random.normal(ks[6], (D,), jnp.float32) * s, 'A': -jnp.exp(jax.random.normal(ks[7], (D, N), jnp.float32) * 0.5), 'D_param': jnp.ones((D,), jnp.float32), 'W_out': jax.random.normal(ks[8], (H, D), jnp.float32) * s}
    _L0_attn_all = _L0_attn_setup()
    _L0_attn_in = {k: v for k, v in _L0_attn_all.items() if k in ('W_in', 'conv_w', 'conv_b', 'Wx', 'dt_ln_w', 'b_ln_w', 'c_ln_w', 'Wdt', 'dt_bias', 'A', 'D_param', 'W_out')}
    del _L0_attn_all

    def _L0_ffn_setup():
        import jax, jax.numpy as jnp
        import numpy as np
        IN_F = 1024
        OUT_F = 1024
        RANK = 8
        NUM_EXPERTS = 64
        TOP_K = 16
        ROUTER_DIM = 16
        ALPHA = 32
        SCALING = ALPHA / TOP_K
        BOTTLENECK = NUM_EXPERTS * RANK
        key = jax.random.key(seed)
        ks = jax.random.split(key, 5)
        x = jax.random.normal(ks[0], (4, 1024, IN_F), dtype=jnp.float32)
        bound_a = float(np.sqrt(6.0 / IN_F))
        A_w = jax.random.uniform(ks[1], (BOTTLENECK, IN_F), jnp.float32, -bound_a, bound_a)
        B_w = jax.random.normal(ks[2], (OUT_F, BOTTLENECK), dtype=jnp.float32) * 0.02
        Wq_w = jax.random.normal(ks[3], (ROUTER_DIM, IN_F), dtype=jnp.float32) * 0.02
        keys = jax.random.normal(ks[4], (NUM_EXPERTS, ROUTER_DIM), dtype=jnp.float32) * 0.01
        return {'x': x, 'A_w': A_w, 'B_w': B_w, 'Wq_w': Wq_w, 'keys': keys}
    _L0_ffn_all = _L0_ffn_setup()
    _L0_ffn_in = {k: v for k, v in _L0_ffn_all.items() if k in ('A_w', 'B_w', 'Wq_w', 'keys')}
    del _L0_ffn_all
    return {'x': x, 'L0_tok_ids': _L0_tok_in['ids'], 'L0_tok_orig_W': _L0_tok_in['orig_W'], 'L0_tok_trainable_W': _L0_tok_in['trainable_W'], 'L0_tok_A_w': _L0_tok_in['A_w'], 'L0_tok_A_b': _L0_tok_in['A_b'], 'L0_tok_B_w': _L0_tok_in['B_w'], 'L0_tok_B_b': _L0_tok_in['B_b'], 'L0_attn_W_in': _L0_attn_in['W_in'], 'L0_attn_conv_w': _L0_attn_in['conv_w'], 'L0_attn_conv_b': _L0_attn_in['conv_b'], 'L0_attn_Wx': _L0_attn_in['Wx'], 'L0_attn_dt_ln_w': _L0_attn_in['dt_ln_w'], 'L0_attn_b_ln_w': _L0_attn_in['b_ln_w'], 'L0_attn_c_ln_w': _L0_attn_in['c_ln_w'], 'L0_attn_Wdt': _L0_attn_in['Wdt'], 'L0_attn_dt_bias': _L0_attn_in['dt_bias'], 'L0_attn_A': _L0_attn_in['A'], 'L0_attn_D_param': _L0_attn_in['D_param'], 'L0_attn_W_out': _L0_attn_in['W_out'], 'L0_ffn_A_w': _L0_ffn_in['A_w'], 'L0_ffn_B_w': _L0_ffn_in['B_w'], 'L0_ffn_Wq_w': _L0_ffn_in['Wq_w'], 'L0_ffn_keys': _L0_ffn_in['keys']}

def reference(x, L0_tok_ids, L0_tok_orig_W, L0_tok_trainable_W, L0_tok_A_w, L0_tok_A_b, L0_tok_B_w, L0_tok_B_b, L0_attn_W_in, L0_attn_conv_w, L0_attn_conv_b, L0_attn_Wx, L0_attn_dt_ln_w, L0_attn_b_ln_w, L0_attn_c_ln_w, L0_attn_Wdt, L0_attn_dt_bias, L0_attn_A, L0_attn_D_param, L0_attn_W_out, L0_ffn_A_w, L0_ffn_B_w, L0_ffn_Wq_w, L0_ffn_keys):
    import jax
    import jax.numpy as jnp

    def _L0_tok_ref(input_ids, ids, orig_W, trainable_W, A_w, A_b, B_w, B_b):
        import jax, jax.numpy as jnp
        import numpy as np
        VOCAB, D, N_IDS, INNER = (8000, 1024, 64, 16)
        N, L = (4, 1024)
        hit = input_ids[..., None] == ids
        mask = jnp.any(hit, axis=-1)
        idx = jnp.argmax(hit, axis=-1)
        base = orig_W[input_ids]
        h = trainable_W @ A_w.T + A_b
        delta_table = h @ B_w.T + B_b
        delta = delta_table[idx]
        out = base + jnp.where(mask[..., None], delta, jnp.zeros((), base.dtype))
        return out

    def _L0_attn_ref(hidden_states, W_in, conv_w, conv_b, Wx, dt_ln_w, b_ln_w, c_ln_w, Wdt, dt_bias, A, D_param, W_out):
        import jax, jax.numpy as jnp
        import numpy as np
        H = 1024
        D = 2048
        N = 16
        K = 4
        R = 64
        BATCH = 1
        L = 512
        EPS = 1e-06

        def _rmsnorm(x, w):
            return x * jax.lax.rsqrt(jnp.mean(x * x, axis=-1, keepdims=True) + EPS) * w
        proj = hidden_states @ W_in.T
        u, gate = jnp.split(proj, 2, axis=-1)
        x = jnp.transpose(u, (0, 2, 1))
        x = jax.lax.conv_general_dilated(x, conv_w[:, None, :], window_strides=(1,), padding=[(K - 1, 0)], dimension_numbers=('NCH', 'OIH', 'NCH'), feature_group_count=D)
        u = jax.nn.silu(jnp.transpose(x, (0, 2, 1)) + conv_b)
        ssm_p = u @ Wx.T
        dt, Bm, Cm = jnp.split(ssm_p, [R, R + N], axis=-1)
        dt = _rmsnorm(dt, dt_ln_w)
        Bm = _rmsnorm(Bm, b_ln_w)
        Cm = _rmsnorm(Cm, c_ln_w)
        delta = jax.nn.softplus(dt @ Wdt.T + dt_bias)

        def step(state, xs):
            d_t, B_t, C_t, u_t = xs
            dA = jnp.exp(d_t[..., None] * A)
            state = dA * state + (d_t * u_t)[..., None] * B_t[:, None, :]
            y_t = jnp.einsum('bdn,bn->bd', state, C_t)
            return (state, y_t)
        init = jnp.zeros((hidden_states.shape[0], D, N), hidden_states.dtype)
        xs = (jnp.swapaxes(delta, 0, 1), jnp.swapaxes(Bm, 0, 1), jnp.swapaxes(Cm, 0, 1), jnp.swapaxes(u, 0, 1))
        _, ys = jax.lax.scan(step, init, xs)
        y = jnp.swapaxes(ys, 0, 1) + u * D_param
        y = y * jax.nn.silu(gate)
        return y @ W_out.T

    def _L0_ffn_ref(x, A_w, B_w, Wq_w, keys):
        import jax, jax.numpy as jnp
        import numpy as np
        IN_F = 1024
        OUT_F = 1024
        RANK = 8
        NUM_EXPERTS = 64
        TOP_K = 16
        ROUTER_DIM = 16
        ALPHA = 32
        SCALING = ALPHA / TOP_K
        BOTTLENECK = NUM_EXPERTS * RANK
        q = jnp.einsum('bsd,rd->bsr', x, Wq_w)
        scores = jnp.einsum('bsr,er->bse', q, keys)
        top_vals, top_idx = jax.lax.top_k(scores, TOP_K)
        top_w = jax.nn.softmax(top_vals, axis=-1)
        gate = jnp.sum(jax.nn.one_hot(top_idx, NUM_EXPERTS, dtype=top_w.dtype) * top_w[..., None], axis=-2)
        z = jnp.einsum('bsd,nd->bsn', x, A_w)
        z = z.reshape(*z.shape[:-1], NUM_EXPERTS, RANK)
        z_gated = (z * gate[..., None]).reshape(*z.shape[:-2], BOTTLENECK)
        out = jnp.einsum('bsn,on->bso', z_gated, B_w) * SCALING
        return out
    h = _L0_tok_ref(x, L0_tok_ids, L0_tok_orig_W, L0_tok_trainable_W, L0_tok_A_w, L0_tok_A_b, L0_tok_B_w, L0_tok_B_b)
    h = h + _L0_attn_ref(_layernorm(h, axis=-1), L0_attn_W_in, L0_attn_conv_w, L0_attn_conv_b, L0_attn_Wx, L0_attn_dt_ln_w, L0_attn_b_ln_w, L0_attn_c_ln_w, L0_attn_Wdt, L0_attn_dt_bias, L0_attn_A, L0_attn_D_param, L0_attn_W_out)
    h = h + _L0_ffn_ref(_layernorm(h, axis=-1), L0_ffn_A_w, L0_ffn_B_w, L0_ffn_Wq_w, L0_ffn_keys)
    return h

_drawn_inputs = setup_inputs


def setup_inputs(seed=0):
    import zlib

    import numpy as np

    out = dict(_drawn_inputs(seed))
    spreads = {'L0_attn_dt_ln_w': (1.0, 0.2),
     'L0_attn_b_ln_w': (1.0, 0.2),
     'L0_attn_c_ln_w': (1.0, 0.2),
     'L0_attn_D_param': (1.0, 0.2)}
    factors = {'L0_tok_trainable_W': 4.02, 'L0_tok_A_w': 7.062, 'L0_tok_A_b': 5.361, 'L0_tok_B_w': 3.246}
    for name, (base, spread) in spreads.items():
        noise = np.random.default_rng([zlib.crc32(name.encode()), seed]).standard_normal(out[name].shape)
        drawn = base * np.exp(spread * noise) if base else spread * noise
        out[name] = jnp.asarray(drawn.astype(out[name].dtype))
    for name, factor in factors.items():
        out[name] = (out[name] * factor).astype(out[name].dtype)
    return out
```

```python
from contextlib import ExitStack

import concourse.bass as bass
from concourse import mybir

F32 = mybir.dt.float32
F32R = mybir.dt.float32r
I32 = mybir.dt.int32
U32 = mybir.dt.uint32
ALU = mybir.AluOpType
ACT = mybir.ActivationFunctionType
AX_X = mybir.AxisListType.X

P = 128
BATCH, L = 8, 512
H = 1024
KH = H // P
VOCAB = 8000
N_IDS, INNER = 64, 16
D, N, R, TAPS = 2048, 16, 64, 4
DT = D // P
XP = R + 2 * N
TT = L // P
EXPERTS, RANK, TOP_K, ROUTER = 64, 8, 16, 16
BN = EXPERTS * RANK
KB = BN // P
SCALING = 32 / TOP_K
LN_EPS, RMS_EPS = 1e-5, 1e-6
G = 2
NG = N // G
WU = KH * 2 * P
WP = WU + XP + P
PAR = N + TAPS + 3
CONV_W, CONV_B, DT_B, D_SKIP = N, N + TAPS, N + TAPS + 1, N + TAPS + 2
NEG = -3.0e38


class Mem:

    def __init__(self, nc, ctx, phase):
        self.nc, self.ctx, self.phase = nc, ctx, phase

    def sb(self, name, shape, dt=F32):
        return self.ctx.enter_context(self.nc.sbuf_tensor(f"{self.phase}_{name}", shape, dt))

    def ps(self, name, shape, dt=F32):
        return self.ctx.enter_context(self.nc.psum_tensor(f"{self.phase}_{name}", shape, dt))

    def sem(self, name):
        return self.ctx.enter_context(self.nc.semaphore(f"{self.phase}_{name}"))

    def sems(self, name, n):
        return [self.sem(f"{name}{i}") for i in range(n)]


def one(ap, i):
    lead = ap[bass.ds(i, 1)]
    names = " ".join("abcde"[:len(ap.shape) - 1])
    return lead.rearrange(f"o {names} -> (o a) {names[2:]}")


def embed_phase(nc, io, scr):
    with ExitStack() as ctx:
        m = Mem(nc, ctx, "emb")
        ids_row = m.sb("ids_row", [N_IDS, BATCH * L], I32)
        tok_col = m.sb("tok_col", [P, BATCH * TT], I32)
        wrap = m.sb("wrap", [P, BATCH * TT], F32)
        row_f = m.sb("row_f", [P, BATCH * TT], F32)
        row_of = m.sb("row_of", [P, BATCH * TT], U32)
        id_col = m.sb("id_col", [N_IDS, 1], I32)
        id_row = m.sb("id_row", [N_IDS, N_IDS], I32)
        same = m.sb("same", [N_IDS, N_IDS])
        lower = m.sb("lower", [N_IDS, N_IDS])
        first = m.sb("first", [N_IDS, 2])
        tw = m.sb("tw", [P, KH, N_IDS])
        aw = m.sb("aw", [P, KH, INNER])
        ab = m.sb("ab", [INNER, 1])
        bw = m.sb("bw", [INNER + 1, H])
        hid = m.sb("hid", [INNER + 1, N_IDS])
        table = m.sb("table", [N_IDS, H])
        ident = m.sb("ident", [P, P])
        diff = m.sb("diff", [N_IDS, 2, P], I32)
        hit = m.sb("hit", [N_IDS, 2, P])
        row = m.sb("row", [P, 2, 1], U32)
        base = m.sb("base", [P, 2, H])
        h0 = m.sb("h0", [P, 2, H])
        stat = m.sb("stat", [P, 2, 12])
        mv = m.sb("mv", [P, 2, 2])
        std = m.sb("std", [P, 2, 1])
        rstd = m.sb("rstd", [P, 2, 1])
        eps = m.sb("eps", [P, 1])
        xln = m.sb("xln", [P, 2, H])
        xhl = m.sb("xhl", [P, 2, 2, H], F32R)
        wf = m.sb("wf", [P, 2, WP])
        whl = m.sb("whl", [P, 2, 2, WP], F32R)
        p_tab = [m.ps(f"p_tab{i}", [P, H]) for i in range(2)]
        p_tr = [m.ps(f"p_tr{i}", [P, H]) for i in range(2)]

        consts = m.sem("consts")
        chain = m.sem("chain")
        hid_mm = m.sem("hid_mm")
        hid_ok = m.sem("hid_ok")
        table_mm = m.sem("table_mm")
        table_ok = m.sem("table_ok")
        row_ok = m.sem("row_ok")
        hit_ok = m.sem("hit_ok")
        gathered = m.sems("gathered", 2)
        tab_mm = m.sem("tab_mm")
        h0_ok = m.sem("h0_ok")
        stats_seen = m.sem("stats_seen")
        row_seen = m.sem("row_seen")
        stats_ok = m.sem("stats_ok")
        mv_ok = m.sem("mv_ok")
        std_ok = m.sem("std_ok")
        rstd_ok = m.sem("rstd_ok")
        xln_ok = m.sem("xln_ok")
        tr_mm = m.sem("tr_mm")
        hi_ok = m.sem("hi_ok")
        lo_ok = m.sem("lo_ok")
        diff_ok = m.sem("diff_ok")
        h0_st = m.sems("h0_st", 2)
        x_st = m.sems("x_st", 2)
        wf_ld = m.sems("wf_ld", 2)
        whi_ok = m.sem("whi_ok")
        wlo_ok = m.sem("wlo_ok")
        w_st = m.sems("w_st", 2)
        wf_free = m.sems("wf_free", 2)
        block = ctx.enter_context(nc.Block())
        N_CONST = 11

        @block.sync
        def _(sp):
            for dst, src in (
                (ids_row[:], io["tok_row"].partition_broadcast(N_IDS).rearrange("p a n -> p (a n)")),
                (id_row[:], io["ids_row"].partition_broadcast(N_IDS).rearrange("p a n -> p (a n)")),
                (tok_col[:], io["tok_col"]), (id_col[:], io["ids_col"]), (lower[:], io["lower"]),
                (tw[:], io["tw"]), (aw[:], io["aw"]), (ab[:], io["ab"]),
                (bw[0:INNER, :], io["bw"]), (bw[INNER:INNER + 1, :], io["bb"]), (ident[:], io["ident"]),
            ):
                sp.dma_start(dst, src).then_inc(consts, 16)
            for s in range(2):
                sp.sem_inc(h0_st[s], 16)
                sp.sem_inc(x_st[s], 16)
                sp.sem_inc(w_st[s], 16)
                sp.sem_inc(wf_free[s], 1)
            with sp.Fori(0, BATCH) as b:
                for s in range(2):
                    sp.wait_ge(wf_free[s], b + 1)
                    sp.dma_start(wf[:, s], one(io["wpack"], 2 * b + s)).then_inc(wf_ld[s], 16)
                for t in range(TT):
                    s = t % 2
                    sp.wait_ge(h0_ok, TT * b + t + 1)
                    sp.dma_start(one(scr["h0"], TT * b + t), h0[:, s]).then_inc(h0_st[s], 16)
                    sp.wait_ge(lo_ok, TT * b + t + 1)
                    sp.dma_start(one(scr["xln"], b).rearrange("p e k (t n) -> p e k t n", t=TT)[:, :, :, t]
                                 .rearrange("p e k n -> p (e k) n"),
                                 xhl[:, s].bitcast(F32).rearrange("p e (k n) -> p (e k) n", k=KH)
                                 ).then_inc(x_st[s], 16)
                    if t >= 2:
                        w = t - 2
                        sp.wait_ge(wlo_ok, 2 * b + w + 1)
                        sp.dma_start(one(scr["w"], 2 * b + w), whl[:, w].bitcast(F32)).then_inc(w_st[w], 16)
            for s in range(2):
                sp.wait_ge(h0_st[s], 16 * (2 * BATCH + 1))
                sp.wait_ge(x_st[s], 16 * (2 * BATCH + 1))
                sp.wait_ge(w_st[s], 16 * (BATCH + 1))

        @block.gpsimd
        def _(pool):
            with pool.Fori(0, BATCH) as b:
                for t in range(TT):
                    s = t % 2
                    pool.wait_ge(row_ok, TT * b + t + 1)
                    pool.sem_inc(row_seen, 1)
                    pool.indirect_dma_start(
                        base[:, s, :], None, io["orig_w"],
                        bass.IndirectOffsetOnAxis(ap=row[:, s, :], axis=0)).then_inc(gathered[s], 16)

        @block.tensor
        def _(pe):
            pe.wait_ge(consts, 16 * N_CONST)
            for k in range(KH):
                mm = pe.matmul(p_tab[0][0:INNER, 0:N_IDS], aw[:, k, :], tw[:, k, :],
                               start=(k == 0), stop=(k == KH - 1))
            mm.then_inc(hid_mm, 1)
            pe.wait_ge(hid_ok, 2)
            for c in range(2):
                mm = pe.matmul(p_tab[1][0:N_IDS, 512 * c:512 * c + 512], hid[:, :], bw[:, 512 * c:512 * c + 512],
                               start=True, stop=True)
            mm.then_inc(table_mm, 1)
            pe.wait_ge(table_ok, 1)
            with pe.Fori(0, BATCH) as b:
                for t in range(TT):
                    s = t % 2
                    pe.wait_ge(hit_ok, TT * b + t + 1)
                    for c in range(2):
                        mm = pe.matmul(p_tab[s][:, 512 * c:512 * c + 512], hit[:, s, :],
                                       table[:, 512 * c:512 * c + 512], start=True, stop=True)
                    mm.then_inc(tab_mm, 1)
                    pe.wait_ge(xln_ok, TT * b + t + 1)
                    for k in range(KH):
                        mm = pe.transpose(p_tr[s][:, P * k:P * k + P], xln[:, s, P * k:P * k + P], ident[:, :])
                    mm.then_inc(tr_mm, 1)

        @block.scalar
        def _(act):
            act.wait_ge(hid_mm, 1)
            act.wait_ge(hid_ok, 1)
            nc.scalar.activation(hid[0:INNER, :], p_tab[0][0:INNER, 0:N_IDS], ACT.Identity,
                                 bias=ab[:, 0:1]).then_inc(hid_ok, 1)
            act.wait_ge(chain, 1)
            with act.Fori(0, BATCH) as b:
                for t in range(TT):
                    s = t % 2
                    act.wait_ge(mv_ok, TT * b + t + 1)
                    nc.scalar.activation(std[:, s], mv[:, s, 1:2], ACT.Sqrt, bias=eps[:, 0:1]).then_inc(std_ok, 1)
                    if t >= 2:
                        w = t - 2
                        act.wait_ge(wf_ld[w], 16 * b + 16)
                        act.wait_ge(w_st[w], 16 * b + 16)
                        nc.scalar.copy(whl[:, w, 0], wf[:, w]).then_inc(whi_ok, 1)
                    act.wait_ge(tr_mm, TT * b + t + 1)
                    act.wait_ge(x_st[s], 32 * b + 16 * (t // 2) + 16)
                    nc.scalar.copy(xhl[:, s, 0], p_tr[s][:, :]).then_inc(hi_ok, 1)

        @block.vector
        def _(dve):
            dve.memset(eps[:], LN_EPS).then_inc(chain, 1)
            dve.memset(hid[:], 1.0).then_inc(hid_ok, 1)
            dve.wait_ge(consts, 16 * N_CONST)
            dve.tensor_scalar(wrap[:], tok_col[:], 0, float(VOCAB), ALU.is_lt, ALU.mult).then_inc(chain, 1)
            dve.wait_ge(chain, 2)
            dve.tensor_tensor(row_f[:], tok_col[:], wrap[:], ALU.add).then_inc(chain, 1)
            dve.wait_ge(chain, 3)
            dve.tensor_scalar(row_of[:], row_f[:], 0.0, float(VOCAB - 1), ALU.max, ALU.min).then_inc(chain, 1)
            dve.tensor_tensor(id_row[:], id_row[:], id_col[:, 0:1].to_broadcast([N_IDS, N_IDS]),
                              ALU.bitwise_xor).then_inc(chain, 1)
            dve.wait_ge(chain, 5)
            dve.tensor_scalar(same[:], id_row[:], 0, None, ALU.is_equal).then_inc(chain, 1)
            dve.wait_ge(chain, 6)
            dve.tensor_tensor(same[:], same[:], lower[:], ALU.mult).then_inc(chain, 1)
            dve.wait_ge(chain, 7)
            dve.tensor_reduce(first[:, 0:1], same[:], AX_X, ALU.max).then_inc(chain, 1)
            dve.wait_ge(chain, 8)
            dve.tensor_scalar(first[:, 1:2], first[:, 0:1], -1.0, 1.0, ALU.mult, ALU.add).then_inc(chain, 1)
            dve.wait_ge(chain, 9)
            dve.wait_ge(table_mm, 1)
            dve.tensor_scalar(table[:], p_tab[1][0:N_IDS, :], first[:, 1:2], None, ALU.mult).then_inc(table_ok, 1)

            with dve.Fori(0, BATCH) as b:
                for t in range(TT):
                    s = t % 2
                    i = TT * b + t
                    dve.tensor_tensor(diff[:, s], ids_row[:, bass.ds(P * i, P)],
                                      id_col[:, 0:1].to_broadcast([N_IDS, P]), ALU.bitwise_xor).then_inc(diff_ok, 1)
                    dve.tensor_copy(row[:, s], row_of[:, bass.ds(i, 1)]).then_inc(row_ok, 1)
                    dve.wait_ge(diff_ok, i + 1)
                    dve.tensor_scalar(hit[:, s], diff[:, s], 0, None, ALU.is_equal).then_inc(hit_ok, 1)
                    dve.wait_ge(gathered[s], 32 * b + 16 * (t // 2) + 16)
                    dve.wait_ge(tab_mm, i + 1)
                    dve.wait_ge(h0_st[s], 32 * b + 16 * (t // 2) + 16)
                    dve.tensor_tensor(h0[:, s], base[:, s], p_tab[s][:, :], ALU.add).then_inc(h0_ok, 1)
                    dve.wait_ge(h0_ok, i + 1)
                    for c in range(2):
                        dve.bn_stats(stat[:, s, 6 * c:6 * c + 6], h0[:, s, 512 * c:512 * c + 512]).then_inc(stats_ok, 1)
                    dve.wait_ge(stats_ok, 2 * i + 2)
                    dve.sem_inc(stats_seen, 1)
                    dve.bn_aggr(mv[:, s], stat[:, s]).then_inc(mv_ok, 1)
                    if t >= 2:
                        w = t - 2
                        dve.wait_ge(whi_ok, 2 * b + w + 1)
                        dve.tensor_tensor(whl[:, w, 1], wf[:, w], whl[:, w, 0], ALU.subtract).then_inc(wlo_ok, 1)
                    dve.wait_ge(std_ok, i + 1)
                    dve.reciprocal(rstd[:, s], std[:, s]).then_inc(rstd_ok, 1)
                    dve.wait_ge(rstd_ok, i + 1)
                    dve.tensor_scalar(xln[:, s], h0[:, s], mv[:, s, 0:1], rstd[:, s, 0:1],
                                      ALU.subtract, ALU.mult).then_inc(xln_ok, 1)
                    dve.wait_ge(hi_ok, i + 1)
                    dve.tensor_tensor(xhl[:, s, 1], p_tr[s][:, :], xhl[:, s, 0], ALU.subtract).then_inc(lo_ok, 1)
                    if t >= 2:
                        dve.wait_ge(wlo_ok, 2 * b + w + 1)
                        dve.sem_inc(wf_free[w], 1)


def mamba_phase(nc, io, scr):
    PAIRS = DT // 2
    HR = 4
    with ExitStack() as ctx:
        m = Mem(nc, ctx, "ssm")
        w = m.sb("w", [P, 2, 2, WP], F32R)
        par = m.sb("par", [P, 2, PAR])
        xln = m.sb("xln", [P, 2, KH, L], F32R)
        b_all = m.sb("b_all", [P, N, L])
        c_all = m.sb("c_all", [P, N, L])
        db = m.sb("db", [P, 2, G, L])
        h = m.sb("h", [P, HR, G, L])
        u = m.sb("u", [P, 2, L])
        g = m.sb("g", [P, 2, L])
        u_new = m.sb("u_new", [P, 2, L])
        g_new = m.sb("g_new", [P, L])
        u_pad = m.sb("u_pad", [P, TAPS - 1 + L])
        conv = m.sb("conv", [P, L])
        u_hl = m.sb("u_hl", [P, 2, L], F32R)
        delta = m.sb("delta", [P, 2, L])
        du = m.sb("du", [P, 2, L])
        soft = m.sb("soft", [P, L])
        y = m.sb("y", [P, 2, L])
        dt_hl = m.sb("dt_hl", [R, 2, L], F32R)
        xn = m.sb("xn", [XP, L])
        sq = m.sb("sq", [XP, L])
        rs = m.sb("rs", [XP, L])
        rms_w = m.sb("rms_w", [XP, 1])
        rms_mean = m.sb("rms_mean", [XP, XP])
        rms_eps = m.sb("rms_eps", [XP, 1])
        ident = m.sb("ident", [P, P])
        zeros = m.sb("zeros", [P, P], F32R)
        da = m.ps("da", [P, 2, G, L])
        p_y = m.ps("p_y", [P, L])
        p_in = m.ps("p_in", [P, L])
        p_dt = m.ps("p_dt", [P, L])
        p_x = m.ps("p_x", [P, L])

        consts = m.sem("consts")
        zeroed = m.sem("zeroed")
        w_ld = m.sems("w_ld", 2)
        w_used = m.sem("w_used")
        xln_ld = m.sem("xln_ld")
        ug_ld = m.sems("ug_ld", 2)
        u_st = m.sems("u_st", 2)
        g_st = m.sem("g_st")
        y_st = m.sems("y_st", 2)
        bc_st = m.sem("bc_st")
        b_ld = m.sems("b_ld", NG)
        c_ld = m.sems("c_ld", NG)
        u_mm = m.sem("u_mm")
        g_mm = m.sem("g_mm")
        dt_mm = m.sem("dt_mm")
        x_mm = m.sem("x_mm")
        ms_mm = m.sem("ms_mm")
        h_used = m.sem("h_used")
        up_ok = m.sem("up_ok")
        gn_ok = m.sem("gn_ok")
        un_ok = m.sem("un_ok")
        hi_ok = m.sem("hi_ok")
        lo_ok = m.sem("lo_ok")
        tap_ok = m.sem("tap_ok")
        abs_ok = m.sem("abs_ok")
        exp_ok = m.sem("exp_ok")
        log_ok = m.sem("log_ok")
        max_ok = m.sem("max_ok")
        delta_ok = m.sem("delta_ok")
        du_ok = m.sem("du_ok")
        da_ok = m.sem("da_ok")
        db_ok = m.sem("db_ok")
        scan_ok = m.sem("scan_ok")
        hc_ok = m.sem("hc_ok")
        skip_ok = m.sem("skip_ok")
        y_ok = m.sem("y_ok")
        sq_ok = m.sem("sq_ok")
        rlog_ok = m.sem("rlog_ok")
        rs_ok = m.sem("rs_ok")
        xn_ok = m.sem("xn_ok")
        dth_ok = m.sem("dth_ok")
        dtl_ok = m.sem("dtl_ok")
        block = ctx.enter_context(nc.Block())

        def schedule(eng, step, between, start=None):
            if start:
                start()
            with eng.Fori(0, PAIRS) as i:
                for s in range(2):
                    step(s, None, i, 0)
            between(0)
            with eng.Fori(0, BATCH - 1) as b:
                with eng.Fori(0, PAIRS) as i:
                    for s in range(2):
                        step(s, PAIRS * b + i, PAIRS * b + i + PAIRS, b)
                between(b + 1)
            with eng.Fori(0, PAIRS) as i:
                for s in range(2):
                    step(s, i + PAIRS * (BATCH - 1), None, BATCH - 1)

        @block.sync
        def _(sp):
            for dst, src in ((ident[:], io["ident"]), (rms_w[:], io["rms_w"]), (rms_mean[:], io["rms_mean"])):
                sp.dma_start(dst, src).then_inc(consts, 16)

            def load_w(s, dt):
                sp.dma_start(w[:, s].bitcast(F32), one(scr["w"], dt)).then_inc(w_ld[s], 16)
                sp.dma_start(par[:, s], one(io["par"], dt)).then_inc(w_ld[s], 16)

            def load_xln(b):
                sp.dma_start(xln[:].bitcast(F32), one(scr["xln"], b)).then_inc(xln_ld, 16)

            def load_ug(s, pair):
                sp.wait_ge(u_st[s], 16 * (pair + 2))
                sp.dma_start(u[:, s], one(scr["u"], 2 * pair + s)).then_inc(ug_ld[s], 16)
                sp.wait_ge(g_st, 16 * (2 * pair + s + 2))
                sp.dma_start(g[:, s], one(scr["g"], 2 * pair + s)).then_inc(ug_ld[s], 16)

            def step(s, ps, pi, next_dt, next_ug):
                if pi is not None:
                    sp.wait_ge(un_ok, 2 * pi + s + 2)
                    sp.dma_start(one(scr["u"], 2 * pi + s), u_new[:, s]).then_inc(u_st[s], 16)
                    sp.wait_ge(gn_ok, 2 * pi + s + 2)
                    sp.dma_start(one(scr["g"], 2 * pi + s), g_new[:]).then_inc(g_st, 16)
                if ps is not None:
                    sp.wait_ge(y_ok, 2 * ps + s + 1)
                    sp.dma_start(one(scr["y"], 2 * ps + s), y[:, s]).then_inc(y_st[s], 16)
                pw = pi if pi is not None else ps + PAIRS
                if next_dt is not None:
                    sp.wait_ge(w_used, 2 * pw + s + 2)
                    load_w(s, next_dt)
                if next_ug:
                    load_ug(s, ps + 1)

            def between(b, again=True):
                sp.wait_ge(xn_ok, b + 1)
                sp.dma_start(one(scr["bc"], b), xn[R:XP, :]).then_inc(bc_st, 16)
                sp.wait_ge(bc_st, 16 * (b + 2))
                for j in range(NG):
                    for all_, ld, ok, first in ((b_all, b_ld, db_ok, 0), (c_all, c_ld, hc_ok, N)):
                        if again:
                            sp.wait_ge(ok, NG * DT * b - NG + j + 1)
                        src = one(scr["bc"], b)[first + G * j:first + G * j + G, :]
                        sp.dma_start(all_[:, G * j:G * j + G, :].rearrange("p n l -> p (n l)"),
                                     src.rearrange("(o n) l -> o (n l)", o=1).partition_broadcast(P)
                                     .rearrange("p o n -> p (o n)")).then_inc(ld[j], 16)

            sp.wait_ge(zeroed, 1)
            for s in range(2):
                sp.sem_inc(u_st[s], 16)
                sp.sem_inc(y_st[s], 16)
            sp.sem_inc(g_st, 16)
            sp.sem_inc(bc_st, 16)
            load_w(0, 0)
            load_xln(0)
            load_w(1, 1)
            with sp.Fori(0, PAIRS - 1) as i:
                for s in range(2):
                    step(s, None, i, 2 * i + 2 + s, False)
            for s in range(2):
                step(s, None, PAIRS - 1, s, False)
            sp.wait_ge(x_mm, 1)
            load_xln(1)
            for s in range(2):
                load_ug(s, 0)
            between(0, again=False)

            def both(b):
                with sp.Fori(0, PAIRS - 1) as i:
                    for s in range(2):
                        step(s, PAIRS * b + i, PAIRS * b + i + PAIRS, 2 * i + 2 + s, True)
                for s in range(2):
                    step(s, PAIRS * b + PAIRS - 1, PAIRS * b + 2 * PAIRS - 1, s, True)
                between(b + 1)

            with sp.Fori(0, BATCH - 2) as b:
                both(b)
                sp.wait_ge(x_mm, b + 2)
                load_xln(b + 2)
            both(BATCH - 2)
            with sp.Fori(0, PAIRS - 1) as i:
                for s in range(2):
                    step(s, i + PAIRS * (BATCH - 1), None, 2 * i + 2 + s, True)
            for s in range(2):
                step(s, PAIRS * BATCH - 1, None, None, False)
            for s in range(2):
                sp.wait_ge(u_st[s], 16 * (PAIRS * BATCH + 1))
                sp.wait_ge(y_st[s], 16 * (PAIRS * BATCH + 1))
            sp.wait_ge(g_st, 16 * (DT * BATCH + 1))
            sp.wait_ge(bc_st, 16 * (BATCH + 1))
            sp.wait_ge(xln_ld, 16 * BATCH)

        @block.gpsimd
        def _(pool):
            def step(s, ps, pi, b):
                if ps is None:
                    return
                q = 2 * ps + s
                pool.wait_ge(du_ok, q + 2)
                for j in range(NG):
                    pool.wait_ge(scan_ok, NG * q + j + 1)
                    if s == 0:
                        pool.wait_ge(b_ld[j], 16 * (b + 1))
                    pool.tensor_tensor(db[:, j % 2], du[:, s:s + 1, :].to_broadcast([P, G, L]),
                                       b_all[:, G * j:G * j + G, :], ALU.mult).then_inc(db_ok, 1)

            with pool.Fori(0, BATCH - 1) as b:
                with pool.Fori(0, PAIRS) as i:
                    for s in range(2):
                        step(s, PAIRS * b + i, None, b)
            with pool.Fori(0, PAIRS) as i:
                for s in range(2):
                    step(s, i + PAIRS * (BATCH - 1), None, BATCH - 1)

        @block.tensor
        def _(pe):
            def product(out, s, cols, k, first, last):
                for n_, (a, c) in enumerate(((0, 0), (1, 0), (0, 1))):
                    mm = pe.matmul(out, w[:, s, a, cols], xln[:, c, k, :],
                                   start=first and n_ == 0, stop=last and n_ == 2)
                return mm

            def in_mm(s, part, ok):
                for k in range(KH):
                    at = (2 * k + part) * P
                    mm = product(p_in[:], s, slice(at, at + P), k, k == 0, k == KH - 1)
                mm.then_inc(ok, 1)

            def add_groups(q, groups):
                for j in groups:
                    pe.wait_ge(hc_ok, NG * q + j + 1)
                    if j == 0:
                        pe.wait_ge(skip_ok, q + 1)
                    for n_ in range(G):
                        mm = pe.matmul(p_y[:], ident[:], h[:, j % HR, n_, :], start=(j == 0 and n_ == 0),
                                       stop=(j == NG - 1 and n_ == G - 1))
                    mm.then_inc(h_used, 1)

            def step(s, ps, pi, b):
                pw = pi if pi is not None else ps + PAIRS
                pe.wait_ge(w_ld[s], 32 * (pw + 1))
                if ps is not None:
                    q = 2 * ps + s
                    pe.wait_ge(dtl_ok, b + 1)
                    pe.wait_ge(du_ok, q + 1)
                    for n_, (a, c) in enumerate(((0, 0), (1, 0), (0, 1))):
                        mm = pe.matmul(p_dt[:], w[0:R, s, a, WU + XP:WP], dt_hl[:, c, :],
                                       start=(n_ == 0), stop=(n_ == 2))
                    mm.then_inc(dt_mm, 1)
                if pi is not None:
                    pe.wait_ge(xln_ld, 16 * (b + 1) if ps is None else 16 * (b + 2))
                    pe.wait_ge(gn_ok, 2 * pi + s + 1)
                    in_mm(s, 0, u_mm)
                if ps is not None:
                    add_groups(q, range(NG // 2))
                if pi is not None:
                    pe.wait_ge(up_ok, 2 * pi + s + 1)
                    in_mm(s, 1, g_mm)
                if ps is not None:
                    add_groups(q, range(NG // 2, NG))
                if pi is not None:
                    pe.wait_ge(lo_ok, 2 * pi + s + 1)
                    for a, c in ((0, 0), (1, 0), (0, 1)):
                        mm = pe.matmul(p_x[0:XP, :], w[:, s, a, WU:WU + XP], u_hl[:, c, :],
                                       start=False, stop=False, skip_group_check=True)
                    mm.then_inc(w_used, 1)
                else:
                    pe.sem_inc(w_used, 1)

            def clear_x(first):
                for c in range(L // P):
                    mm = pe.matmul(p_x[0:XP, P * c:P * c + P], zeros[:, 0:XP], zeros[:], start=first and c == 0,
                                   stop=not first, skip_group_check=True)
                return mm

            def between(b):
                clear_x(False).then_inc(x_mm, 1)
                pe.wait_ge(sq_ok, b + 1)
                pe.wait_ge(gn_ok, DT * b + DT + 1)
                pe.matmul(p_in[0:XP, :], rms_mean[:], sq[:], start=True, stop=True).then_inc(ms_mm, 1)
                pe.wait_ge(rlog_ok, b + 1)
                pe.wait_ge(xn_ok, b + 1)
                clear_x(True)

            pe.wait_ge(consts, 48)
            pe.wait_ge(zeroed, 1)
            pe.sem_inc(w_used, 1)
            pe.sem_inc(dt_mm, 1)
            pe.sem_inc(h_used, HR)
            clear_x(True)
            schedule(pe, step, between)

        @block.scalar
        def _(act):
            def exps(q, s, groups):
                for j in groups:
                    act.wait_ge(scan_ok, NG * q + j + 1)
                    for n_ in range(G):
                        a = nc.scalar.activation(da[:, j % 2, n_, 1:L], delta[:, s, 1:L], ACT.Exp,
                                                 scale=par[:, s, G * j + n_:G * j + n_ + 1])
                    a.then_inc(da_ok, 1)

            def step(s, ps, pi, b):
                if ps is not None:
                    q = 2 * ps + s
                    act.wait_ge(dt_mm, q + 2)
                    act.wait_ge(du_ok, q + 1)
                    nc.scalar.activation(soft[:], p_dt[:], ACT.Abs, bias=par[:, s, DT_B:DT_B + 1]).then_inc(abs_ok, 1)
                    act.wait_ge(abs_ok, q + 1)
                    nc.scalar.activation(soft[:], soft[:], ACT.Exp, scale=-1.0).then_inc(exp_ok, 1)
                    act.wait_ge(exp_ok, q + 1)
                    nc.scalar.activation(soft[:], soft[:], ACT.Ln, bias=1.0).then_inc(log_ok, 1)
                if pi is not None:
                    t = 2 * pi + s
                    act.wait_ge(u_mm, t + 1)
                    act.wait_ge(tap_ok, TAPS * (t + 1))
                    nc.scalar.copy(u_pad[:, TAPS - 1:], p_in[:]).then_inc(up_ok, 1)
                if ps is not None:
                    act.wait_ge(delta_ok, q + 1)
                    exps(q, s, range(6))
                if pi is not None:
                    act.wait_ge(tap_ok, TAPS * (t + 2))
                    act.wait_ge(u_st[s], 16 * (pi + 1))
                    nc.scalar.activation(u_new[:, s], conv[:], ACT.Silu).then_inc(un_ok, 1)
                    act.wait_ge(g_mm, t + 1)
                    act.wait_ge(g_st, 16 * (t + 1))
                    nc.scalar.activation(g_new[:], p_in[:], ACT.Silu).then_inc(gn_ok, 1)
                    act.wait_ge(un_ok, t + 2)
                    act.wait_ge(w_used, t + 1)
                    nc.scalar.copy(u_hl[:, 0], u_new[:, s]).then_inc(hi_ok, 1)
                if ps is not None:
                    exps(q, s, range(6, NG))

            def between(b):
                act.wait_ge(x_mm, b + 1)
                nc.scalar.activation(sq[:], p_x[0:XP, :], ACT.Square).then_inc(sq_ok, 1)
                act.wait_ge(ms_mm, b + 1)
                nc.scalar.activation(rs[:], p_in[0:XP, :], ACT.Ln, bias=rms_eps[:, 0:1]).then_inc(rlog_ok, 1)
                act.wait_ge(rlog_ok, b + 1)
                nc.scalar.activation(rs[:], rs[:], ACT.Exp, scale=-0.5).then_inc(rs_ok, 1)
                act.wait_ge(xn_ok, b + 1)
                act.wait_ge(dt_mm, DT * b + 1)
                nc.scalar.copy(dt_hl[:, 0], xn[0:R, :]).then_inc(dth_ok, 1)

            act.sem_inc(gn_ok, 1)
            act.sem_inc(un_ok, 1)
            act.wait_ge(zeroed, 1)
            schedule(act, step, between)

        @block.vector
        def _(dve):
            dve.memset(u_pad[:, 0:TAPS - 1], 0.0)
            dve.memset(rms_eps[:], RMS_EPS)
            dve.memset(da[:, :, :, 0:1], 0.0)
            dve.memset(zeros[:].bitcast(F32), 0.0).then_inc(zeroed, 1)
            dve.sem_inc(du_ok, 1)
            dve.sem_inc(skip_ok, 1)
            dve.sem_inc(scan_ok, 2)
            dve.sem_inc(tap_ok, TAPS)
            dve.wait_ge(consts, 48)
            dve.wait_ge(zeroed, 1)

            def tap(t, s, k):
                if k == 0:
                    dve.wait_ge(up_ok, t + 1)
                    dve.wait_ge(un_ok, t + 1)
                    dve.tensor_scalar(conv[:], u_pad[:, TAPS - 1:], par[:, s, CONV_W + 3:CONV_W + 4],
                                      par[:, s, CONV_B:CONV_B + 1], ALU.mult, ALU.add).then_inc(tap_ok, 1)
                else:
                    dve.wait_ge(tap_ok, TAPS * (t + 1) + k)
                    c = TAPS - 1 - k
                    dve.scalar_tensor_tensor(out=conv[:], in0=u_pad[:, c:c + L],
                                             scalar=par[:, s, CONV_W + c:CONV_W + c + 1], in1=conv[:],
                                             op0=ALU.mult, op1=ALU.add).then_inc(tap_ok, 1)

            def low_u(t, s):
                dve.wait_ge(hi_ok, t + 1)
                dve.tensor_tensor(u_hl[:, 1], u_new[:, s], u_hl[:, 0], ALU.subtract).then_inc(lo_ok, 1)

            def scan(q, s, j):
                dve.wait_ge(da_ok, NG * q + j + 1)
                dve.wait_ge(db_ok, NG * q + j + 1)
                dve.wait_ge(h_used, NG * q + j + 1)
                dve.tensor_tensor_scan(h[:, j % HR].rearrange("p n l -> p (n l)"),
                                       da[:, j % 2].rearrange("p n l -> p (n l)"),
                                       db[:, j % 2].rearrange("p n l -> p (n l)"),
                                       0.0, ALU.mult, ALU.add).then_inc(scan_ok, 1)

            def times_c(q, s, j, b):
                dve.wait_ge(scan_ok, NG * q + j + 3)
                if s == 0:
                    dve.wait_ge(c_ld[j], 16 * (b + 1))
                dve.tensor_tensor(h[:, j % HR], h[:, j % HR], c_all[:, G * j:G * j + G, :],
                                  ALU.mult).then_inc(hc_ok, 1)

            def step(s, ps, pi, b):
                if pi is not None:
                    t = 2 * pi + s
                if ps is None:
                    for k in range(TAPS):
                        tap(t, s, k)
                    low_u(t, s)
                    return
                q = 2 * ps + s
                dve.wait_ge(abs_ok, q + 1)
                dve.tensor_scalar(delta[:, s], p_dt[:], par[:, s, DT_B:DT_B + 1], 0.0,
                                  ALU.add, ALU.max).then_inc(max_ok, 1)
                dve.wait_ge(max_ok, q + 1)
                dve.wait_ge(log_ok, q + 1)
                dve.tensor_tensor(delta[:, s], delta[:, s], soft[:], ALU.add).then_inc(delta_ok, 1)
                dve.wait_ge(delta_ok, q + 1)
                dve.wait_ge(ug_ld[s], 32 * (ps + 1))
                dve.tensor_tensor(du[:, s], delta[:, s], u[:, s], ALU.mult).then_inc(du_ok, 1)
                for j in range(NG + 1):
                    if j < NG:
                        scan(q, s, j)
                    if pi is not None and 1 <= j <= TAPS:
                        tap(t, s, j - 1)
                    if pi is not None and j == 7:
                        low_u(t, s)
                    if j >= 1:
                        times_c(q, s, j - 1, b)
                dve.wait_ge(h_used, NG * q + NG + HR)
                dve.wait_ge(y_st[s], 16 * (ps + 1))
                dve.scalar_tensor_tensor(out=y[:, s], in0=u[:, s], scalar=par[:, s, D_SKIP:D_SKIP + 1], in1=p_y[:],
                                         op0=ALU.mult, op1=ALU.add).then_inc(skip_ok, 1)
                dve.wait_ge(skip_ok, q + 2)
                dve.tensor_tensor(y[:, s], y[:, s], g[:, s], ALU.mult).then_inc(y_ok, 1)

            def between(b):
                dve.wait_ge(rs_ok, b + 1)
                dve.wait_ge(bc_st, 16 * (b + 1))
                dve.scalar_tensor_tensor(out=xn[:], in0=p_x[0:XP, :], scalar=rms_w[:, 0:1], in1=rs[:],
                                         op0=ALU.mult, op1=ALU.mult).then_inc(xn_ok, 1)
                dve.wait_ge(xn_ok, b + 1)
                dve.wait_ge(dth_ok, b + 1)
                dve.tensor_tensor(dt_hl[:, 1], xn[0:R, :], dt_hl[:, 0], ALU.subtract).then_inc(dtl_ok, 1)

            schedule(dve, step, between)


def out_phase(nc, io, scr, stats):
    HC = H // 512
    with ExitStack() as ctx:
        m = Mem(nc, ctx, "out")
        wo_hl = m.sb("wo_hl", [P, 2, DT, H], F32R)
        wo = m.sb("wo", [P, 2, H])
        y = m.sb("y", [P, 2, DT, P])
        y_hl = m.sb("y_hl", [P, 2, DT, P], F32R)
        y_hl2 = m.sb("y_hl2", [P, 2, DT, P], F32R)
        h0 = m.sb("h0", [P, H])
        h1 = m.sb("h1", [P, H])
        ys = (y_hl, y_hl2)
        p_o = [m.ps(f"p_o{i}", [P, H]) for i in range(2)]
        bstat = m.sb("bstat", [P, 12])
        mv = m.sb("mv", [P, 2])

        wo_ld = m.sems("wo_ld", 2)
        whi_ok = m.sem("whi_ok")
        wlo_ok = m.sem("wlo_ok")
        y_ld = m.sems("y_ld", 2)
        h0_ld = m.sem("h0_ld")
        hi_ok = m.sem("hi_ok")
        lo_ok = m.sem("lo_ok")
        o_mm = m.sem("o_mm")
        h1_ok = m.sem("h1_ok")
        h1_st = m.sem("h1_st")
        bn_ok = m.sem("bn_ok")
        bn_seen = m.sem("bn_seen")
        mv_ok = m.sem("mv_ok")
        st_ok = m.sem("st_ok")
        block = ctx.enter_context(nc.Block())

        @block.sync
        def _(sp):
            sp.sem_inc(h1_st, 16)
            for k in range(DT):
                if k >= 2:
                    sp.wait_ge(wlo_ok, k - 1)
                sp.dma_start(wo[:, k % 2], io["wo"][:, k, :]).then_inc(wo_ld[k % 2], 16)
            with sp.Fori(0, BATCH) as b:
                for t in range(TT):
                    i = TT * b + t
                    s = t % 2
                    sp.wait_ge(lo_ok, i + 1)
                    sp.dma_start(y[:, s], scr["y"].rearrange("(b k) p l -> b p k l", b=BATCH)
                                 [bass.ds(b, 1), :, :, P * t:P * t + P].rearrange("o p k l -> p (o k) l")
                                 ).then_inc(y_ld[s], 16)
                    sp.wait_ge(h1_ok, i + 2)
                    sp.dma_start(h0[:], one(scr["h0"], i)).then_inc(h0_ld, 16)
            sp.wait_ge(h1_st, 16 * (BATCH * TT + 1))

        @block.tensor
        def _(pe):
            pe.sem_inc(o_mm, 2)
            pe.wait_ge(wlo_ok, DT)
            with pe.Fori(0, BATCH) as b:
                for t in range(TT):
                    i = TT * b + t
                    s = t % 2
                    pe.wait_ge(lo_ok, i + 3)
                    pe.wait_ge(h1_ok, i + 1)
                    for k in range(DT):
                        for c in range(HC):
                            for n_, (a, e) in enumerate(((0, 0), (1, 0), (0, 1))):
                                mm = pe.matmul(p_o[s][:, 512 * c:512 * c + 512], ys[s][:, a, k, :],
                                               wo_hl[:, e, k, 512 * c:512 * c + 512],
                                               start=(k == 0 and n_ == 0), stop=(k == DT - 1 and n_ == 2))
                    mm.then_inc(o_mm, 1)

        @block.scalar
        def _(act):
            for k in range(DT):
                act.wait_ge(wo_ld[k % 2], 16 * (k // 2 + 1))
                nc.scalar.copy(wo_hl[:, 0, k, :], wo[:, k % 2]).then_inc(whi_ok, 1)

            def high(i, b, t):
                s = t % 2
                act.wait_ge(y_ld[s], 32 * b + 16 * (t // 2) + 16)
                act.wait_ge(o_mm, i + 1)
                nc.scalar.copy(ys[s][:, 0], y[:, s]).then_inc(hi_ok, 1)

            def tiles(b, last=False):
                for t in range(TT):
                    i = TT * b + t
                    if t < TT - 1:
                        high(i + 1, b, t + 1)
                    elif not last:
                        high(i + 1, b + 1, 0)
                    act.wait_ge(h1_ok, i + 3)
                    act.dma_start(one(scr["h1"], i), h1[:]).then_inc(h1_st, 16)

            high(0, 0, 0)
            with act.Fori(0, BATCH - 1) as b:
                tiles(b)
            tiles(BATCH - 1, last=True)

        @block.vector
        def _(dve):
            dve.sem_inc(lo_ok, 2)
            dve.sem_inc(h1_ok, 2)
            for k in range(DT):
                dve.wait_ge(whi_ok, k + 1)
                dve.tensor_tensor(wo_hl[:, 1, k, :], wo[:, k % 2], wo_hl[:, 0, k, :], ALU.subtract).then_inc(wlo_ok, 1)

            def low(i, s):
                dve.wait_ge(hi_ok, i + 1)
                dve.tensor_tensor(ys[s][:, 1], y[:, s], ys[s][:, 0], ALU.subtract).then_inc(lo_ok, 1)

            def tiles(b, last=False):
                for t in range(TT):
                    i = TT * b + t
                    s = t % 2
                    if not (last and t == TT - 1):
                        low(i + 1, 1 - s)
                    dve.wait_ge(o_mm, i + 3)
                    dve.wait_ge(h0_ld, 16 * i + 16)
                    dve.wait_ge(h1_st, 16 * i + 16)
                    dve.tensor_tensor(h1[:], h0[:], p_o[s][:, :], ALU.add).then_inc(h1_ok, 1)
                    dve.wait_ge(h1_ok, i + 3)
                    for c in range(HC):
                        dve.bn_stats(bstat[:, 6 * c:6 * c + 6], h1[:, 512 * c:512 * c + 512]).then_inc(bn_ok, 1)
                    dve.wait_ge(bn_ok, 2 * i + 2)
                    dve.sem_inc(bn_seen, 1)
                    dve.bn_aggr(mv[:], bstat[:]).then_inc(mv_ok, 1)
                    dve.wait_ge(mv_ok, i + 1)
                    dve.tensor_scalar(stats[:, bass.ds(2 * i, 2)], mv[:], 1.0, None, ALU.mult).then_inc(st_ok, 1)

            low(0, 0)
            with dve.Fori(0, BATCH - 1) as b:
                tiles(b)
            tiles(BATCH - 1, last=True)
            dve.wait_ge(st_ok, BATCH * TT)


def ffn_phase(nc, io, scr, stats, out):
    HC = H // 512
    with ExitStack() as ctx:
        m = Mem(nc, ctx, "ffn")
        wz_hl = m.sb("wz_hl", [P, 2, KH, BN], F32R)
        wb_hl = m.sb("wb_hl", [P, 2, KB, H], F32R)
        w_f = m.sb("w_f", [P, 2, KH * BN])
        wr = m.sb("wr", [P, KH, ROUTER])
        keys = m.sb("keys", [ROUTER, EXPERTS])
        ident = m.sb("ident", [P, P])
        rstd = m.sb("rstd", [P, BATCH * TT])
        std = m.sb("std", [P, BATCH * TT])
        eps = m.sb("eps", [P, 1])
        h1 = m.sb("h1", [P, 2, H])
        xln = m.sb("xln", [P, H])
        x_f = m.sb("x_f", [P, KH, P])
        x_hl = m.sb("x_hl", [P, 2, KH, P], F32R)
        qt = m.sb("qt", [ROUTER, P])
        score = m.sb("score", [P, EXPERTS])
        rest = m.sb("rest", [P, 2, EXPERTS])
        top = m.sb("top", [P, 2, 8])
        neg_max = m.sb("neg_max", [P, 1])
        ex = m.sb("ex", [P, EXPERTS])
        chosen = m.sb("chosen", [P, EXPERTS])
        total = m.sb("total", [P, 1])
        inv = m.sb("inv", [P, 1])
        gate = m.sb("gate", [P, EXPERTS, 1])
        zg = m.sb("zg", [P, BN])
        z_hl = m.sb("z_hl", [P, 2, KB, P], F32R)
        res = m.sb("res", [P, 2, H])
        p_xt = m.ps("p_xt", [P, H])
        p_z = m.ps("p_z", [P, BN])
        p_q = m.ps("p_q", [P, 512])
        p_s = m.ps("p_s", [P, 512])
        p_zt = m.ps("p_zt", [P, KB * P])
        p_o = m.ps("p_o", [P, H])

        consts = m.sem("consts")
        w_ldz = m.sem("w_ldz")
        w_ldb = m.sem("w_ldb")
        whi_ok = m.sem("whi_ok")
        wlo_ok = m.sem("wlo_ok")
        eps_ok = m.sem("eps_ok")
        std_ok = m.sem("std_ok")
        rstd_ok = m.sem("rstd_ok")
        h1_ld = m.sems("h1_ld", 2)
        xln_ok = m.sem("xln_ok")
        xt_mm = m.sem("xt_mm")
        xf_ok = m.sem("xf_ok")
        hi_ok = m.sem("hi_ok")
        lo_ok = m.sem("lo_ok")
        q_mm = m.sem("q_mm")
        q_ok = m.sem("q_ok")
        s_mm = m.sem("s_mm")
        z_mm = m.sem("z_mm")
        score_ok = m.sem("score_ok")
        pick = m.sem("pick")
        PICKS = 8
        pick_seen = m.sem("pick_seen")
        inv_ok = m.sem("inv_ok")
        gate_ok = m.sem("gate_ok")
        ex_ok = m.sem("ex_ok")
        zg_ok = m.sem("zg_ok")
        zt_mm = m.sem("zt_mm")
        zhi_ok = m.sem("zhi_ok")
        zlo_ok = m.sem("zlo_ok")
        o_mm = m.sem("o_mm")
        res_ok = m.sem("res_ok")
        out_st = m.sems("out_st", 2)
        block = ctx.enter_context(nc.Block())

        @block.sync
        def _(sp):
            for dst, src in ((wr[:], io["wr"]), (keys[:], io["keys"]), (ident[:], io["ident"])):
                sp.dma_start(dst, src).then_inc(consts, 16)
            sp.dma_start(w_f[:, 0].rearrange("p (k n) -> p k n", k=KH), io["wz"]).then_inc(w_ldz, 16)
            sp.dma_start(w_f[:, 1].rearrange("p (k n) -> p k n", k=KB), io["wb"]).then_inc(w_ldb, 16)
            for s in range(2):
                sp.sem_inc(out_st[s], 16)
            with sp.Fori(0, BATCH) as b:
                for t in range(TT):
                    i = TT * b + t
                    s = t % 2
                    sp.wait_ge(res_ok, i + 1)
                    sp.dma_start(h1[:, s], one(scr["h1"], i)).then_inc(h1_ld[s], 16)
            for s in range(2):
                sp.wait_ge(out_st[s], 16 * (2 * BATCH + 1))

        @block.tensor
        def _(pe):
            pe.sem_inc(o_mm, 1)
            pe.wait_ge(consts, 48)
            pe.wait_ge(wlo_ok, 2)
            with pe.Fori(0, BATCH) as b:
                for t in range(TT):
                    i = TT * b + t
                    pe.wait_ge(xln_ok, i + 1)
                    for k in range(KH):
                        mm = pe.transpose(p_xt[:, P * k:P * k + P], xln[:, P * k:P * k + P], ident[:, :])
                    mm.then_inc(xt_mm, 1)
                    pe.wait_ge(xf_ok, i + 1)
                    for k in range(KH):
                        mm = pe.matmul(p_q[0:ROUTER, 0:P], wr[:, k, :], x_f[:, k, :], start=(k == 0), stop=(k == KH - 1))
                    mm.then_inc(q_mm, 1)
                    pe.wait_ge(lo_ok, i + 1)
                    for k in range(KH):
                        if k == 2:
                            pe.wait_ge(q_ok, i + 1)
                            pe.matmul(p_s[:, 0:EXPERTS], qt[:, :], keys[:, :], start=True, stop=True).then_inc(s_mm, 1)
                        for n_, (a, e) in enumerate(((0, 0), (1, 0), (0, 1))):
                            mm = pe.matmul(p_z[:], x_hl[:, a, k, :], wz_hl[:, e, k, :],
                                           start=(k == 0 and n_ == 0), stop=(k == KH - 1 and n_ == 2))
                    mm.then_inc(z_mm, 1)
                    pe.wait_ge(zg_ok, i + 1)
                    for k in range(KB):
                        mm = pe.transpose(p_zt[:, P * k:P * k + P], zg[:, P * k:P * k + P], ident[:, :])
                    mm.then_inc(zt_mm, 1)
                    pe.wait_ge(zlo_ok, i + 1)
                    pe.wait_ge(res_ok, i + 2)
                    for k in range(KB):
                        for c in range(HC):
                            for n_, (a, e) in enumerate(((0, 0), (1, 0), (0, 1))):
                                mm = pe.matmul(p_o[:, 512 * c:512 * c + 512], z_hl[:, a, k, :],
                                               wb_hl[:, e, k, 512 * c:512 * c + 512],
                                               start=(k == 0 and n_ == 0), stop=(k == KB - 1 and n_ == 2))
                    mm.then_inc(o_mm, 1)

        @block.scalar
        def _(act):
            act.wait_ge(eps_ok, 1)
            nc.scalar.activation(std[:], stats[:].rearrange("p (i e) -> p i e", e=2)[:, :, 1], ACT.Sqrt,
                                 bias=eps[:, 0:1]).then_inc(std_ok, 1)
            act.wait_ge(w_ldz, 16)
            nc.scalar.copy(wz_hl[:, 0].rearrange("p k n -> p (k n)"), w_f[:, 0]).then_inc(whi_ok, 1)
            act.wait_ge(w_ldb, 16)
            nc.scalar.copy(wb_hl[:, 0].rearrange("p k n -> p (k n)"), w_f[:, 1]).then_inc(whi_ok, 1)
            with act.Fori(0, BATCH) as b:
                for t in range(TT):
                    i = TT * b + t
                    s = t % 2
                    act.wait_ge(xt_mm, i + 1)
                    nc.scalar.copy(x_f[:].rearrange("p k n -> p (k n)"), p_xt[:]).then_inc(xf_ok, 1)
                    act.wait_ge(xf_ok, i + 1)
                    act.wait_ge(o_mm, i + 1)
                    nc.scalar.copy(x_hl[:, 0], x_f[:]).then_inc(hi_ok, 1)
                    act.wait_ge(q_mm, i + 1)
                    nc.scalar.copy(qt[:], p_q[0:ROUTER, 0:P]).then_inc(q_ok, 1)
                    act.wait_ge(pick, PICKS * i + 2)
                    nc.scalar.activation(ex[:], score[:], ACT.Exp, bias=neg_max[:, 0:1]).then_inc(ex_ok, 1)
                    act.wait_ge(zt_mm, i + 1)
                    nc.scalar.copy(z_hl[:, 0].rearrange("p k n -> p (k n)"), p_zt[:]).then_inc(zhi_ok, 1)
                    act.wait_ge(res_ok, i + 3)
                    act.dma_start(one(out, i), res[:, s]).then_inc(out_st[s], 16)

        @block.vector
        def _(dve):
            dve.memset(eps[:], LN_EPS).then_inc(eps_ok, 1)
            dve.sem_inc(res_ok, 2)
            for n_, (hl, f) in enumerate(((wz_hl, 0), (wb_hl, 1))):
                dve.wait_ge(whi_ok, n_ + 1)
                dve.tensor_tensor(hl[:, 1].rearrange("p k n -> p (k n)"), w_f[:, f],
                                  hl[:, 0].rearrange("p k n -> p (k n)"), ALU.subtract).then_inc(wlo_ok, 1)
            dve.wait_ge(std_ok, 1)
            dve.reciprocal(rstd[:], std[:]).then_inc(rstd_ok, 1)
            dve.wait_ge(rstd_ok, 1)
            with dve.Fori(0, BATCH) as b:
                for t in range(TT):
                    i = TT * b + t
                    s = t % 2

                    def picked(k):
                        dve.wait_ge(pick, PICKS * i + k)
                        dve.sem_inc(pick_seen, 1)

                    dve.wait_ge(h1_ld[s], 32 * b + 16 * (t // 2) + 16)
                    dve.tensor_scalar(xln[:], h1[:, s], stats[:, bass.ds(2 * i, 1)], rstd[:, bass.ds(i, 1)],
                                      ALU.subtract, ALU.mult).then_inc(xln_ok, 1)
                    dve.wait_ge(hi_ok, i + 1)
                    dve.tensor_tensor(x_hl[:, 1], x_f[:], x_hl[:, 0], ALU.subtract).then_inc(lo_ok, 1)
                    dve.wait_ge(s_mm, i + 1)
                    dve.tensor_copy(score[:], p_s[:, 0:EXPERTS]).then_inc(score_ok, 1)
                    dve.wait_ge(score_ok, i + 1)
                    dve.sem_inc(pick_seen, 1)
                    dve.max(top[:, 0], score[:]).then_inc(pick, 1)
                    picked(1)
                    dve.tensor_scalar(neg_max[:], top[:, 0, 0:1], -1.0, None, ALU.mult).then_inc(pick, 1)
                    picked(2)
                    dve.match_replace(rest[:, 0], top[:, 0], score[:], NEG).then_inc(pick, 1)
                    picked(3)
                    dve.max(top[:, 1], rest[:, 0]).then_inc(pick, 1)
                    picked(4)
                    dve.match_replace(rest[:, 1], top[:, 1], rest[:, 0], NEG).then_inc(pick, 1)
                    picked(5)
                    dve.tensor_scalar(chosen[:], rest[:, 1], NEG, None, ALU.is_equal).then_inc(pick, 1)
                    picked(6)
                    dve.wait_ge(ex_ok, i + 1)
                    dve.tensor_tensor(chosen[:], chosen[:], ex[:], ALU.mult).then_inc(pick, 1)
                    picked(7)
                    dve.tensor_reduce(total[:], chosen[:], AX_X, ALU.add).then_inc(pick, 1)
                    picked(8)
                    dve.reciprocal(inv[:], total[:]).then_inc(inv_ok, 1)
                    dve.wait_ge(inv_ok, i + 1)
                    dve.tensor_scalar(gate[:].rearrange("p e o -> p (e o)"), chosen[:], inv[:, 0:1], SCALING,
                                      ALU.mult, ALU.mult).then_inc(gate_ok, 1)
                    dve.wait_ge(gate_ok, i + 1)
                    dve.wait_ge(z_mm, i + 1)
                    dve.tensor_tensor(zg[:].rearrange("p (e r) -> p e r", r=RANK),
                                      p_z[:].rearrange("p (e r) -> p e r", r=RANK),
                                      gate[:].to_broadcast([P, EXPERTS, RANK]), ALU.mult).then_inc(zg_ok, 1)
                    dve.wait_ge(zhi_ok, i + 1)
                    dve.tensor_tensor(z_hl[:, 1].rearrange("p k n -> p (k n)"), p_zt[:],
                                      z_hl[:, 0].rearrange("p k n -> p (k n)"), ALU.subtract).then_inc(zlo_ok, 1)
                    dve.wait_ge(o_mm, i + 2)
                    dve.wait_ge(out_st[s], 32 * b + 16 * (t // 2) + 16)
                    dve.tensor_tensor(res[:, s], h1[:, s], p_o[:], ALU.add).then_inc(res_ok, 1)


_IN = ["orig_w", "tok_row", "tok_col", "ids_row", "ids_col", "lower", "tw", "aw", "ab", "bw", "bb", "ident",
       "wpack", "par", "rms_w", "rms_mean", "wo", "wz", "wr", "keys", "wb"]


def lay_out(np, a):
    f = np.ascontiguousarray
    win = a["L0_attn_W_in"].reshape(2, DT, P, KH, P).transpose(1, 4, 3, 0, 2).reshape(DT, P, WU)
    wx = a["L0_attn_Wx"].reshape(XP, DT, P).transpose(1, 2, 0)
    wdt = np.zeros((DT, P, P), np.float32)
    wdt[:, 0:R, :] = a["L0_attn_Wdt"].reshape(DT, P, R).transpose(0, 2, 1)
    par = np.concatenate([a["L0_attn_A"], a["L0_attn_conv_w"], a["L0_attn_conv_b"][:, None],
                          a["L0_attn_dt_bias"][:, None], a["L0_attn_D_param"][:, None]], axis=1)
    mean = np.zeros((XP, XP), np.float32)
    for lo, hi in ((0, R), (R, R + N), (R + N, XP)):
        mean[lo:hi, lo:hi] = 1.0 / (hi - lo)
    return {
        "orig_w": f(a["L0_tok_orig_W"]),
        "tok_row": f(a["x"].reshape(1, BATCH * L)),
        "tok_col": f(a["x"].reshape(BATCH * TT, P).T),
        "ids_row": f(a["L0_tok_ids"].reshape(1, N_IDS)),
        "ids_col": f(a["L0_tok_ids"].reshape(N_IDS, 1)),
        "lower": np.tril(np.ones((N_IDS, N_IDS), np.float32), -1),
        "tw": f(a["L0_tok_trainable_W"].reshape(N_IDS, KH, P).transpose(2, 1, 0)),
        "aw": f(a["L0_tok_A_w"].reshape(INNER, KH, P).transpose(2, 1, 0)),
        "ab": f(a["L0_tok_A_b"].reshape(INNER, 1)),
        "bw": f(a["L0_tok_B_w"].T),
        "bb": f(a["L0_tok_B_b"].reshape(1, H)),
        "ident": np.eye(P, dtype=np.float32),
        "wpack": f(np.concatenate([win, wx, wdt], axis=2)),
        "par": f(par.reshape(DT, P, PAR)),
        "rms_w": f(np.concatenate([a["L0_attn_dt_ln_w"], a["L0_attn_b_ln_w"], a["L0_attn_c_ln_w"]]).reshape(XP, 1)),
        "rms_mean": mean,
        "wo": f(a["L0_attn_W_out"].reshape(H, DT, P).transpose(2, 1, 0)),
        "wz": f(a["L0_ffn_A_w"].reshape(BN, KH, P).transpose(2, 1, 0)),
        "wr": f(a["L0_ffn_Wq_w"].reshape(ROUTER, KH, P).transpose(2, 1, 0)),
        "keys": f(a["L0_ffn_keys"].T),
        "wb": f(a["L0_ffn_B_w"].reshape(H, KB, P).transpose(2, 1, 0)),
    }


def build(nc, io, out):
    scr = {
        "h0": nc.dram_tensor("h0_scratch", (BATCH * TT, P, H), F32).ap(),
        "xln": nc.dram_tensor("xln_scratch", (BATCH, P, 2, KH, L), F32).ap(),
        "w": nc.dram_tensor("w_scratch", (DT, P, 2, WP), F32).ap(),
        "bc": nc.dram_tensor("bc_scratch", (BATCH, 2 * N, L), F32).ap(),
        "u": nc.dram_tensor("u_scratch", (BATCH * DT, P, L), F32).ap(),
        "g": nc.dram_tensor("g_scratch", (BATCH * DT, P, L), F32).ap(),
        "y": nc.dram_tensor("y_scratch", (BATCH * DT, P, L), F32).ap(),
        "h1": nc.dram_tensor("h1_scratch", (BATCH * TT, P, H), F32).ap(),
    }
    embed_phase(nc, io, scr)
    mamba_phase(nc, io, scr)
    with nc.sbuf_tensor("stats", [P, 2 * BATCH * TT], F32) as stats:
        out_phase(nc, io, scr, stats)
        ffn_phase(nc, io, scr, stats, out)


def kernel(**inputs):
    import numpy as _np
    import concourse.bacc as _bacc
    from concourse import mybir as _mybir
    from concourse.bass_utils import run_bass_kernel_spmd as _run

    nc = _bacc.Bacc("TRN2", target_bir_lowering=False, num_devices=1)
    laid = lay_out(_np, {k: _np.asarray(v) for k, v in inputs.items()})
    arrays, io = {}, {}
    for name in _IN:
        a = laid[name]
        arrays[f"in_{name}"] = a
        io[name] = nc.dram_tensor(f"in_{name}", a.shape, _mybir.dt.from_np(a.dtype), kind="ExternalInput").ap()
    out = nc.dram_tensor("out_h", (BATCH * TT, P, H), F32, kind="ExternalOutput").ap()
    build(nc, io, out)
    r = _run(nc, [arrays], core_ids=[0])
    return r.results[0]["out_h"].reshape(BATCH, L, H)
```

```python
from contextlib import ExitStack

import concourse.bass as bass
from concourse import mybir

F32 = mybir.dt.float32
F32R = mybir.dt.float32r
I32 = mybir.dt.int32
U32 = mybir.dt.uint32
ALU = mybir.AluOpType
ACT = mybir.ActivationFunctionType
AX_X = mybir.AxisListType.X

P = 128
BATCH, L = 8, 512
H = 1024
KH = H // P
VOCAB = 8000
N_IDS, INNER = 64, 16
D, N, R, TAPS = 2048, 16, 64, 4
DT = D // P
XP = R + 2 * N
TT = L // P
EXPERTS, RANK, TOP_K, ROUTER = 64, 8, 16, 16
BN = EXPERTS * RANK
KB = BN // P
SCALING = 32 / TOP_K
LN_EPS, RMS_EPS = 1e-5, 1e-6
G = 2
NG = N // G
WU = KH * 2 * P
WP = WU + XP + P
PAR = N + TAPS + 3
CONV_W, CONV_B, DT_B, D_SKIP = N, N + TAPS, N + TAPS + 1, N + TAPS + 2
NEG = -3.0e38
LOG_EXP = "natural_log_exp_and_others"


class Mem:

    def __init__(self, nc, ctx, phase):
        self.nc, self.ctx, self.phase = nc, ctx, phase

    def sb(self, name, shape, dt=F32):
        return self.ctx.enter_context(self.nc.sbuf_tensor(f"{self.phase}_{name}", shape, dt))

    def ps(self, name, shape, dt=F32):
        return self.ctx.enter_context(self.nc.psum_tensor(f"{self.phase}_{name}", shape, dt))

    def sem(self, name):
        return self.ctx.enter_context(self.nc.semaphore(f"{self.phase}_{name}"))

    def sems(self, name, n):
        return [self.sem(f"{name}{i}") for i in range(n)]


def one(ap, i):
    lead = ap[bass.ds(i, 1)]
    names = " ".join("abcde"[:len(ap.shape) - 1])
    return lead.rearrange(f"o {names} -> (o a) {names[2:]}")


def embed_phase(nc, io, scr):
    with ExitStack() as ctx:
        m = Mem(nc, ctx, "emb")
        ids_row = m.sb("ids_row", [N_IDS, BATCH * L], I32)
        tok_col = m.sb("tok_col", [P, BATCH * TT], I32)
        wrap = m.sb("wrap", [P, BATCH * TT], F32)
        row_f = m.sb("row_f", [P, BATCH * TT], F32)
        row_of = m.sb("row_of", [P, BATCH * TT], U32)
        id_col = m.sb("id_col", [N_IDS, 1], I32)
        id_row = m.sb("id_row", [N_IDS, N_IDS], I32)
        same = m.sb("same", [N_IDS, N_IDS])
        lower = m.sb("lower", [N_IDS, N_IDS])
        first = m.sb("first", [N_IDS, 2])
        tw = m.sb("tw", [P, KH, N_IDS])
        aw = m.sb("aw", [P, KH, INNER])
        ab = m.sb("ab", [INNER, 1])
        bw = m.sb("bw", [INNER + 1, H])
        hid = m.sb("hid", [INNER + 1, N_IDS])
        table = m.sb("table", [N_IDS, H])
        ident = m.sb("ident", [P, P])
        diff = m.sb("diff", [N_IDS, 2, P], I32)
        hit = m.sb("hit", [N_IDS, 2, P])
        row = m.sb("row", [P, 2, 1], U32)
        base = m.sb("base", [P, 2, H])
        h0 = m.sb("h0", [P, 2, H])
        stat = m.sb("stat", [P, 2, 12])
        mv = m.sb("mv", [P, 2, 2])
        std = m.sb("std", [P, 2, 1])
        rstd = m.sb("rstd", [P, 2, 1])
        eps = m.sb("eps", [P, 1])
        xln = m.sb("xln", [P, 2, H])
        xhl = m.sb("xhl", [P, 2, 2, H], F32R)
        wf = m.sb("wf", [P, 2, WP])
        whl = m.sb("whl", [P, 2, 2, WP], F32R)
        p_tab = [m.ps(f"p_tab{i}", [P, H]) for i in range(2)]
        p_tr = [m.ps(f"p_tr{i}", [P, H]) for i in range(2)]

        consts = m.sem("consts")
        chain = m.sem("chain")
        hid_mm = m.sem("hid_mm")
        hid_ok = m.sem("hid_ok")
        table_mm = m.sem("table_mm")
        table_ok = m.sem("table_ok")
        row_ok = m.sem("row_ok")
        hit_ok = m.sem("hit_ok")
        gathered = m.sems("gathered", 2)
        tab_mm = m.sem("tab_mm")
        h0_ok = m.sem("h0_ok")
        stats_seen = m.sem("stats_seen")
        row_seen = m.sem("row_seen")
        stats_ok = m.sem("stats_ok")
        mv_ok = m.sem("mv_ok")
        std_ok = m.sem("std_ok")
        rstd_ok = m.sem("rstd_ok")
        xln_ok = m.sem("xln_ok")
        tr_mm = m.sem("tr_mm")
        hi_ok = m.sem("hi_ok")
        lo_ok = m.sem("lo_ok")
        diff_ok = m.sem("diff_ok")
        h0_st = m.sems("h0_st", 2)
        x_st = m.sems("x_st", 2)
        wf_ld = m.sems("wf_ld", 2)
        whi_ok = m.sem("whi_ok")
        wlo_ok = m.sem("wlo_ok")
        w_st = m.sems("w_st", 2)
        wf_free = m.sems("wf_free", 2)
        block = ctx.enter_context(nc.Block())
        N_CONST = 11

        @block.sync
        def _(sp):
            for dst, src in (
                (ids_row[:], io["tok_row"].partition_broadcast(N_IDS).rearrange("p a n -> p (a n)")),
                (id_row[:], io["ids_row"].partition_broadcast(N_IDS).rearrange("p a n -> p (a n)")),
                (tok_col[:], io["tok_col"]), (id_col[:], io["ids_col"]), (lower[:], io["lower"]),
                (tw[:], io["tw"]), (aw[:], io["aw"]), (ab[:], io["ab"]),
                (bw[0:INNER, :], io["bw"]), (bw[INNER:INNER + 1, :], io["bb"]), (ident[:], io["ident"]),
            ):
                sp.dma_start(dst, src).then_inc(consts, 16)
            for s in range(2):
                sp.sem_inc(h0_st[s], 16)
                sp.sem_inc(x_st[s], 16)
                sp.sem_inc(w_st[s], 16)
                sp.sem_inc(wf_free[s], 1)
            with sp.Fori(0, BATCH) as b:
                for s in range(2):
                    sp.wait_ge(wf_free[s], b + 1)
                    sp.dma_start(wf[:, s], one(io["wpack"], 2 * b + s)).then_inc(wf_ld[s], 16)
                for t in range(TT):
                    s = t % 2
                    sp.wait_ge(h0_ok, TT * b + t + 1)
                    sp.dma_start(one(scr["h0"], TT * b + t), h0[:, s]).then_inc(h0_st[s], 16)
                    sp.wait_ge(lo_ok, TT * b + t + 1)
                    sp.dma_start(one(scr["xln"], b).rearrange("p e k (t n) -> p e k t n", t=TT)[:, :, :, t]
                                 .rearrange("p e k n -> p (e k) n"),
                                 xhl[:, s].bitcast(F32).rearrange("p e (k n) -> p (e k) n", k=KH)
                                 ).then_inc(x_st[s], 16)
                    if t >= 2:
                        w = t - 2
                        sp.wait_ge(wlo_ok, 2 * b + w + 1)
                        sp.dma_start(one(scr["w"], 2 * b + w), whl[:, w].bitcast(F32)).then_inc(w_st[w], 16)
            for s in range(2):
                sp.wait_ge(h0_st[s], 16 * (2 * BATCH + 1))
                sp.wait_ge(x_st[s], 16 * (2 * BATCH + 1))
                sp.wait_ge(w_st[s], 16 * (BATCH + 1))

        @block.gpsimd
        def _(pool):
            with pool.Fori(0, BATCH) as b:
                for t in range(TT):
                    s = t % 2
                    pool.wait_ge(row_ok, TT * b + t + 1)
                    pool.sem_inc(row_seen, 1)
                    pool.indirect_dma_start(
                        base[:, s, :], None, io["orig_w"],
                        bass.IndirectOffsetOnAxis(ap=row[:, s, :], axis=0)).then_inc(gathered[s], 16)

        @block.tensor
        def _(pe):
            pe.wait_ge(consts, 16 * N_CONST)
            for k in range(KH):
                mm = pe.matmul(p_tab[0][0:INNER, 0:N_IDS], aw[:, k, :], tw[:, k, :],
                               start=(k == 0), stop=(k == KH - 1))
            mm.then_inc(hid_mm, 1)
            pe.wait_ge(hid_ok, 2)
            for c in range(2):
                mm = pe.matmul(p_tab[1][0:N_IDS, 512 * c:512 * c + 512], hid[:, :], bw[:, 512 * c:512 * c + 512],
                               start=True, stop=True)
            mm.then_inc(table_mm, 1)
            pe.wait_ge(table_ok, 1)
            with pe.Fori(0, BATCH) as b:
                for t in range(TT):
                    s = t % 2
                    pe.wait_ge(hit_ok, TT * b + t + 1)
                    for c in range(2):
                        mm = pe.matmul(p_tab[s][:, 512 * c:512 * c + 512], hit[:, s, :],
                                       table[:, 512 * c:512 * c + 512], start=True, stop=True)
                    mm.then_inc(tab_mm, 1)
                    pe.wait_ge(xln_ok, TT * b + t + 1)
                    for k in range(KH):
                        mm = pe.transpose(p_tr[s][:, P * k:P * k + P], xln[:, s, P * k:P * k + P], ident[:, :])
                    mm.then_inc(tr_mm, 1)

        @block.scalar
        def _(act):
            act.wait_ge(hid_mm, 1)
            act.wait_ge(hid_ok, 1)
            nc.scalar.activation(hid[0:INNER, :], p_tab[0][0:INNER, 0:N_IDS], ACT.Identity,
                                 bias=ab[:, 0:1]).then_inc(hid_ok, 1)
            act.wait_ge(chain, 1)
            with act.Fori(0, BATCH) as b:
                for t in range(TT):
                    s = t % 2
                    act.wait_ge(mv_ok, TT * b + t + 1)
                    nc.scalar.activation(std[:, s], mv[:, s, 1:2], ACT.Sqrt, bias=eps[:, 0:1]).then_inc(std_ok, 1)
                    if t >= 2:
                        w = t - 2
                        act.wait_ge(wf_ld[w], 16 * b + 16)
                        act.wait_ge(w_st[w], 16 * b + 16)
                        nc.scalar.copy(whl[:, w, 0], wf[:, w]).then_inc(whi_ok, 1)
                    act.wait_ge(tr_mm, TT * b + t + 1)
                    act.wait_ge(x_st[s], 32 * b + 16 * (t // 2) + 16)
                    nc.scalar.copy(xhl[:, s, 0], p_tr[s][:, :]).then_inc(hi_ok, 1)

        @block.vector
        def _(dve):
            dve.memset(eps[:], LN_EPS).then_inc(chain, 1)
            dve.memset(hid[:], 1.0).then_inc(hid_ok, 1)
            dve.wait_ge(consts, 16 * N_CONST)
            dve.tensor_scalar(wrap[:], tok_col[:], 0, float(VOCAB), ALU.is_lt, ALU.mult).then_inc(chain, 1)
            dve.wait_ge(chain, 2)
            dve.tensor_tensor(row_f[:], tok_col[:], wrap[:], ALU.add).then_inc(chain, 1)
            dve.wait_ge(chain, 3)
            dve.tensor_scalar(row_of[:], row_f[:], 0.0, float(VOCAB - 1), ALU.max, ALU.min).then_inc(chain, 1)
            dve.tensor_tensor(id_row[:], id_row[:], id_col[:, 0:1].to_broadcast([N_IDS, N_IDS]),
                              ALU.bitwise_xor).then_inc(chain, 1)
            dve.wait_ge(chain, 5)
            dve.tensor_scalar(same[:], id_row[:], 0, None, ALU.is_equal).then_inc(chain, 1)
            dve.wait_ge(chain, 6)
            dve.tensor_tensor(same[:], same[:], lower[:], ALU.mult).then_inc(chain, 1)
            dve.wait_ge(chain, 7)
            dve.tensor_reduce(first[:, 0:1], same[:], AX_X, ALU.max).then_inc(chain, 1)
            dve.wait_ge(chain, 8)
            dve.tensor_scalar(first[:, 1:2], first[:, 0:1], -1.0, 1.0, ALU.mult, ALU.add).then_inc(chain, 1)
            dve.wait_ge(chain, 9)
            dve.wait_ge(table_mm, 1)
            dve.tensor_scalar(table[:], p_tab[1][0:N_IDS, :], first[:, 1:2], None, ALU.mult).then_inc(table_ok, 1)

            with dve.Fori(0, BATCH) as b:
                for t in range(TT):
                    s = t % 2
                    i = TT * b + t
                    dve.tensor_tensor(diff[:, s], ids_row[:, bass.ds(P * i, P)],
                                      id_col[:, 0:1].to_broadcast([N_IDS, P]), ALU.bitwise_xor).then_inc(diff_ok, 1)
                    dve.tensor_copy(row[:, s], row_of[:, bass.ds(i, 1)]).then_inc(row_ok, 1)
                    dve.wait_ge(diff_ok, i + 1)
                    dve.tensor_scalar(hit[:, s], diff[:, s], 0, None, ALU.is_equal).then_inc(hit_ok, 1)
                    dve.wait_ge(gathered[s], 32 * b + 16 * (t // 2) + 16)
                    dve.wait_ge(tab_mm, i + 1)
                    dve.wait_ge(h0_st[s], 32 * b + 16 * (t // 2) + 16)
                    dve.tensor_tensor(h0[:, s], base[:, s], p_tab[s][:, :], ALU.add).then_inc(h0_ok, 1)
                    dve.wait_ge(h0_ok, i + 1)
                    for c in range(2):
                        dve.bn_stats(stat[:, s, 6 * c:6 * c + 6], h0[:, s, 512 * c:512 * c + 512]).then_inc(stats_ok, 1)
                    dve.wait_ge(stats_ok, 2 * i + 2)
                    dve.sem_inc(stats_seen, 1)
                    dve.bn_aggr(mv[:, s], stat[:, s]).then_inc(mv_ok, 1)
                    if t >= 2:
                        w = t - 2
                        dve.wait_ge(whi_ok, 2 * b + w + 1)
                        dve.tensor_tensor(whl[:, w, 1], wf[:, w], whl[:, w, 0], ALU.subtract).then_inc(wlo_ok, 1)
                    dve.wait_ge(std_ok, i + 1)
                    dve.reciprocal(rstd[:, s], std[:, s]).then_inc(rstd_ok, 1)
                    dve.wait_ge(rstd_ok, i + 1)
                    dve.tensor_scalar(xln[:, s], h0[:, s], mv[:, s, 0:1], rstd[:, s, 0:1],
                                      ALU.subtract, ALU.mult).then_inc(xln_ok, 1)
                    dve.wait_ge(hi_ok, i + 1)
                    dve.tensor_tensor(xhl[:, s, 1], p_tr[s][:, :], xhl[:, s, 0], ALU.subtract).then_inc(lo_ok, 1)
                    if t >= 2:
                        dve.wait_ge(wlo_ok, 2 * b + w + 1)
                        dve.sem_inc(wf_free[w], 1)


def mamba_phase(nc, io, scr):
    PAIRS = DT // 2
    HR, DR = 4, 4
    with ExitStack() as ctx:
        m = Mem(nc, ctx, "ssm")
        w = m.sb("w", [P, 2, 2, WU + XP], F32R)
        wdt = m.sb("wdt", [R, 2, 2, P], F32R)
        par = m.sb("par", [P, 2, PAR])
        xln = m.sb("xln", [P, 2, KH, L], F32R)
        b_all = m.sb("b_all", [P, N, L])
        c_all = m.sb("c_all", [P, N, L])
        db = m.sb("db", [P, DR, G, L])
        h = m.sb("h", [P, HR, G, L])
        u = m.sb("u", [P, 2, L])
        u_new = m.sb("u_new", [P, 2, L])
        g_new = m.sb("g_new", [P, L])
        u_pad = m.sb("u_pad", [P, TAPS - 1 + L])
        conv = m.sb("conv", [P, L])
        u_hl = m.sb("u_hl", [P, 2, L], F32R)
        delta = m.sb("delta", [P, 2, L])
        du = m.sb("du", [P, 2, L])
        soft = m.sb("soft", [P, L])
        y = m.sb("y", [P, 2, L])
        dt_hl = m.sb("dt_hl", [R, 2, L], F32R)
        xn = m.sb("xn", [XP, L])
        sq, rs = conv[0:XP, :], soft[0:XP, :]
        rms_w = m.sb("rms_w", [XP, 1])
        rms_mean = m.sb("rms_mean", [XP, XP])
        rms_eps = m.sb("rms_eps", [XP, 1])
        ident = m.sb("ident", [P, P])
        zeros = m.sb("zeros", [P, P], F32R)
        da = m.ps("da", [P, 2, G, L])
        p_y = m.ps("p_y", [P, L])
        p_in = m.ps("p_in", [P, L])
        p_dt = m.ps("p_dt", [P, L])
        p_x = m.ps("p_x", [P, L])

        consts = m.sem("consts")
        zeroed = m.sem("zeroed")
        sp_passed = m.sem("sp_passed")
        w_ld = m.sems("w_ld", 2)
        small_ld = m.sems("small_ld", 2)
        w_used = m.sem("w_used")
        xln_ld = m.sem("xln_ld")
        u_ld = m.sems("u_ld", 2)
        u_st = m.sems("u_st", 2)
        g_st = m.sem("g_st")
        y_st = m.sems("y_st", 2)
        bc_st = m.sem("bc_st")
        b_ld = m.sems("b_ld", NG)
        c_ld = m.sems("c_ld", NG)
        u_mm = m.sem("u_mm")
        g_mm = m.sem("g_mm")
        dt_mm = m.sem("dt_mm")
        x_mm = m.sem("x_mm")
        ms_mm = m.sem("ms_mm")
        h_used = m.sem("h_used")
        up_ok = m.sem("up_ok")
        gn_ok = m.sem("gn_ok")
        un_ok = m.sem("un_ok")
        hi_ok = m.sem("hi_ok")
        lo_ok = m.sem("lo_ok")
        tap_ok = m.sem("tap_ok")
        abs_ok = m.sem("abs_ok")
        exp_ok = m.sem("exp_ok")
        log_ok = m.sem("log_ok")
        max_ok = m.sem("max_ok")
        delta_ok = m.sem("delta_ok")
        du_ok = m.sem("du_ok")
        da_ok = m.sem("da_ok")
        db_ok = m.sem("db_ok")
        scan_ok = m.sem("scan_ok")
        hc_ok = m.sem("hc_ok")
        y_ok = m.sem("y_ok")
        sq_ok = m.sem("sq_ok")
        rlog_ok = m.sem("rlog_ok")
        rs_ok = m.sem("rs_ok")
        xn_ok = m.sem("xn_ok")
        dth_ok = m.sem("dth_ok")
        dtl_ok = m.sem("dtl_ok")
        block = ctx.enter_context(nc.Block())

        def schedule(eng, step, between, start, in_only=True):
            if in_only:
                with eng.Fori(0, PAIRS) as i:
                    for s in range(2):
                        step(s, None, i, 0, False)
            between(0)
            start(0, 0)

            def sequence(b, both):
                lead = PAIRS if both else None
                with eng.Fori(0, PAIRS - 1) as i:
                    for s in range(2):
                        step(s, PAIRS * b + i, PAIRS * b + i + lead if both else None, b, True)
                for s in range(2):
                    last = PAIRS * b + PAIRS - 1
                    step(s, last, last + lead if both else None, b, s == 0)

            with eng.Fori(0, BATCH - 1) as b:
                sequence(b, True)
                between(b + 1)
                start(PAIRS * b + PAIRS, b + 1)
            sequence(BATCH - 1, False)

        def after(s, ps):
            return (1, ps) if s == 0 else (0, ps + 1)

        @block.sync
        def _(sp):
            for dst, src in ((ident[:], io["ident"]), (rms_w[:], io["rms_w"]), (rms_mean[:], io["rms_mean"])):
                sp.dma_start(dst, src).then_inc(consts, 16)

            def load_w(s, dt):
                sp.dma_start(w[:, s].bitcast(F32), one(scr["w"], dt)[:, :, 0:WU + XP]).then_inc(w_ld[s], 16)

            def load_small(s, dt):
                sp.dma_start(par[:, s], one(io["par"], dt)).then_inc(small_ld[s], 16)
                sp.dma_start(wdt[:, s].bitcast(F32), one(scr["w"], dt)[0:R, :, WU + XP:WP]).then_inc(small_ld[s], 16)

            def load_xln(b):
                sp.dma_start(xln[:].bitcast(F32), one(scr["xln"], b)).then_inc(xln_ld, 16)

            def load_u(s, pair):
                sp.wait_ge(u_st[s], 16 * (pair + 2))
                sp.dma_start(u[:, s], one(scr["u"], 2 * pair + s)).then_inc(u_ld[s], 16)

            def step(s, ps, pi, next_w, next_small, next_ug):
                if ps is not None:
                    sp.wait_ge(y_ok, 2 * ps + s + 2)
                    sp.sem_inc(sp_passed, 1)
                    if next_small is not None:
                        load_small(s, next_small)
                    if next_ug:
                        load_u(s, ps + 1)
                    sp.dma_start(one(scr["y"], 2 * ps + s), y[:, s]).then_inc(y_st[s], 16)
                if pi is not None:
                    sp.wait_ge(un_ok, 2 * pi + s + 2)
                    sp.dma_start(one(scr["u"], 2 * pi + s), u_new[:, s]).then_inc(u_st[s], 16)
                    sp.wait_ge(gn_ok, 2 * pi + s + 2)
                    sp.dma_start(one(scr["g"], 2 * pi + s), g_new[:]).then_inc(g_st, 16)
                    if next_w is not None:
                        sp.wait_ge(w_used, 2 * pi + s + 2)
                        sp.sem_inc(sp_passed, 1)
                        load_w(s, next_w)
                    if ps is None:
                        load_small(s, next_small)

            def between(b, again=True):
                sp.wait_ge(xn_ok, b + 1)
                sp.dma_start(one(scr["bc"], b), xn[R:XP, :]).then_inc(bc_st, 16)
                sp.wait_ge(bc_st, 16 * (b + 2))
                for j in range(NG):
                    for all_, ld, ok, first in ((b_all, b_ld, db_ok, 0), (c_all, c_ld, hc_ok, N)):
                        if again:
                            sp.wait_ge(ok, NG * DT * b - NG + j + 1)
                            sp.sem_inc(sp_passed, 1)
                        src = one(scr["bc"], b)[first + G * j:first + G * j + G, :]
                        sp.dma_start(all_[:, G * j:G * j + G, :].rearrange("p n l -> p (n l)"),
                                     src.rearrange("(o n) l -> o (n l)", o=1).partition_broadcast(P)
                                     .rearrange("p o n -> p (o n)")).then_inc(ld[j], 16)

            sp.wait_ge(zeroed, 1)
            for s in range(2):
                sp.sem_inc(u_st[s], 16)
                sp.sem_inc(y_st[s], 16)
            sp.sem_inc(g_st, 16)
            sp.sem_inc(bc_st, 16)
            load_w(0, 0)
            load_xln(0)
            load_w(1, 1)
            load_small(0, 0)
            load_small(1, 1)
            with sp.Fori(0, PAIRS - 1) as i:
                for s in range(2):
                    step(s, None, i, 2 * i + 2 + s, 2 * i + 2 + s, False)
            for s in range(2):
                step(s, None, PAIRS - 1, s, s, False)
            between(0, again=False)
            sp.wait_ge(x_mm, 1)
            load_xln(1)
            for s in range(2):
                load_u(s, 0)

            def both(b, last):
                with sp.Fori(0, PAIRS - 1) as i:
                    for s in range(2):
                        step(s, PAIRS * b + i, PAIRS * b + i + PAIRS, 2 * i + 2 + s, 2 * i + 2 + s, True)
                for s in range(2):
                    step(s, PAIRS * b + PAIRS - 1, PAIRS * b + 2 * PAIRS - 1, None if last else s, s, True)
                between(b + 1)

            with sp.Fori(0, BATCH - 2) as b:
                both(b, False)
                sp.wait_ge(x_mm, b + 2)
                load_xln(b + 2)
            both(BATCH - 2, True)
            with sp.Fori(0, PAIRS - 1) as i:
                for s in range(2):
                    step(s, i + PAIRS * (BATCH - 1), None, None, 2 * i + 2 + s, True)
            for s in range(2):
                step(s, PAIRS * BATCH - 1, None, None, None, False)
            for s in range(2):
                sp.wait_ge(u_st[s], 16 * (PAIRS * BATCH + 1))
                sp.wait_ge(y_st[s], 16 * (PAIRS * BATCH + 1))
            sp.wait_ge(g_st, 16 * (DT * BATCH + 1))
            sp.wait_ge(bc_st, 16 * (BATCH + 1))

        @block.gpsimd
        def _(pool):
            def drive(q, s, groups, b):
                for j in groups:
                    pool.wait_ge(scan_ok, NG * q + j + 1)
                    if s == 0:
                        pool.wait_ge(b_ld[j], 16 * (b + 1))
                    pool.tensor_tensor(db[:, j % DR], du[:, s:s + 1, :].to_broadcast([P, G, L]),
                                       b_all[:, G * j:G * j + G, :], ALU.mult).then_inc(db_ok, 1)

            def make_du(s, ps):
                q = 2 * ps + s
                pool.wait_ge(delta_ok, q + 2)
                pool.wait_ge(u_ld[s], 16 * (ps + 1))
                pool.tensor_tensor(du[:, s], delta[:, s], u[:, s], ALU.mult).then_inc(du_ok, 1)

            def low_u(s, pi):
                pool.wait_ge(hi_ok, 2 * pi + s + 1)
                pool.tensor_tensor(u_hl[:, 1], u_new[:, s], u_hl[:, 0], ALU.subtract).then_inc(lo_ok, 1)

            def step(s, ps, pi, b, nxt):
                if ps is None:
                    low_u(s, pi)
                    return
                q = 2 * ps + s
                drive(q, s, range(4, NG), b)
                if nxt:
                    make_du(*after(s, ps))
                    pool.wait_ge(du_ok, q + 2)
                    drive(q + 1, 1 - s, (0, 1), b)
                if pi is not None:
                    low_u(s, pi)
                if nxt:
                    drive(q + 1, 1 - s, (2, 3), b)

            def start(ps, b):
                make_du(0, ps)
                pool.wait_ge(du_ok, 2 * ps + 1)
                drive(2 * ps, 0, range(4), b)

            schedule(pool, step, lambda b: None, start)

        @block.tensor
        def _(pe):
            def in_mm(s, part, ks, ok):
                for k in ks:
                    at = (2 * k + part) * P
                    for n_, (a, c) in enumerate(((0, 0), (1, 0), (0, 1))):
                        mm = pe.matmul(p_in[:], w[:, s, a, at:at + P], xln[:, c, k, :],
                                       start=(k == 0 and n_ == 0), stop=(k == KH - 1 and n_ == 2))
                if KH - 1 in ks:
                    mm.then_inc(ok, 1)

            def add_group(q, j):
                pe.wait_ge(hc_ok, NG * q + j + 1)
                if j == 0:
                    pe.wait_ge(y_ok, q + 1)
                for n_ in range(G):
                    mm = pe.matmul(p_y[:], ident[:], h[:, j % HR, n_, :], start=(j == 0 and n_ == 0),
                                   stop=(j == NG - 1 and n_ == G - 1))
                mm.then_inc(h_used, 1)

            def dt_product(s, ps, b):
                pe.wait_ge(small_ld[s], 32 * (ps + PAIRS + 1))
                pe.wait_ge(dtl_ok, b + 1)
                pe.wait_ge(delta_ok, 2 * ps + s + 1)
                for n_, (a, c) in enumerate(((0, 0), (1, 0), (0, 1))):
                    mm = pe.matmul(p_dt[:], wdt[:, s, a, :], dt_hl[:, c, :], start=(n_ == 0), stop=(n_ == 2))
                mm.then_inc(dt_mm, 1)

            def x_product(s, pi):
                pe.wait_ge(lo_ok, 2 * pi + s + 1)
                for a, c in ((0, 0), (1, 0), (0, 1)):
                    mm = pe.matmul(p_x[0:XP, :], w[:, s, a, WU:WU + XP], u_hl[:, c, :],
                                   start=False, stop=False, skip_group_check=True)
                mm.then_inc(w_used, 1)

            U_AT = {0: (0, 1, 2), 1: (3, 4, 5), 2: (6, 7)}
            G_AT = {3: (0, 1), 4: (2, 3), 5: (4, 5), 6: (6, 7)}

            def step(s, ps, pi, b, nxt):
                if pi is not None:
                    t = 2 * pi + s
                    pe.wait_ge(w_ld[s], 16 * (pi + 1))
                    pe.wait_ge(xln_ld, 16 * (b + 1) if ps is None else 16 * (b + 2))
                    pe.wait_ge(gn_ok, t + 1)
                if ps is None:
                    in_mm(s, 0, range(KH), u_mm)
                    pe.wait_ge(up_ok, t + 1)
                    in_mm(s, 1, range(KH), g_mm)
                    x_product(s, pi)
                    return
                q = 2 * ps + s
                for j in range(NG):
                    add_group(q, j)
                    if j == 0 and nxt:
                        dt_product(*after(s, ps), b)
                    if pi is not None:
                        if j in U_AT:
                            in_mm(s, 0, U_AT[j], u_mm)
                        if j in G_AT:
                            if 0 in G_AT[j]:
                                pe.wait_ge(up_ok, t + 1)
                            in_mm(s, 1, G_AT[j], g_mm)
                if pi is not None:
                    x_product(s, pi)

            def clear_x(first):
                for c in range(L // P):
                    mm = pe.matmul(p_x[0:XP, P * c:P * c + P], zeros[:, 0:XP], zeros[:], start=first and c == 0,
                                   stop=not first, skip_group_check=True)
                return mm

            def between(b):
                clear_x(False).then_inc(x_mm, 1)
                pe.wait_ge(sq_ok, b + 1)
                pe.wait_ge(gn_ok, DT * b + DT + 1)
                pe.matmul(p_in[0:XP, :], rms_mean[:], sq, start=True, stop=True).then_inc(ms_mm, 1)
                pe.wait_ge(rlog_ok, b + 1)
                pe.wait_ge(xn_ok, b + 1)
                clear_x(True)

            pe.wait_ge(consts, 48)
            pe.wait_ge(zeroed, 1)
            pe.sem_inc(w_used, 1)
            pe.sem_inc(dt_mm, 1)
            pe.sem_inc(h_used, HR)
            clear_x(True)
            schedule(pe, step, between, lambda ps, b: dt_product(0, ps, b))

        @block.scalar
        def _(act):
            def exps(q, s, groups):
                for j in groups:
                    act.wait_ge(scan_ok, NG * q + j + DR - 1)
                    for n_ in range(G):
                        a = nc.scalar.activation(da[:, j % 2, n_, 1:L], delta[:, s, 1:L], ACT.Exp,
                                                 scale=par[:, s, G * j + n_:G * j + n_ + 1])
                    a.then_inc(da_ok, 1)

            def soft_part(s, ps):
                q = 2 * ps + s
                act.wait_ge(dt_mm, q + 2)
                act.wait_ge(delta_ok, q + 1)
                nc.scalar.activation(soft[:], p_dt[:], ACT.Abs, bias=par[:, s, DT_B:DT_B + 1]).then_inc(abs_ok, 1)
                act.wait_ge(abs_ok, q + 1)
                nc.scalar.activation(soft[:], soft[:], ACT.Exp, scale=-1.0).then_inc(exp_ok, 1)
                act.wait_ge(exp_ok, q + 1)
                nc.scalar.activation(soft[:], soft[:], ACT.Ln, bias=1.0).then_inc(log_ok, 1)

            def pad_u(s, pi):
                t = 2 * pi + s
                act.wait_ge(u_mm, t + 1)
                act.wait_ge(tap_ok, TAPS * (t + 1))
                nc.scalar.copy(u_pad[:, TAPS - 1:], p_in[:]).then_inc(up_ok, 1)

            def keep_gate(s, pi):
                t = 2 * pi + s
                act.wait_ge(g_mm, t + 1)
                act.wait_ge(g_st, 16 * (t + 1))
                nc.scalar.copy(g_new[:], p_in[:]).then_inc(gn_ok, 1)

            def silu_u(s, pi):
                t = 2 * pi + s
                act.wait_ge(tap_ok, TAPS * (t + 2))
                act.wait_ge(u_st[s], 16 * (pi + 1))
                nc.scalar.activation(u_new[:, s], conv[:], ACT.Silu).then_inc(un_ok, 1)
                act.wait_ge(un_ok, t + 2)
                act.wait_ge(w_used, t + 1)
                nc.scalar.copy(u_hl[:, 0], u_new[:, s]).then_inc(hi_ok, 1)

            def step(s, ps, pi, b, nxt):
                if ps is None:
                    pad_u(s, pi)
                    silu_u(s, pi)
                    keep_gate(s, pi)
                    return
                q = 2 * ps + s
                exps(q, s, (2, 3, 4))
                if nxt:
                    soft_part(*after(s, ps))
                exps(q, s, (5,))
                if pi is not None:
                    pad_u(s, pi)
                exps(q, s, range(6, NG))
                if nxt:
                    act.wait_ge(delta_ok, q + 3)
                    exps(q + 1, 1 - s, (0, 1))
                if pi is not None:
                    silu_u(s, pi)
                    nc.scalar.preload_act_table_set(LOG_EXP)
                    keep_gate(s, pi)

            def between(b):
                nc.scalar.preload_act_table_set(LOG_EXP)
                act.wait_ge(x_mm, b + 1)
                nc.scalar.activation(sq, p_x[0:XP, :], ACT.Square).then_inc(sq_ok, 1)
                act.wait_ge(ms_mm, b + 1)
                nc.scalar.activation(rs, p_in[0:XP, :], ACT.Ln, bias=rms_eps[:, 0:1]).then_inc(rlog_ok, 1)
                act.wait_ge(rlog_ok, b + 1)
                nc.scalar.activation(rs, rs, ACT.Exp, scale=-0.5).then_inc(rs_ok, 1)
                act.wait_ge(xn_ok, b + 1)
                act.wait_ge(dt_mm, DT * b + 1)
                nc.scalar.copy(dt_hl[:, 0], xn[0:R, :]).then_inc(dth_ok, 1)

            def start(ps, b):
                soft_part(0, ps)
                act.wait_ge(delta_ok, 2 * ps + 2)
                exps(2 * ps, 0, (0, 1))

            act.sem_inc(gn_ok, 1)
            act.sem_inc(un_ok, 1)
            act.wait_ge(zeroed, 1)
            schedule(act, step, between, start)

        @block.vector
        def _(dve):
            dve.memset(u_pad[:, 0:TAPS - 1], 0.0)
            dve.memset(rms_eps[:], RMS_EPS)
            dve.memset(da[:, :, :, 0:1], 0.0)
            dve.memset(zeros[:].bitcast(F32), 0.0).then_inc(zeroed, 1)
            dve.sem_inc(delta_ok, 1)
            dve.sem_inc(y_ok, 1)
            dve.sem_inc(scan_ok, DR)
            dve.sem_inc(tap_ok, TAPS)
            dve.wait_ge(consts, 48)
            dve.wait_ge(zeroed, 1)

            def tap(s, pi, k):
                t = 2 * pi + s
                if k == 0:
                    dve.wait_ge(up_ok, t + 1)
                    dve.wait_ge(un_ok, t + 1)
                    dve.tensor_scalar(conv[:], u_pad[:, TAPS - 1:], par[:, s, CONV_W + 3:CONV_W + 4],
                                      par[:, s, CONV_B:CONV_B + 1], ALU.mult, ALU.add).then_inc(tap_ok, 1)
                else:
                    dve.wait_ge(tap_ok, TAPS * (t + 1) + k)
                    c = TAPS - 1 - k
                    dve.scalar_tensor_tensor(out=conv[:], in0=u_pad[:, c:c + L],
                                             scalar=par[:, s, CONV_W + c:CONV_W + c + 1], in1=conv[:],
                                             op0=ALU.mult, op1=ALU.add).then_inc(tap_ok, 1)

            def scan(q, j):
                dve.wait_ge(da_ok, NG * q + j + 1)
                dve.wait_ge(db_ok, NG * q + j + 1)
                dve.wait_ge(h_used, NG * q + j + 1)
                dve.tensor_tensor_scan(h[:, j % HR].rearrange("p n l -> p (n l)"),
                                       da[:, j % 2].rearrange("p n l -> p (n l)"),
                                       db[:, j % DR].rearrange("p n l -> p (n l)"),
                                       0.0, ALU.mult, ALU.add).then_inc(scan_ok, 1)

            def times_c(q, s, j, b):
                dve.wait_ge(scan_ok, NG * q + j + DR + 1)
                if s == 0:
                    dve.wait_ge(c_ld[j], 16 * (b + 1))
                dve.tensor_tensor(h[:, j % HR], h[:, j % HR], c_all[:, G * j:G * j + G, :],
                                  ALU.mult).then_inc(hc_ok, 1)

            def delta_max(s, ps):
                dve.wait_ge(abs_ok, 2 * ps + s + 1)
                dve.tensor_scalar(delta[:, s], p_dt[:], par[:, s, DT_B:DT_B + 1], 0.0,
                                  ALU.add, ALU.max).then_inc(max_ok, 1)

            def delta_add(s, ps):
                q = 2 * ps + s
                dve.wait_ge(max_ok, q + 1)
                dve.wait_ge(log_ok, q + 1)
                dve.tensor_tensor(delta[:, s], delta[:, s], soft[:], ALU.add).then_inc(delta_ok, 1)

            def step(s, ps, pi, b, nxt):
                if ps is None:
                    dve.wait_ge(small_ld[s], 32 * (pi + 1))
                    for k in range(TAPS):
                        tap(s, pi, k)
                    return
                q = 2 * ps + s
                for j in range(NG):
                    times_c(q, s, j, b)
                    if j + 2 < NG:
                        scan(q, j + 2)
                    if nxt and j == 4:
                        delta_max(*after(s, ps))
                    if nxt and j == 5:
                        delta_add(*after(s, ps))
                    if pi is not None and j >= NG - TAPS:
                        tap(s, pi, j - (NG - TAPS))
                if nxt:
                    scan(q + 1, 0)
                    scan(q + 1, 1)
                dve.wait_ge(h_used, NG * q + NG + HR)
                dve.wait_ge(y_st[s], 16 * (ps + 1))
                dve.scalar_tensor_tensor(out=y[:, s], in0=u[:, s], scalar=par[:, s, D_SKIP:D_SKIP + 1], in1=p_y[:],
                                         op0=ALU.mult, op1=ALU.add).then_inc(y_ok, 1)

            def between(b):
                dve.wait_ge(rs_ok, b + 1)
                dve.wait_ge(bc_st, 16 * (b + 1))
                dve.scalar_tensor_tensor(out=xn[:], in0=p_x[0:XP, :], scalar=rms_w[:, 0:1], in1=rs,
                                         op0=ALU.mult, op1=ALU.mult).then_inc(xn_ok, 1)
                dve.wait_ge(xn_ok, b + 1)
                dve.wait_ge(dth_ok, b + 1)
                dve.tensor_tensor(dt_hl[:, 1], xn[0:R, :], dt_hl[:, 0], ALU.subtract).then_inc(dtl_ok, 1)

            def start(ps, b):
                delta_max(0, ps)
                delta_add(0, ps)
                scan(2 * ps, 0)
                scan(2 * ps, 1)

            schedule(dve, step, between, start)


def out_phase(nc, io, scr, stats):
    HC = H // 512
    with ExitStack() as ctx:
        m = Mem(nc, ctx, "out")
        wo_hl = m.sb("wo_hl", [P, 2, DT, H], F32R)
        wo = m.sb("wo", [P, 2, H])
        y = m.sb("y", [P, 2, DT, P])
        g = m.sb("g", [P, DT, P])
        y_hl = m.sb("y_hl", [P, 2, DT, P], F32R)
        y_hl2 = m.sb("y_hl2", [P, 2, DT, P], F32R)
        h0 = m.sb("h0", [P, H])
        h1 = m.sb("h1", [P, H])
        ys = (y_hl, y_hl2)
        p_o = [m.ps(f"p_o{i}", [P, H]) for i in range(2)]
        bstat = m.sb("bstat", [P, 12])
        mv = m.sb("mv", [P, 2])

        wo_ld = m.sems("wo_ld", 2)
        whi_ok = m.sem("whi_ok")
        wlo_ok = m.sem("wlo_ok")
        y_ld = m.sems("y_ld", 2)
        g_ld = m.sem("g_ld")
        silu_ok = m.sem("silu_ok")
        yg_ok = m.sem("yg_ok")
        h0_ld = m.sem("h0_ld")
        hi_ok = m.sem("hi_ok")
        lo_ok = m.sem("lo_ok")
        o_mm = m.sem("o_mm")
        h1_ok = m.sem("h1_ok")
        h1_st = m.sem("h1_st")
        bn_ok = m.sem("bn_ok")
        bn_seen = m.sem("bn_seen")
        mv_ok = m.sem("mv_ok")
        st_ok = m.sem("st_ok")
        block = ctx.enter_context(nc.Block())

        def tile_of(ap, b, t):
            return (ap.rearrange("(b k) p l -> b p k l", b=BATCH)[bass.ds(b, 1), :, :, P * t:P * t + P]
                    .rearrange("o p k l -> p (o k) l"))

        @block.sync
        def _(sp):
            sp.sem_inc(h1_st, 16)
            for k in range(DT):
                if k >= 2:
                    sp.wait_ge(wlo_ok, k - 1)
                sp.dma_start(wo[:, k % 2], io["wo"][:, k, :]).then_inc(wo_ld[k % 2], 16)
            with sp.Fori(0, BATCH) as b:
                for t in range(TT):
                    i = TT * b + t
                    s = t % 2
                    sp.wait_ge(yg_ok, i + 1)
                    sp.dma_start(g[:], tile_of(scr["g"], b, t)).then_inc(g_ld, 16)
                    sp.wait_ge(lo_ok, i + 1)
                    sp.dma_start(y[:, s], tile_of(scr["y"], b, t)).then_inc(y_ld[s], 16)
                    sp.wait_ge(h1_ok, i + 2)
                    sp.dma_start(h0[:], one(scr["h0"], i)).then_inc(h0_ld, 16)
            sp.wait_ge(h1_st, 16 * (BATCH * TT + 1))

        @block.tensor
        def _(pe):
            pe.sem_inc(o_mm, 2)
            pe.wait_ge(wlo_ok, DT)
            with pe.Fori(0, BATCH) as b:
                for t in range(TT):
                    i = TT * b + t
                    s = t % 2
                    pe.wait_ge(lo_ok, i + 3)
                    pe.wait_ge(h1_ok, i + 1)
                    for k in range(DT):
                        for c in range(HC):
                            for n_, (a, e) in enumerate(((0, 0), (1, 0), (0, 1))):
                                mm = pe.matmul(p_o[s][:, 512 * c:512 * c + 512], ys[s][:, a, k, :],
                                               wo_hl[:, e, k, 512 * c:512 * c + 512],
                                               start=(k == 0 and n_ == 0), stop=(k == DT - 1 and n_ == 2))
                    mm.then_inc(o_mm, 1)

        @block.scalar
        def _(act):
            for k in range(DT):
                act.wait_ge(wo_ld[k % 2], 16 * (k // 2 + 1))
                nc.scalar.copy(wo_hl[:, 0, k, :], wo[:, k % 2]).then_inc(whi_ok, 1)

            def high(i, b, t):
                s = t % 2
                act.wait_ge(g_ld, 16 * i + 16)
                nc.scalar.activation(g[:], g[:], ACT.Silu).then_inc(silu_ok, 1)
                act.wait_ge(yg_ok, i + 2)
                act.wait_ge(o_mm, i + 1)
                nc.scalar.copy(ys[s][:, 0], y[:, s]).then_inc(hi_ok, 1)

            def tiles(b, last=False):
                for t in range(TT):
                    i = TT * b + t
                    if t < TT - 1:
                        high(i + 1, b, t + 1)
                    elif not last:
                        high(i + 1, b + 1, 0)
                    act.wait_ge(h1_ok, i + 3)
                    act.dma_start(one(scr["h1"], i), h1[:]).then_inc(h1_st, 16)

            high(0, 0, 0)
            with act.Fori(0, BATCH - 1) as b:
                tiles(b)
            tiles(BATCH - 1, last=True)

        @block.vector
        def _(dve):
            dve.sem_inc(lo_ok, 2)
            dve.sem_inc(yg_ok, 1)
            dve.sem_inc(h1_ok, 2)
            for k in range(DT):
                dve.wait_ge(whi_ok, k + 1)
                dve.tensor_tensor(wo_hl[:, 1, k, :], wo[:, k % 2], wo_hl[:, 0, k, :], ALU.subtract).then_inc(wlo_ok, 1)

            def low(i, b, t):
                s = t % 2
                dve.wait_ge(y_ld[s], 32 * b + 16 * (t // 2) + 16)
                dve.wait_ge(silu_ok, i + 1)
                dve.tensor_tensor(y[:, s], y[:, s], g[:], ALU.mult).then_inc(yg_ok, 1)
                dve.wait_ge(hi_ok, i + 1)
                dve.tensor_tensor(ys[s][:, 1], y[:, s], ys[s][:, 0], ALU.subtract).then_inc(lo_ok, 1)

            def tiles(b, last=False):
                for t in range(TT):
                    i = TT * b + t
                    s = t % 2
                    if t < TT - 1:
                        low(i + 1, b, t + 1)
                    elif not last:
                        low(i + 1, b + 1, 0)
                    dve.wait_ge(o_mm, i + 3)
                    dve.wait_ge(h0_ld, 16 * i + 16)
                    dve.wait_ge(h1_st, 16 * i + 16)
                    dve.tensor_tensor(h1[:], h0[:], p_o[s][:, :], ALU.add).then_inc(h1_ok, 1)
                    dve.wait_ge(h1_ok, i + 3)
                    for c in range(HC):
                        dve.bn_stats(bstat[:, 6 * c:6 * c + 6], h1[:, 512 * c:512 * c + 512]).then_inc(bn_ok, 1)
                    dve.wait_ge(bn_ok, 2 * i + 2)
                    dve.sem_inc(bn_seen, 1)
                    dve.bn_aggr(mv[:], bstat[:]).then_inc(mv_ok, 1)
                    dve.wait_ge(mv_ok, i + 1)
                    dve.tensor_scalar(stats[:, bass.ds(2 * i, 2)], mv[:], 1.0, None, ALU.mult).then_inc(st_ok, 1)

            low(0, 0, 0)
            with dve.Fori(0, BATCH - 1) as b:
                tiles(b)
            tiles(BATCH - 1, last=True)
            dve.wait_ge(st_ok, BATCH * TT)


def ffn_phase(nc, io, scr, stats, out):
    HC = H // 512
    with ExitStack() as ctx:
        m = Mem(nc, ctx, "ffn")
        wz_hl = m.sb("wz_hl", [P, 2, KH, BN], F32R)
        wb_hl = m.sb("wb_hl", [P, 2, KB, H], F32R)
        w_f = m.sb("w_f", [P, 2, KH * BN])
        wr = m.sb("wr", [P, KH, ROUTER])
        keys = m.sb("keys", [ROUTER, EXPERTS])
        ident = m.sb("ident", [P, P])
        rstd = m.sb("rstd", [P, BATCH * TT])
        std = m.sb("std", [P, BATCH * TT])
        eps = m.sb("eps", [P, 1])
        h1 = m.sb("h1", [P, 2, H])
        xln = m.sb("xln", [P, H])
        x_f = m.sb("x_f", [P, KH, P])
        x_hl = m.sb("x_hl", [P, 2, KH, P], F32R)
        qt = m.sb("qt", [ROUTER, P])
        score = m.sb("score", [P, EXPERTS])
        rest = m.sb("rest", [P, 2, EXPERTS])
        top = m.sb("top", [P, 2, 8])
        neg_max = m.sb("neg_max", [P, 1])
        ex = m.sb("ex", [P, EXPERTS])
        chosen = m.sb("chosen", [P, EXPERTS])
        total = m.sb("total", [P, 1])
        inv = m.sb("inv", [P, 1])
        gate = m.sb("gate", [P, EXPERTS, 1])
        zg = m.sb("zg", [P, BN])
        z_hl = m.sb("z_hl", [P, 2, KB, P], F32R)
        res = m.sb("res", [P, 2, H])
        p_xt = m.ps("p_xt", [P, H])
        p_z = m.ps("p_z", [P, BN])
        p_q = m.ps("p_q", [P, 512])
        p_s = m.ps("p_s", [P, 512])
        p_zt = m.ps("p_zt", [P, KB * P])
        p_o = m.ps("p_o", [P, H])

        consts = m.sem("consts")
        w_ldz = m.sem("w_ldz")
        w_ldb = m.sem("w_ldb")
        whi_ok = m.sem("whi_ok")
        wlo_ok = m.sem("wlo_ok")
        eps_ok = m.sem("eps_ok")
        std_ok = m.sem("std_ok")
        rstd_ok = m.sem("rstd_ok")
        h1_ld = m.sems("h1_ld", 2)
        xln_ok = m.sem("xln_ok")
        xt_mm = m.sem("xt_mm")
        xf_ok = m.sem("xf_ok")
        hi_ok = m.sem("hi_ok")
        lo_ok = m.sem("lo_ok")
        q_mm = m.sem("q_mm")
        q_ok = m.sem("q_ok")
        s_mm = m.sem("s_mm")
        z_mm = m.sem("z_mm")
        score_ok = m.sem("score_ok")
        pick = m.sem("pick")
        PICKS = 8
        pick_seen = m.sem("pick_seen")
        inv_ok = m.sem("inv_ok")
        gate_ok = m.sem("gate_ok")
        ex_ok = m.sem("ex_ok")
        zg_ok = m.sem("zg_ok")
        zt_mm = m.sem("zt_mm")
        zhi_ok = m.sem("zhi_ok")
        zlo_ok = m.sem("zlo_ok")
        o_mm = m.sem("o_mm")
        res_ok = m.sem("res_ok")
        out_st = m.sems("out_st", 2)
        block = ctx.enter_context(nc.Block())

        @block.sync
        def _(sp):
            for dst, src in ((wr[:], io["wr"]), (keys[:], io["keys"]), (ident[:], io["ident"])):
                sp.dma_start(dst, src).then_inc(consts, 16)
            sp.dma_start(w_f[:, 0].rearrange("p (k n) -> p k n", k=KH), io["wz"]).then_inc(w_ldz, 16)
            sp.dma_start(w_f[:, 1].rearrange("p (k n) -> p k n", k=KB), io["wb"]).then_inc(w_ldb, 16)
            for s in range(2):
                sp.sem_inc(out_st[s], 16)
            with sp.Fori(0, BATCH) as b:
                for t in range(TT):
                    i = TT * b + t
                    s = t % 2
                    sp.wait_ge(res_ok, i + 1)
                    sp.dma_start(h1[:, s], one(scr["h1"], i)).then_inc(h1_ld[s], 16)
            for s in range(2):
                sp.wait_ge(out_st[s], 16 * (2 * BATCH + 1))

        @block.tensor
        def _(pe):
            pe.sem_inc(o_mm, 1)
            pe.wait_ge(consts, 48)
            pe.wait_ge(wlo_ok, 2)
            with pe.Fori(0, BATCH) as b:
                for t in range(TT):
                    i = TT * b + t
                    pe.wait_ge(xln_ok, i + 1)
                    for k in range(KH):
                        mm = pe.transpose(p_xt[:, P * k:P * k + P], xln[:, P * k:P * k + P], ident[:, :])
                    mm.then_inc(xt_mm, 1)
                    pe.wait_ge(xf_ok, i + 1)
                    for k in range(KH):
                        mm = pe.matmul(p_q[0:ROUTER, 0:P], wr[:, k, :], x_f[:, k, :], start=(k == 0), stop=(k == KH - 1))
                    mm.then_inc(q_mm, 1)
                    pe.wait_ge(lo_ok, i + 1)
                    for k in range(KH):
                        if k == 2:
                            pe.wait_ge(q_ok, i + 1)
                            pe.matmul(p_s[:, 0:EXPERTS], qt[:, :], keys[:, :], start=True, stop=True).then_inc(s_mm, 1)
                        for n_, (a, e) in enumerate(((0, 0), (1, 0), (0, 1))):
                            mm = pe.matmul(p_z[:], x_hl[:, a, k, :], wz_hl[:, e, k, :],
                                           start=(k == 0 and n_ == 0), stop=(k == KH - 1 and n_ == 2))
                    mm.then_inc(z_mm, 1)
                    pe.wait_ge(zg_ok, i + 1)
                    for k in range(KB):
                        mm = pe.transpose(p_zt[:, P * k:P * k + P], zg[:, P * k:P * k + P], ident[:, :])
                    mm.then_inc(zt_mm, 1)
                    pe.wait_ge(zlo_ok, i + 1)
                    pe.wait_ge(res_ok, i + 2)
                    for k in range(KB):
                        for c in range(HC):
                            for n_, (a, e) in enumerate(((0, 0), (1, 0), (0, 1))):
                                mm = pe.matmul(p_o[:, 512 * c:512 * c + 512], z_hl[:, a, k, :],
                                               wb_hl[:, e, k, 512 * c:512 * c + 512],
                                               start=(k == 0 and n_ == 0), stop=(k == KB - 1 and n_ == 2))
                    mm.then_inc(o_mm, 1)

        @block.scalar
        def _(act):
            act.wait_ge(eps_ok, 1)
            nc.scalar.activation(std[:], stats[:].rearrange("p (i e) -> p i e", e=2)[:, :, 1], ACT.Sqrt,
                                 bias=eps[:, 0:1]).then_inc(std_ok, 1)
            act.wait_ge(w_ldz, 16)
            nc.scalar.copy(wz_hl[:, 0].rearrange("p k n -> p (k n)"), w_f[:, 0]).then_inc(whi_ok, 1)
            act.wait_ge(w_ldb, 16)
            nc.scalar.copy(wb_hl[:, 0].rearrange("p k n -> p (k n)"), w_f[:, 1]).then_inc(whi_ok, 1)
            with act.Fori(0, BATCH) as b:
                for t in range(TT):
                    i = TT * b + t
                    s = t % 2
                    act.wait_ge(xt_mm, i + 1)
                    nc.scalar.copy(x_f[:].rearrange("p k n -> p (k n)"), p_xt[:]).then_inc(xf_ok, 1)
                    act.wait_ge(xf_ok, i + 1)
                    act.wait_ge(o_mm, i + 1)
                    nc.scalar.copy(x_hl[:, 0], x_f[:]).then_inc(hi_ok, 1)
                    act.wait_ge(q_mm, i + 1)
                    nc.scalar.copy(qt[:], p_q[0:ROUTER, 0:P]).then_inc(q_ok, 1)
                    act.wait_ge(pick, PICKS * i + 2)
                    nc.scalar.activation(ex[:], score[:], ACT.Exp, bias=neg_max[:, 0:1]).then_inc(ex_ok, 1)
                    act.wait_ge(zt_mm, i + 1)
                    nc.scalar.copy(z_hl[:, 0].rearrange("p k n -> p (k n)"), p_zt[:]).then_inc(zhi_ok, 1)
                    act.wait_ge(res_ok, i + 3)
                    act.dma_start(one(out, i), res[:, s]).then_inc(out_st[s], 16)

        @block.vector
        def _(dve):
            dve.memset(eps[:], LN_EPS).then_inc(eps_ok, 1)
            dve.sem_inc(res_ok, 2)
            for n_, (hl, f) in enumerate(((wz_hl, 0), (wb_hl, 1))):
                dve.wait_ge(whi_ok, n_ + 1)
                dve.tensor_tensor(hl[:, 1].rearrange("p k n -> p (k n)"), w_f[:, f],
                                  hl[:, 0].rearrange("p k n -> p (k n)"), ALU.subtract).then_inc(wlo_ok, 1)
            dve.wait_ge(std_ok, 1)
            dve.reciprocal(rstd[:], std[:]).then_inc(rstd_ok, 1)
            dve.wait_ge(rstd_ok, 1)
            with dve.Fori(0, BATCH) as b:
                for t in range(TT):
                    i = TT * b + t
                    s = t % 2

                    def picked(k):
                        dve.wait_ge(pick, PICKS * i + k)
                        dve.sem_inc(pick_seen, 1)

                    dve.wait_ge(h1_ld[s], 32 * b + 16 * (t // 2) + 16)
                    dve.tensor_scalar(xln[:], h1[:, s], stats[:, bass.ds(2 * i, 1)], rstd[:, bass.ds(i, 1)],
                                      ALU.subtract, ALU.mult).then_inc(xln_ok, 1)
                    dve.wait_ge(hi_ok, i + 1)
                    dve.tensor_tensor(x_hl[:, 1], x_f[:], x_hl[:, 0], ALU.subtract).then_inc(lo_ok, 1)
                    dve.wait_ge(s_mm, i + 1)
                    dve.tensor_copy(score[:], p_s[:, 0:EXPERTS]).then_inc(score_ok, 1)
                    dve.wait_ge(score_ok, i + 1)
                    dve.sem_inc(pick_seen, 1)
                    dve.max(top[:, 0], score[:]).then_inc(pick, 1)
                    picked(1)
                    dve.tensor_scalar(neg_max[:], top[:, 0, 0:1], -1.0, None, ALU.mult).then_inc(pick, 1)
                    picked(2)
                    dve.match_replace(rest[:, 0], top[:, 0], score[:], NEG).then_inc(pick, 1)
                    picked(3)
                    dve.max(top[:, 1], rest[:, 0]).then_inc(pick, 1)
                    picked(4)
                    dve.match_replace(rest[:, 1], top[:, 1], rest[:, 0], NEG).then_inc(pick, 1)
                    picked(5)
                    dve.tensor_scalar(chosen[:], rest[:, 1], NEG, None, ALU.is_equal).then_inc(pick, 1)
                    picked(6)
                    dve.wait_ge(ex_ok, i + 1)
                    dve.tensor_tensor(chosen[:], chosen[:], ex[:], ALU.mult).then_inc(pick, 1)
                    picked(7)
                    dve.tensor_reduce(total[:], chosen[:], AX_X, ALU.add).then_inc(pick, 1)
                    picked(8)
                    dve.reciprocal(inv[:], total[:]).then_inc(inv_ok, 1)
                    dve.wait_ge(inv_ok, i + 1)
                    dve.tensor_scalar(gate[:].rearrange("p e o -> p (e o)"), chosen[:], inv[:, 0:1], SCALING,
                                      ALU.mult, ALU.mult).then_inc(gate_ok, 1)
                    dve.wait_ge(gate_ok, i + 1)
                    dve.wait_ge(z_mm, i + 1)
                    dve.tensor_tensor(zg[:].rearrange("p (e r) -> p e r", r=RANK),
                                      p_z[:].rearrange("p (e r) -> p e r", r=RANK),
                                      gate[:].to_broadcast([P, EXPERTS, RANK]), ALU.mult).then_inc(zg_ok, 1)
                    dve.wait_ge(zhi_ok, i + 1)
                    dve.tensor_tensor(z_hl[:, 1].rearrange("p k n -> p (k n)"), p_zt[:],
                                      z_hl[:, 0].rearrange("p k n -> p (k n)"), ALU.subtract).then_inc(zlo_ok, 1)
                    dve.wait_ge(o_mm, i + 2)
                    dve.wait_ge(out_st[s], 32 * b + 16 * (t // 2) + 16)
                    dve.tensor_tensor(res[:, s], h1[:, s], p_o[:], ALU.add).then_inc(res_ok, 1)


_IN = ["orig_w", "tok_row", "tok_col", "ids_row", "ids_col", "lower", "tw", "aw", "ab", "bw", "bb", "ident",
       "wpack", "par", "rms_w", "rms_mean", "wo", "wz", "wr", "keys", "wb"]


def lay_out(np, a):
    f = np.ascontiguousarray
    win = a["L0_attn_W_in"].reshape(2, DT, P, KH, P).transpose(1, 4, 3, 0, 2).reshape(DT, P, WU)
    wx = a["L0_attn_Wx"].reshape(XP, DT, P).transpose(1, 2, 0)
    wdt = np.zeros((DT, P, P), np.float32)
    wdt[:, 0:R, :] = a["L0_attn_Wdt"].reshape(DT, P, R).transpose(0, 2, 1)
    par = np.concatenate([a["L0_attn_A"], a["L0_attn_conv_w"], a["L0_attn_conv_b"][:, None],
                          a["L0_attn_dt_bias"][:, None], a["L0_attn_D_param"][:, None]], axis=1)
    mean = np.zeros((XP, XP), np.float32)
    for lo, hi in ((0, R), (R, R + N), (R + N, XP)):
        mean[lo:hi, lo:hi] = 1.0 / (hi - lo)
    return {
        "orig_w": f(a["L0_tok_orig_W"]),
        "tok_row": f(a["x"].reshape(1, BATCH * L)),
        "tok_col": f(a["x"].reshape(BATCH * TT, P).T),
        "ids_row": f(a["L0_tok_ids"].reshape(1, N_IDS)),
        "ids_col": f(a["L0_tok_ids"].reshape(N_IDS, 1)),
        "lower": np.tril(np.ones((N_IDS, N_IDS), np.float32), -1),
        "tw": f(a["L0_tok_trainable_W"].reshape(N_IDS, KH, P).transpose(2, 1, 0)),
        "aw": f(a["L0_tok_A_w"].reshape(INNER, KH, P).transpose(2, 1, 0)),
        "ab": f(a["L0_tok_A_b"].reshape(INNER, 1)),
        "bw": f(a["L0_tok_B_w"].T),
        "bb": f(a["L0_tok_B_b"].reshape(1, H)),
        "ident": np.eye(P, dtype=np.float32),
        "wpack": f(np.concatenate([win, wx, wdt], axis=2)),
        "par": f(par.reshape(DT, P, PAR)),
        "rms_w": f(np.concatenate([a["L0_attn_dt_ln_w"], a["L0_attn_b_ln_w"], a["L0_attn_c_ln_w"]]).reshape(XP, 1)),
        "rms_mean": mean,
        "wo": f(a["L0_attn_W_out"].reshape(H, DT, P).transpose(2, 1, 0)),
        "wz": f(a["L0_ffn_A_w"].reshape(BN, KH, P).transpose(2, 1, 0)),
        "wr": f(a["L0_ffn_Wq_w"].reshape(ROUTER, KH, P).transpose(2, 1, 0)),
        "keys": f(a["L0_ffn_keys"].T),
        "wb": f(a["L0_ffn_B_w"].reshape(H, KB, P).transpose(2, 1, 0)),
    }


def build(nc, io, out):
    scr = {
        "h0": nc.dram_tensor("h0_scratch", (BATCH * TT, P, H), F32).ap(),
        "xln": nc.dram_tensor("xln_scratch", (BATCH, P, 2, KH, L), F32).ap(),
        "w": nc.dram_tensor("w_scratch", (DT, P, 2, WP), F32).ap(),
        "bc": nc.dram_tensor("bc_scratch", (BATCH, 2 * N, L), F32).ap(),
        "u": nc.dram_tensor("u_scratch", (BATCH * DT, P, L), F32).ap(),
        "g": nc.dram_tensor("g_scratch", (BATCH * DT, P, L), F32).ap(),
        "y": nc.dram_tensor("y_scratch", (BATCH * DT, P, L), F32).ap(),
        "h1": nc.dram_tensor("h1_scratch", (BATCH * TT, P, H), F32).ap(),
    }
    embed_phase(nc, io, scr)
    mamba_phase(nc, io, scr)
    with nc.sbuf_tensor("stats", [P, 2 * BATCH * TT], F32) as stats:
        out_phase(nc, io, scr, stats)
        ffn_phase(nc, io, scr, stats, out)


def kernel(**inputs):
    import numpy as _np
    import concourse.bacc as _bacc
    from concourse import mybir as _mybir
    from concourse.bass_utils import run_bass_kernel_spmd as _run

    nc = _bacc.Bacc("TRN2", target_bir_lowering=False, num_devices=1)
    laid = lay_out(_np, {k: _np.asarray(v) for k, v in inputs.items()})
    arrays, io = {}, {}
    for name in _IN:
        a = laid[name]
        arrays[f"in_{name}"] = a
        io[name] = nc.dram_tensor(f"in_{name}", a.shape, _mybir.dt.from_np(a.dtype), kind="ExternalInput").ap()
    out = nc.dram_tensor("out_h", (BATCH * TT, P, H), F32, kind="ExternalOutput").ap()
    build(nc, io, out)
    r = _run(nc, [arrays], core_ids=[0])
    return r.results[0]["out_h"].reshape(BATCH, L, H)
```

```python
from contextlib import ExitStack

import concourse.bass as bass
from concourse import mybir

F32 = mybir.dt.float32
F32R = mybir.dt.float32r
I32 = mybir.dt.int32
U32 = mybir.dt.uint32
ALU = mybir.AluOpType
ACT = mybir.ActivationFunctionType
AX_X = mybir.AxisListType.X

P = 128
BATCH, L = 8, 512
H = 1024
KH = H // P
VOCAB = 8000
N_IDS, INNER = 64, 16
D, N, R, TAPS = 2048, 16, 64, 4
DT = D // P
XP = R + 2 * N
TT = L // P
EXPERTS, RANK, TOP_K, ROUTER = 64, 8, 16, 16
BN = EXPERTS * RANK
KB = BN // P
SCALING = 32 / TOP_K
LN_EPS, RMS_EPS = 1e-5, 1e-6
G = 2
NG = N // G
WU = KH * 2 * P
WP = WU + XP + P
PAR = N + TAPS + 3
CONV_W, CONV_B, DT_B, D_SKIP = N, N + TAPS, N + TAPS + 1, N + TAPS + 2
NEG = -3.0e38
LOG_EXP = "natural_log_exp_and_others"


class Mem:

    def __init__(self, nc, ctx, phase):
        self.nc, self.ctx, self.phase = nc, ctx, phase

    def sb(self, name, shape, dt=F32):
        return self.ctx.enter_context(self.nc.sbuf_tensor(f"{self.phase}_{name}", shape, dt))

    def ps(self, name, shape, dt=F32):
        return self.ctx.enter_context(self.nc.psum_tensor(f"{self.phase}_{name}", shape, dt))

    def sem(self, name):
        return self.ctx.enter_context(self.nc.semaphore(f"{self.phase}_{name}"))

    def sems(self, name, n):
        return [self.sem(f"{name}{i}") for i in range(n)]


def one(ap, i):
    lead = ap[bass.ds(i, 1)]
    names = " ".join("abcde"[:len(ap.shape) - 1])
    return lead.rearrange(f"o {names} -> (o a) {names[2:]}")


def run_tiles(eng, tile):
    with eng.Fori(0, BATCH - 1) as b:
        for t in range(TT):
            tile(b, t, lambda v: True)
    for t in range(TT):
        tile(BATCH - 1, t, lambda v: v < TT)


def embed_phase(nc, io, scr):
    with ExitStack() as ctx:
        m = Mem(nc, ctx, "emb")
        ids_row = m.sb("ids_row", [N_IDS, BATCH * L], I32)
        tok_col = m.sb("tok_col", [P, BATCH * TT], I32)
        wrap = m.sb("wrap", [P, BATCH * TT], F32)
        row_f = m.sb("row_f", [P, BATCH * TT], F32)
        row_of = m.sb("row_of", [P, BATCH * TT], U32)
        id_col = m.sb("id_col", [N_IDS, 1], I32)
        id_row = m.sb("id_row", [N_IDS, N_IDS], I32)
        same = m.sb("same", [N_IDS, N_IDS])
        lower = m.sb("lower", [N_IDS, N_IDS])
        first = m.sb("first", [N_IDS, 2])
        tw = m.sb("tw", [P, KH, N_IDS])
        aw = m.sb("aw", [P, KH, INNER])
        ab = m.sb("ab", [INNER, 1])
        bw = m.sb("bw", [INNER + 1, H])
        hid = m.sb("hid", [INNER + 1, N_IDS])
        table = m.sb("table", [N_IDS, H])
        ident = m.sb("ident", [P, P])
        diff = m.sb("diff", [N_IDS, 2, P], I32)
        hit = m.sb("hit", [N_IDS, 2, P])
        row = m.sb("row", [P, TT, 1], U32)
        base = m.sb("base", [P, TT, H])
        h0 = m.sb("h0", [P, 2, H])
        stat = m.sb("stat", [P, 2, 12])
        mv = m.sb("mv", [P, 2, 2])
        std = m.sb("std", [P, 2, 1])
        rstd = m.sb("rstd", [P, 2, 1])
        eps = m.sb("eps", [P, 1])
        xln = m.sb("xln", [P, 2, H])
        xhl = m.sb("xhl", [P, 2, 2, H], F32R)
        p_tab = [m.ps(f"p_tab{i}", [P, H]) for i in range(2)]
        p_tr = [m.ps(f"p_tr{i}", [P, H]) for i in range(2)]

        consts = m.sem("consts")
        chain = m.sem("chain")
        hid_mm = m.sem("hid_mm")
        hid_ok = m.sem("hid_ok")
        table_mm = m.sem("table_mm")
        table_ok = m.sem("table_ok")
        row_ok = m.sem("row_ok")
        hit_ok = m.sem("hit_ok")
        gathered = m.sems("gathered", TT)
        tab_mm = m.sem("tab_mm")
        h0_ok = m.sem("h0_ok")
        stats_seen = m.sem("stats_seen")
        row_seen = m.sem("row_seen")
        stats_ok = m.sem("stats_ok")
        mv_ok = m.sem("mv_ok")
        std_ok = m.sem("std_ok")
        rstd_ok = m.sem("rstd_ok")
        xln_ok = m.sem("xln_ok")
        tr_mm = m.sem("tr_mm")
        hi_ok = m.sem("hi_ok")
        lo_ok = m.sem("lo_ok")
        diff_ok = m.sem("diff_ok")
        h0_st = m.sems("h0_st", 2)
        x_st = m.sems("x_st", 2)
        block = ctx.enter_context(nc.Block())
        N_CONST = 11

        @block.sync
        def _(sp):
            for dst, src in (
                (ids_row[:], io["tok_row"].partition_broadcast(N_IDS).rearrange("p a n -> p (a n)")),
                (id_row[:], io["ids_row"].partition_broadcast(N_IDS).rearrange("p a n -> p (a n)")),
                (tok_col[:], io["tok_col"]), (id_col[:], io["ids_col"]), (lower[:], io["lower"]),
                (tw[:], io["tw"]), (aw[:], io["aw"]), (ab[:], io["ab"]),
                (bw[0:INNER, :], io["bw"]), (bw[INNER:INNER + 1, :], io["bb"]), (ident[:], io["ident"]),
            ):
                sp.dma_start(dst, src).then_inc(consts, 16)
            for s in range(2):
                sp.sem_inc(h0_st[s], 16)
                sp.sem_inc(x_st[s], 16)
            def store_h0(b, v):
                sp.wait_ge(h0_ok, TT * b + v + 1)
                sp.dma_start(one(scr["h0"], TT * b + v), h0[:, v % 2]).then_inc(h0_st[v % 2], 16)

            def tile(b, t, more):
                if more(t + 2):
                    store_h0(b, t + 2)
                sp.wait_ge(lo_ok, TT * b + t + 1)
                sp.dma_start(one(scr["xln"], b).rearrange("p e k (t n) -> p e k t n", t=TT)[:, :, :, t]
                             .rearrange("p e k n -> p (e k) n"),
                             xhl[:, t % 2].bitcast(F32).rearrange("p e (k n) -> p (e k) n", k=KH)
                             ).then_inc(x_st[t % 2], 16)

            for v in range(2):
                store_h0(0, v)
            run_tiles(sp, tile)
            for s in range(2):
                sp.wait_ge(h0_st[s], 16 * (2 * BATCH + 1))
                sp.wait_ge(x_st[s], 16 * (2 * BATCH + 1))

        @block.gpsimd
        def _(pool):
            with pool.Fori(0, BATCH) as b:
                for t in range(TT):
                    pool.wait_ge(row_ok, TT * b + t + 1)
                    pool.sem_inc(row_seen, 1)
                    pool.indirect_dma_start(
                        base[:, t, :], None, io["orig_w"],
                        bass.IndirectOffsetOnAxis(ap=row[:, t, :], axis=0)).then_inc(gathered[t], 16)

        @block.tensor
        def _(pe):
            pe.wait_ge(consts, 16 * N_CONST)
            for k in range(KH):
                mm = pe.matmul(p_tab[0][0:INNER, 0:N_IDS], aw[:, k, :], tw[:, k, :],
                               start=(k == 0), stop=(k == KH - 1))
            mm.then_inc(hid_mm, 1)
            pe.wait_ge(hid_ok, 2)
            for c in range(2):
                mm = pe.matmul(p_tab[1][0:N_IDS, 512 * c:512 * c + 512], hid[:, :], bw[:, 512 * c:512 * c + 512],
                               start=True, stop=True)
            mm.then_inc(table_mm, 1)
            pe.wait_ge(table_ok, 1)

            def correct(b, v):
                pe.wait_ge(hit_ok, TT * b + v + 1)
                for c in range(2):
                    mm = pe.matmul(p_tab[v % 2][:, 512 * c:512 * c + 512], hit[:, v % 2, :],
                                   table[:, 512 * c:512 * c + 512], start=True, stop=True)
                mm.then_inc(tab_mm, 1)

            def turn(b, v):
                pe.wait_ge(xln_ok, TT * b + v + 1)
                for k in range(KH):
                    mm = pe.transpose(p_tr[v % 2][:, P * k:P * k + P], xln[:, v % 2, P * k:P * k + P], ident[:, :])
                mm.then_inc(tr_mm, 1)

            def tile(b, t, more):
                if more(t + 3):
                    correct(b, t + 3)
                if more(t + 1):
                    turn(b, t + 1)

            for v in range(3):
                correct(0, v)
            turn(0, 0)
            run_tiles(pe, tile)

        @block.scalar
        def _(act):
            act.wait_ge(hid_mm, 1)
            act.wait_ge(hid_ok, 1)
            nc.scalar.activation(hid[0:INNER, :], p_tab[0][0:INNER, 0:N_IDS], ACT.Identity,
                                 bias=ab[:, 0:1]).then_inc(hid_ok, 1)
            act.wait_ge(chain, 1)

            def deviation(b, v):
                act.wait_ge(mv_ok, TT * b + v + 1)
                nc.scalar.activation(std[:, v % 2], mv[:, v % 2, 1:2], ACT.Sqrt, bias=eps[:, 0:1]).then_inc(std_ok, 1)

            def tile(b, t, more):
                if more(t + 2):
                    deviation(b, t + 2)
                act.wait_ge(tr_mm, TT * b + t + 1)
                act.wait_ge(x_st[t % 2], 32 * b + 16 * (t // 2) + 16)
                nc.scalar.copy(xhl[:, t % 2, 0], p_tr[t % 2][:, :]).then_inc(hi_ok, 1)

            for v in range(2):
                deviation(0, v)
            run_tiles(act, tile)

        @block.vector
        def _(dve):
            dve.memset(eps[:], LN_EPS).then_inc(chain, 1)
            dve.memset(hid[:], 1.0).then_inc(hid_ok, 1)
            dve.wait_ge(consts, 16 * N_CONST)
            dve.tensor_scalar(wrap[:], tok_col[:], 0, float(VOCAB), ALU.is_lt, ALU.mult).then_inc(chain, 1)
            dve.wait_ge(chain, 2)
            dve.tensor_tensor(row_f[:], tok_col[:], wrap[:], ALU.add).then_inc(chain, 1)
            dve.wait_ge(chain, 3)
            dve.tensor_scalar(row_of[:], row_f[:], 0.0, float(VOCAB - 1), ALU.max, ALU.min).then_inc(chain, 1)
            dve.tensor_tensor(id_row[:], id_row[:], id_col[:, 0:1].to_broadcast([N_IDS, N_IDS]),
                              ALU.bitwise_xor).then_inc(chain, 1)
            dve.wait_ge(chain, 5)
            dve.tensor_scalar(same[:], id_row[:], 0, None, ALU.is_equal).then_inc(chain, 1)
            dve.wait_ge(chain, 6)
            dve.tensor_tensor(same[:], same[:], lower[:], ALU.mult).then_inc(chain, 1)
            dve.wait_ge(chain, 7)
            dve.tensor_reduce(first[:, 0:1], same[:], AX_X, ALU.max).then_inc(chain, 1)
            dve.wait_ge(chain, 8)
            dve.tensor_scalar(first[:, 1:2], first[:, 0:1], -1.0, 1.0, ALU.mult, ALU.add).then_inc(chain, 1)
            dve.wait_ge(chain, 9)
            dve.wait_ge(table_mm, 1)
            dve.tensor_scalar(table[:], p_tab[1][0:N_IDS, :], first[:, 1:2], None, ALU.mult).then_inc(table_ok, 1)

            def find_row(b, v):
                dve.tensor_copy(row[:, v % TT], row_of[:, bass.ds(TT * b + v, 1)]).then_inc(row_ok, 1)

            def mask(b, v):
                s, i = v % 2, TT * b + v
                dve.tensor_tensor(diff[:, s], ids_row[:, bass.ds(P * i, P)],
                                  id_col[:, 0:1].to_broadcast([N_IDS, P]), ALU.bitwise_xor).then_inc(diff_ok, 1)
                dve.wait_ge(diff_ok, i + 1)
                dve.tensor_scalar(hit[:, s], diff[:, s], 0, None, ALU.is_equal).then_inc(hit_ok, 1)

            def token(b, v, begin=False):
                s, i = v % 2, TT * b + v
                dve.wait_ge(gathered[v % TT], 16 * (b + v // TT) + 16)
                dve.wait_ge(tab_mm, i + 1)
                dve.wait_ge(h0_st[s], 32 * b + 16 * (v // 2) + 16)
                if not begin:
                    dve.wait_ge(xln_ok, i - 1)
                dve.tensor_tensor(h0[:, s], base[:, v % TT], p_tab[s][:, :], ALU.add).then_inc(h0_ok, 1)
                dve.wait_ge(h0_ok, i + 1)
                for c in range(2):
                    dve.bn_stats(stat[:, s, 6 * c:6 * c + 6], h0[:, s, 512 * c:512 * c + 512]).then_inc(stats_ok, 1)
                dve.wait_ge(stats_ok, 2 * i + 2)
                dve.sem_inc(stats_seen, 1)
                dve.bn_aggr(mv[:, s], stat[:, s]).then_inc(mv_ok, 1)

            def norm(b, v):
                s, i = v % 2, TT * b + v
                dve.wait_ge(std_ok, i + 1)
                dve.reciprocal(rstd[:, s], std[:, s]).then_inc(rstd_ok, 1)
                dve.wait_ge(rstd_ok, i + 1)
                dve.tensor_scalar(xln[:, s], h0[:, s], mv[:, s, 0:1], rstd[:, s, 0:1],
                                  ALU.subtract, ALU.mult).then_inc(xln_ok, 1)

            def tile(b, t, more):
                i = TT * b + t
                if more(t + 4):
                    find_row(b, t + 4)
                if more(t + 3):
                    mask(b, t + 3)
                if more(t + 2):
                    token(b, t + 2)
                if more(t + 1):
                    norm(b, t + 1)
                dve.wait_ge(hi_ok, i + 1)
                dve.tensor_tensor(xhl[:, t % 2, 1], p_tr[t % 2][:, :], xhl[:, t % 2, 0],
                                  ALU.subtract).then_inc(lo_ok, 1)

            for v in range(4):
                find_row(0, v)
            for v in range(3):
                mask(0, v)
                if v == 1:
                    token(0, 0, begin=True)
            token(0, 1, begin=True)
            norm(0, 0)
            run_tiles(dve, tile)


def mamba_phase(nc, io, scr):
    PAIRS = DT // 2
    HR, DR = 4, 4
    with ExitStack() as ctx:
        m = Mem(nc, ctx, "ssm")
        w = m.sb("w", [P, 2, 2, WU + XP], F32R)
        wdt = m.sb("wdt", [R, 2, 2, P], F32R)
        par = m.sb("par", [P, 2, PAR])
        xln = m.sb("xln", [P, 2, KH, L], F32R)
        b_all = m.sb("b_all", [P, N, L])
        c_all = m.sb("c_all", [P, N, L])
        db = m.sb("db", [P, DR, G, L])
        h = m.sb("h", [P, HR, G, L])
        u = m.sb("u", [P, 2, L])
        u_new = m.sb("u_new", [P, 2, L])
        g_new = m.sb("g_new", [P, L])
        u_pad = m.sb("u_pad", [P, TAPS - 1 + L])
        conv = m.sb("conv", [P, L])
        u_hl = m.sb("u_hl", [P, 2, L], F32R)
        delta = m.sb("delta", [P, 2, L])
        du = m.sb("du", [P, 2, L])
        soft = m.sb("soft", [P, L])
        y = m.sb("y", [P, 2, L])
        dt_hl = m.sb("dt_hl", [R, 2, L], F32R)
        xn = m.sb("xn", [XP, L])
        wf = [b_all[:].rearrange("p n l -> p (n l)")[:, WP * s:WP * (s + 1)] for s in range(2)]
        wdt_new = [c_all[:].rearrange("p n l -> p (n l)")[0:R, 2 * P * s:2 * P * (s + 1)].bitcast(F32R)
                   .rearrange("r (e n) -> r e n", e=2) for s in range(2)]
        sq, rs = conv[0:XP, :], soft[0:XP, :]
        rms_w = m.sb("rms_w", [XP, 1])
        rms_mean = m.sb("rms_mean", [XP, XP])
        rms_eps = m.sb("rms_eps", [XP, 1])
        ident = m.sb("ident", [P, P])
        zeros = m.sb("zeros", [P, P], F32R)
        da = m.ps("da", [P, 2, G, L])
        p_y = m.ps("p_y", [P, L])
        p_in = m.ps("p_in", [P, L])
        p_dt = m.ps("p_dt", [P, L])
        p_x = m.ps("p_x", [P, L])

        consts = m.sem("consts")
        zeroed = m.sem("zeroed")
        sp_passed = m.sem("sp_passed")
        w_ld = m.sems("w_ld", 2)
        par_ld = m.sems("par_ld", 2)
        wdt_ld = m.sems("wdt_ld", 2)
        wf_ld = m.sems("wf_ld", 2)
        whi_ok = m.sem("whi_ok")
        wlo_ok = m.sem("wlo_ok")
        w_st = m.sems("w_st", 2)
        w_used = m.sem("w_used")
        xln_ld = m.sems("xln_ld", 2)
        u_ld = m.sems("u_ld", 2)
        u_st = m.sems("u_st", 2)
        g_st = m.sem("g_st")
        y_st = m.sems("y_st", 2)
        bc_st = m.sem("bc_st")
        b_ld = m.sems("b_ld", NG)
        c_ld = m.sems("c_ld", NG)
        u_mm = m.sem("u_mm")
        g_mm = m.sem("g_mm")
        dt_mm = m.sem("dt_mm")
        x_mm = m.sem("x_mm")
        ms_mm = m.sem("ms_mm")
        h_used = m.sem("h_used")
        up_ok = m.sem("up_ok")
        gn_ok = m.sem("gn_ok")
        un_ok = m.sem("un_ok")
        hi_ok = m.sem("hi_ok")
        lo_ok = m.sem("lo_ok")
        tap_ok = m.sem("tap_ok")
        abs_ok = m.sem("abs_ok")
        exp_ok = m.sem("exp_ok")
        log_ok = m.sem("log_ok")
        max_ok = m.sem("max_ok")
        delta_ok = m.sem("delta_ok")
        du_ok = m.sem("du_ok")
        da_ok = m.sem("da_ok")
        db_ok = m.sem("db_ok")
        scan_ok = m.sem("scan_ok")
        hc_ok = m.sem("hc_ok")
        hc_last = m.sem("hc_last")
        y_ok = m.sem("y_ok")
        sq_ok = m.sem("sq_ok")
        rlog_ok = m.sem("rlog_ok")
        rs_ok = m.sem("rs_ok")
        xn_ok = m.sem("xn_ok")
        dth_ok = m.sem("dth_ok")
        dtl_ok = m.sem("dtl_ok")
        block = ctx.enter_context(nc.Block())

        def schedule(eng, step, between, start):
            with eng.Fori(0, PAIRS - 1) as i:
                for s in range(2):
                    step(s, None, i, 0, split=True)
            step(0, None, PAIRS - 1, 0, split=True)
            step(1, None, PAIRS - 1, 0)
            between(0)
            start(0, 0)

            def sequence(b, both):
                lead = PAIRS if both else None
                last = PAIRS * b + PAIRS - 1
                with eng.Fori(0, PAIRS - 1) as i:
                    for s in range(2):
                        step(s, PAIRS * b + i, PAIRS * b + i + lead if both else None, b, nxt=True)
                step(0, last, last + lead if both else None, b, nxt=True)
                if both:
                    step(1, None, last + lead, b + 1, early=True)
                step(1, last, None, b, nxt=both, close=both)

            with eng.Fori(0, BATCH - 1) as b:
                sequence(b, True)
            sequence(BATCH - 1, False)

        def after(s, ps):
            return (1, ps) if s == 0 else (0, ps + 1)

        @block.sync
        def _(sp):
            for dst, src in ((ident[:], io["ident"]), (rms_w[:], io["rms_w"]), (rms_mean[:], io["rms_mean"])):
                sp.dma_start(dst, src).then_inc(consts, 16)

            def load_w(s, dt):
                sp.dma_start(w[:, s].bitcast(F32), one(scr["w"], dt)[:, :, 0:WU + XP]).then_inc(w_ld[s], 16)

            def load_small(s, dt):
                sp.dma_start(par[:, s], one(io["par"], dt)).then_inc(par_ld[s], 16)
                sp.dma_start(wdt[:, s].bitcast(F32), one(scr["w"], dt)[0:R, :, WU + XP:WP]).then_inc(wdt_ld[s], 16)

            def load_wf(s, pair):
                sp.dma_start(wf[s], one(io["wpack"], 2 * pair + s)).then_inc(wf_ld[s], 16)

            def load_par(s, pair):
                sp.dma_start(par[:, s], one(io["par"], 2 * pair + s)).then_inc(par_ld[s], 16)

            def store_w(s, pair):
                sp.wait_ge(wlo_ok, 4 * pair + 2 * s + 2)
                sp.dma_start(one(scr["w"], 2 * pair + s)[:, :, 0:WU + XP], w[:, s].bitcast(F32)).then_inc(w_st[s], 16)
                sp.dma_start(one(scr["w"], 2 * pair + s)[0:R, :, WU + XP:WP],
                             wdt_new[s].bitcast(F32)).then_inc(w_st[s], 16)

            def load_xln(b, half):
                at = slice(KH // 2 * half, KH // 2 * (half + 1))
                sp.dma_start(xln[:, :, at, :].bitcast(F32), one(scr["xln"], b)[:, :, at, :]).then_inc(xln_ld[half], 16)

            def load_u(s, pair):
                sp.wait_ge(u_st[s], 16 * (pair + 2))
                sp.dma_start(u[:, s], one(scr["u"], 2 * pair + s)).then_inc(u_ld[s], 16)

            def step(s, ps, pi, next_w, next_small, next_ug):
                if ps is not None:
                    sp.wait_ge(y_ok, 2 * ps + s + 2)
                    sp.sem_inc(sp_passed, 1)
                    if next_small is not None:
                        load_small(s, next_small)
                    if next_ug:
                        load_u(s, ps + 1)
                    sp.dma_start(one(scr["y"], 2 * ps + s), y[:, s]).then_inc(y_st[s], 16)
                if pi is not None:
                    sp.wait_ge(un_ok, 2 * pi + s + 2)
                    sp.dma_start(one(scr["u"], 2 * pi + s), u_new[:, s]).then_inc(u_st[s], 16)
                    sp.wait_ge(gn_ok, 2 * pi + s + 2)
                    sp.dma_start(one(scr["g"], 2 * pi + s), g_new[:]).then_inc(g_st, 16)
                    if next_w is not None:
                        sp.wait_ge(w_used, 2 * pi + s + 3)
                        sp.sem_inc(sp_passed, 1)
                        load_w(s, next_w)

            def between(b, again=True, next_xln=None, meanwhile=None):
                if next_xln is not None:
                    sp.wait_ge(x_mm, b + 1)
                    load_xln(next_xln, 0)
                sp.wait_ge(xn_ok, b + 1)
                sp.dma_start(one(scr["bc"], b), xn[R:XP, :]).then_inc(bc_st, 16)
                sp.wait_ge(bc_st, 16 * (b + 2))
                for j in range(NG):
                    for all_, ld, first in ((b_all, b_ld, 0), (c_all, c_ld, N)):
                        if again:
                            if first == 0:
                                sp.wait_ge(db_ok, NG * (DT * b - 1) + j + 1)
                            elif j < NG - 1:
                                sp.wait_ge(hc_ok, (NG - 1) * (DT * b - 1) + j + 1)
                            else:
                                sp.wait_ge(hc_last, DT * b)
                            sp.sem_inc(sp_passed, 1)
                        src = one(scr["bc"], b)[first + G * j:first + G * j + G, :]
                        sp.dma_start(all_[:, G * j:G * j + G, :].rearrange("p n l -> p (n l)"),
                                     src.rearrange("(o n) l -> o (n l)", o=1).partition_broadcast(P)
                                     .rearrange("p o n -> p (o n)")).then_inc(ld[j], 16)
                    if j == 3 and next_xln is not None:
                        load_xln(next_xln, 1)
                    if j == 4 and meanwhile:
                        meanwhile()

            sp.wait_ge(zeroed, 1)
            for s in range(2):
                sp.sem_inc(u_st[s], 16)
                sp.sem_inc(y_st[s], 16)
            sp.sem_inc(g_st, 16)
            sp.sem_inc(bc_st, 16)
            for s in range(2):
                sp.sem_inc(w_st[s], 32)
                load_wf(s, 0)
                load_par(s, 0)
            for half in range(2):
                load_xln(0, half)
            store_w(0, 0)
            load_wf(0, 1)

            def alone(s, i, more):
                store_w(*after(s, i))
                if more:
                    load_wf(1 - s, i + 1 + s)
                step(s, None, i, None, None, False)
                load_par(s, i + 1)

            with sp.Fori(0, PAIRS - 2) as i:
                for s in range(2):
                    alone(s, i, True)
            alone(0, PAIRS - 2, True)
            alone(1, PAIRS - 2, False)
            store_w(1, PAIRS - 1)
            step(0, None, PAIRS - 1, None, None, False)
            for s in range(2):
                sp.wait_ge(w_st[s], 32 * (PAIRS + 1))
            load_small(0, 0)
            load_u(0, 0)
            step(1, None, PAIRS - 1, None, None, False)
            sp.wait_ge(x_mm, 1)
            load_small(1, 1)
            load_u(1, 0)
            between(0, again=False, next_xln=1)
            for s in range(2):
                load_w(s, s)

            def both(b, last):
                with sp.Fori(0, PAIRS - 1) as i:
                    for s in range(2):
                        step(s, PAIRS * b + i, PAIRS * b + i + PAIRS, 2 * i + 2 + s, 2 * i + 2 + s, True)
                pair = PAIRS * b + PAIRS - 1
                step(0, pair, pair + PAIRS, None if last else 0, 0, True)
                step(1, None, pair + PAIRS, None, None, False)
                between(b + 1, next_xln=None if last else b + 2,
                        meanwhile=lambda: step(1, pair, None, None, 1, True))
                if not last:
                    load_w(1, 1)

            with sp.Fori(0, BATCH - 2) as b:
                both(b, False)
            both(BATCH - 2, True)
            with sp.Fori(0, PAIRS - 1) as i:
                for s in range(2):
                    step(s, i + PAIRS * (BATCH - 1), None, None, 2 * i + 2 + s, True)
            for s in range(2):
                step(s, PAIRS * BATCH - 1, None, None, None, False)
            for s in range(2):
                sp.wait_ge(u_st[s], 16 * (PAIRS * BATCH + 1))
                sp.wait_ge(y_st[s], 16 * (PAIRS * BATCH + 1))
            sp.wait_ge(g_st, 16 * (DT * BATCH + 1))
            sp.wait_ge(bc_st, 16 * (BATCH + 1))

        @block.gpsimd
        def _(pool):
            def drive(q, s, groups, b):
                for j in groups:
                    pool.wait_ge(scan_ok, NG * q + j + 1)
                    if s == 0:
                        pool.wait_ge(b_ld[j], 16 * (b + 1))
                    pool.tensor_tensor(db[:, j % DR], du[:, s:s + 1, :].to_broadcast([P, G, L]),
                                       b_all[:, G * j:G * j + G, :], ALU.mult).then_inc(db_ok, 1)

            def times_last_c(q, s, b):
                j = NG - 1
                pool.wait_ge(scan_ok, NG * q + j + DR + 1)
                if s == 0:
                    pool.wait_ge(c_ld[j], 16 * (b + 1))
                pool.tensor_tensor(h[:, j % HR], h[:, j % HR], c_all[:, G * j:G * j + G, :],
                                   ALU.mult).then_inc(hc_last, 1)

            def make_du(s, ps):
                q = 2 * ps + s
                pool.wait_ge(delta_ok, q + 2)
                pool.wait_ge(u_ld[s], 16 * (ps + 1))
                pool.tensor_tensor(du[:, s], delta[:, s], u[:, s], ALU.mult).then_inc(du_ok, 1)

            def low_u(s, pi):
                pool.wait_ge(hi_ok, 2 * pi + s + 1)
                pool.tensor_tensor(u_hl[:, 1], u_new[:, s], u_hl[:, 0], ALU.subtract).then_inc(lo_ok, 1)

            def step(s, ps, pi, b, nxt=False, close=False, early=False, split=False):
                if ps is None:
                    low_u(s, pi)
                    return
                q = 2 * ps + s
                after_b = b + 1 if close else b
                drive(q, s, range(4, NG), b)
                if nxt:
                    make_du(*after(s, ps))
                    pool.wait_ge(du_ok, q + 2)
                    drive(q + 1, 1 - s, (0, 1), after_b)
                if not close:
                    times_last_c(q, s, b)
                if nxt:
                    drive(q + 1, 1 - s, (2,), after_b)
                if pi is not None:
                    low_u(s, pi)
                if nxt:
                    drive(q + 1, 1 - s, (3,), after_b)

            def start(ps, b):
                make_du(0, ps)
                pool.wait_ge(du_ok, 2 * ps + 1)
                drive(2 * ps, 0, range(4), b)

            schedule(pool, step, lambda b: None, start)

        @block.tensor
        def _(pe):
            def in_mm(s, part, ks, ok, bank=p_in, x_b=None):
                for k in ks:
                    if x_b is not None and k == KH // 2:
                        pe.wait_ge(xln_ld[1], 16 * (x_b + 1))
                    at = (2 * k + part) * P
                    for n_, (a, c) in enumerate(((0, 0), (1, 0), (0, 1))):
                        mm = pe.matmul(bank[:], w[:, s, a, at:at + P], xln[:, c, k, :],
                                       start=(k == 0 and n_ == 0), stop=(k == KH - 1 and n_ == 2))
                if KH - 1 in ks:
                    mm.then_inc(ok, 1)

            def add_group(q, j):
                if j < NG - 1:
                    pe.wait_ge(hc_ok, (NG - 1) * q + j + 1)
                else:
                    pe.wait_ge(hc_last, q + 1)
                if j == 0:
                    pe.wait_ge(y_ok, q + 1)
                for n_ in range(G):
                    mm = pe.matmul(p_y[:], ident[:], h[:, j % HR, n_, :], start=(j == 0 and n_ == 0),
                                   stop=(j == NG - 1 and n_ == G - 1))
                mm.then_inc(h_used, 1)

            def dt_product(s, ps, b):
                pe.wait_ge(par_ld[s], 16 * (ps + PAIRS + 1))
                pe.wait_ge(wdt_ld[s], 16 * (ps + 1))
                pe.wait_ge(dtl_ok, b + 1)
                pe.wait_ge(delta_ok, 2 * ps + s + 1)
                for n_, (a, c) in enumerate(((0, 0), (1, 0), (0, 1))):
                    mm = pe.matmul(p_dt[:], wdt[:, s, a, :], dt_hl[:, c, :], start=(n_ == 0), stop=(n_ == 2))
                mm.then_inc(dt_mm, 1)

            def x_product(s, pi):
                pe.wait_ge(lo_ok, 2 * pi + s + 1)
                for a, c in ((0, 0), (1, 0), (0, 1)):
                    mm = pe.matmul(p_x[0:XP, :], w[:, s, a, WU:WU + XP], u_hl[:, c, :],
                                   start=False, stop=False, skip_group_check=True)
                mm.then_inc(w_used, 1)

            U_AT = {0: (0, 1, 2), 1: (3, 4, 5), 2: (6, 7)}
            G_AT = {3: (0, 1), 4: (2, 3), 5: (4, 5), 6: (6,), 7: (7,)}

            def clear_x(first):
                for c in range(L // P):
                    mm = pe.matmul(p_x[0:XP, P * c:P * c + P], zeros[:, 0:XP], zeros[:], start=first and c == 0,
                                   stop=not first, skip_group_check=True)
                return mm

            def mean_square(b):
                pe.wait_ge(sq_ok, b + 1)
                pe.wait_ge(gn_ok, DT * b + DT + 1)
                pe.wait_ge(delta_ok, DT * b + 1)
                pe.matmul(p_dt[0:XP, :], rms_mean[:], sq, start=True, stop=True).then_inc(ms_mm, 1)

            def step(s, ps, pi, b, nxt=False, close=False, early=False, split=False):
                def inputs_ready(x_b):
                    pe.wait_ge(w_ld[s], 16 * (pi - PAIRS + 1))
                    pe.wait_ge(xln_ld[0], 16 * (x_b + 1))
                    pe.wait_ge(gn_ok, 2 * pi + s + 1)

                if ps is None:
                    t = 2 * pi + s
                    if early:
                        inputs_ready(b)
                    else:
                        pe.wait_ge(wlo_ok, 2 * t + 2)
                        pe.wait_ge(xln_ld[0], 16)
                    pe.wait_ge(up_ok, t + 1)
                    in_mm(s, 0, range(KH), u_mm, x_b=b)
                    pe.wait_ge(gn_ok, t + 1)
                    if early:
                        pe.wait_ge(delta_ok, DT * b)
                    in_mm(s, 1, range(KH), g_mm, p_dt)
                    if not early:
                        x_product(s, pi)
                    return
                q = 2 * ps + s
                for j in range(NG):
                    add_group(q, j)
                    if j == 1 and nxt and not close:
                        dt_product(*after(s, ps), b)
                    if close and j == 1:
                        x_product(1, ps + PAIRS)
                        clear_x(False).then_inc(x_mm, 1)
                    if close and j == 2:
                        mean_square(b + 1)
                    if close and j == 3:
                        dt_product(*after(s, ps), b + 1)
                        clear_x(True)
                    if pi is not None:
                        if j == 0:
                            t = 2 * pi + s
                            inputs_ready(b + 1)
                        if j in U_AT:
                            in_mm(s, 0, U_AT[j], u_mm, x_b=b + 1)
                        if j in G_AT:
                            if 0 in G_AT[j]:
                                pe.wait_ge(up_ok, t + 2)
                            in_mm(s, 1, G_AT[j], g_mm)
                if pi is not None:
                    x_product(s, pi)

            def between(b):
                clear_x(False).then_inc(x_mm, 1)
                mean_square(b)
                pe.wait_ge(xn_ok, b + 1)
                clear_x(True)

            pe.wait_ge(consts, 48)
            pe.wait_ge(zeroed, 1)
            pe.sem_inc(w_used, 2)
            pe.sem_inc(dt_mm, 1)
            pe.sem_inc(h_used, HR)
            clear_x(True)
            schedule(pe, step, between, lambda ps, b: dt_product(0, ps, b))

        @block.scalar
        def _(act):
            def exps(q, s, groups):
                for j in groups:
                    act.wait_ge(scan_ok, NG * q + j + DR - 1)
                    for n_ in range(G):
                        a = nc.scalar.activation(da[:, j % 2, n_, 1:L], delta[:, s, 1:L], ACT.Exp,
                                                 scale=par[:, s, G * j + n_:G * j + n_ + 1])
                    a.then_inc(da_ok, 1)

            def soft_part(s, ps, first=False):
                q = 2 * ps + s
                act.wait_ge(dt_mm, q + 2)
                act.wait_ge(delta_ok, q + 1)
                nc.scalar.activation(soft[:], p_dt[:], ACT.Abs, bias=par[:, s, DT_B:DT_B + 1]).then_inc(abs_ok, 1)
                if not first:
                    act.wait_ge(da_ok, NG * (q - 1) + 1)
                    act.wait_ge(du_ok, q)
                nc.scalar.activation(delta[:, s], p_dt[:], ACT.Relu, bias=par[:, s, DT_B:DT_B + 1]).then_inc(max_ok, 1)
                act.wait_ge(abs_ok, q + 1)
                nc.scalar.activation(soft[:], soft[:], ACT.Exp, scale=-1.0).then_inc(exp_ok, 1)
                act.wait_ge(exp_ok, q + 1)
                nc.scalar.activation(soft[:], soft[:], ACT.Ln, bias=1.0).then_inc(log_ok, 1)

            def pad_u(s, pi):
                t = 2 * pi + s
                act.wait_ge(u_mm, t + 1)
                act.wait_ge(tap_ok, TAPS * (t + 1))
                nc.scalar.copy(u_pad[:, TAPS - 1:], p_in[:]).then_inc(up_ok, 1)
                act.wait_ge(up_ok, t + 2)
                act.wait_ge(un_ok, t + 1)
                nc.scalar.activation(conv[:], u_pad[:, TAPS - 1:], ACT.Identity,
                                     scale=par[:, s, CONV_W + 3:CONV_W + 4],
                                     bias=par[:, s, CONV_B:CONV_B + 1]).then_inc(tap_ok, 1)

            def keep_gate(s, pi, bank=p_in):
                t = 2 * pi + s
                act.wait_ge(g_mm, t + 1)
                act.wait_ge(g_st, 16 * (t + 1))
                nc.scalar.copy(g_new[:], bank[:]).then_inc(gn_ok, 1)

            def high_w(s, pair):
                act.wait_ge(wf_ld[s], 16 * (pair + 1))
                act.wait_ge(w_used, 2 * pair + s + 1)
                act.wait_ge(w_st[s], 32 * (pair + 1))
                nc.scalar.copy(w[:, s, 0], wf[s][:, 0:WU + XP]).then_inc(whi_ok, 1)
                nc.scalar.copy(wdt_new[s][:, 0], wf[s][0:R, WU + XP:WP]).then_inc(whi_ok, 1)

            def silu_u(s, pi):
                t = 2 * pi + s
                act.wait_ge(tap_ok, TAPS * (t + 2))
                act.wait_ge(u_st[s], 16 * (pi + 1))
                nc.scalar.activation(u_new[:, s], conv[:], ACT.Silu).then_inc(un_ok, 1)
                act.wait_ge(un_ok, t + 2)
                act.wait_ge(w_used, t + 2)
                nc.scalar.copy(u_hl[:, 0], u_new[:, s]).then_inc(hi_ok, 1)

            def square(b):
                act.wait_ge(x_mm, b + 1)
                nc.scalar.activation(sq, p_x[0:XP, :], ACT.Square).then_inc(sq_ok, 1)

            def inverse_root(b):
                act.wait_ge(ms_mm, b + 1)
                nc.scalar.activation(rs, p_dt[0:XP, :], ACT.Ln, bias=rms_eps[:, 0:1]).then_inc(rlog_ok, 1)
                act.wait_ge(rlog_ok, b + 1)
                nc.scalar.activation(rs, rs, ACT.Exp, scale=-0.5).then_inc(rs_ok, 1)

            def high_dt(b):
                act.wait_ge(xn_ok, b + 1)
                act.wait_ge(dt_mm, DT * b + 1)
                nc.scalar.copy(dt_hl[:, 0], xn[0:R, :]).then_inc(dth_ok, 1)

            def step(s, ps, pi, b, nxt=False, close=False, early=False, split=False):
                if ps is None:
                    if split:
                        high_w(*after(s, pi))
                    if not early:
                        act.wait_ge(par_ld[s], 16 * (pi + 1))
                    pad_u(s, pi)
                    silu_u(s, pi)
                    if early:
                        nc.scalar.preload_act_table_set(LOG_EXP)
                    keep_gate(s, pi, p_dt)
                    return
                q = 2 * ps + s
                if close:
                    exps(q, s, (3, 4))
                    square(b + 1)
                    exps(q, s, (5,))
                    inverse_root(b + 1)
                    high_dt(b + 1)
                    exps(q, s, (6, 7))
                    soft_part(*after(s, ps))
                else:
                    exps(q, s, (3, 4, 5))
                    if nxt:
                        soft_part(*after(s, ps))
                    exps(q, s, (6,))
                    if pi is not None:
                        pad_u(s, pi)
                    exps(q, s, (7,))
                if nxt:
                    act.wait_ge(delta_ok, q + 3)
                    exps(q + 1, 1 - s, (0, 1))
                if pi is not None:
                    silu_u(s, pi)
                    nc.scalar.preload_act_table_set(LOG_EXP)
                if nxt:
                    exps(q + 1, 1 - s, (2,))
                if pi is not None:
                    keep_gate(s, pi)

            def between(b):
                nc.scalar.preload_act_table_set(LOG_EXP)
                square(b)
                inverse_root(b)
                high_dt(b)

            def start(ps, b):
                soft_part(0, ps, first=True)
                act.wait_ge(delta_ok, 2 * ps + 2)
                exps(2 * ps, 0, (0, 1, 2))

            act.sem_inc(gn_ok, 1)
            act.sem_inc(up_ok, 1)
            act.sem_inc(un_ok, 1)
            act.wait_ge(zeroed, 1)
            high_w(0, 0)
            schedule(act, step, between, start)

        @block.vector
        def _(dve):
            dve.memset(u_pad[:, 0:TAPS - 1], 0.0)
            dve.memset(rms_eps[:], RMS_EPS)
            dve.memset(da[:, :, :, 0:1], 0.0)
            dve.memset(zeros[:].bitcast(F32), 0.0).then_inc(zeroed, 1)
            dve.sem_inc(delta_ok, 1)
            dve.sem_inc(y_ok, 1)
            dve.sem_inc(scan_ok, DR)
            dve.sem_inc(tap_ok, TAPS)
            dve.wait_ge(consts, 48)
            dve.wait_ge(zeroed, 1)

            def tap(s, pi, k):
                t = 2 * pi + s
                if k == 1:
                    dve.wait_ge(up_ok, t + 2)
                dve.wait_ge(tap_ok, TAPS * (t + 1) + k)
                c = TAPS - 1 - k
                dve.scalar_tensor_tensor(out=conv[:], in0=u_pad[:, c:c + L],
                                         scalar=par[:, s, CONV_W + c:CONV_W + c + 1], in1=conv[:],
                                         op0=ALU.mult, op1=ALU.add).then_inc(tap_ok, 1)

            def scan(q, j):
                dve.wait_ge(da_ok, NG * q + j + 1)
                dve.wait_ge(db_ok, NG * q + j + 1)
                dve.wait_ge(h_used, NG * q + j + 1)
                dve.tensor_tensor_scan(h[:, j % HR].rearrange("p n l -> p (n l)"),
                                       da[:, j % 2].rearrange("p n l -> p (n l)"),
                                       db[:, j % DR].rearrange("p n l -> p (n l)"),
                                       0.0, ALU.mult, ALU.add).then_inc(scan_ok, 1)

            def times_c(q, s, j, b):
                dve.wait_ge(scan_ok, NG * q + j + DR + 1)
                if s == 0:
                    dve.wait_ge(c_ld[j], 16 * (b + 1))
                dve.tensor_tensor(h[:, j % HR], h[:, j % HR], c_all[:, G * j:G * j + G, :],
                                  ALU.mult).then_inc(hc_ok if j < NG - 1 else hc_last, 1)

            def delta_add(s, ps):
                q = 2 * ps + s
                dve.wait_ge(max_ok, q + 1)
                dve.wait_ge(log_ok, q + 1)
                dve.tensor_tensor(delta[:, s], delta[:, s], soft[:], ALU.add).then_inc(delta_ok, 1)

            def norm_x(b):
                dve.wait_ge(rs_ok, b + 1)
                dve.wait_ge(bc_st, 16 * (b + 1))
                dve.scalar_tensor_tensor(out=xn[:], in0=p_x[0:XP, :], scalar=rms_w[:, 0:1], in1=rs,
                                         op0=ALU.mult, op1=ALU.mult).then_inc(xn_ok, 1)

            def low_dt(b):
                dve.wait_ge(xn_ok, b + 1)
                dve.wait_ge(dth_ok, b + 1)
                dve.tensor_tensor(dt_hl[:, 1], xn[0:R, :], dt_hl[:, 0], ALU.subtract).then_inc(dtl_ok, 1)

            def low_w(s, pair):
                dve.wait_ge(whi_ok, 4 * pair + 2 * s + 2)
                dve.tensor_tensor(w[:, s, 1], wf[s][:, 0:WU + XP], w[:, s, 0], ALU.subtract).then_inc(wlo_ok, 1)
                dve.tensor_tensor(wdt_new[s][:, 1], wf[s][0:R, WU + XP:WP], wdt_new[s][:, 0],
                                  ALU.subtract).then_inc(wlo_ok, 1)

            TAP_AT = {6: (1,), 7: (2, 3)}

            def step(s, ps, pi, b, nxt=False, close=False, early=False, split=False):
                if ps is None:
                    if split:
                        low_w(*after(s, pi))
                    if not early:
                        dve.wait_ge(par_ld[s], 16 * (pi + 1))
                    for k in range(1, TAPS):
                        tap(s, pi, k)
                    return
                q = 2 * ps + s
                for j in range(NG):
                    if 0 < j < NG - 1 or close and j > 0:
                        times_c(q, s, j, b)
                    if j + 2 < NG:
                        scan(q, j + 2)
                    if close and j == 3:
                        norm_x(b + 1)
                    if close and j == 3:
                        low_dt(b + 1)
                    if nxt and j == (7 if close else 3):
                        delta_add(*after(s, ps))
                    if pi is not None:
                        for k in TAP_AT.get(j, ()):
                            tap(s, pi, k)
                if nxt:
                    begin(q + 1, 1 - s, b + 1 if close else b)
                dve.wait_ge(h_used, NG * q + NG + HR)
                dve.wait_ge(y_st[s], 16 * (ps + 1))
                dve.scalar_tensor_tensor(out=y[:, s], in0=u[:, s], scalar=par[:, s, D_SKIP:D_SKIP + 1], in1=p_y[:],
                                         op0=ALU.mult, op1=ALU.add).then_inc(y_ok, 1)

            def begin(q, s, b):
                scan(q, 0)
                scan(q, 1)
                times_c(q, s, 0, b)

            def between(b):
                norm_x(b)
                low_dt(b)

            def start(ps, b):
                delta_add(0, ps)
                begin(2 * ps, 0, b)

            low_w(0, 0)
            schedule(dve, step, between, start)


def out_phase(nc, io, scr, stats):
    HC = H // 512
    with ExitStack() as ctx:
        m = Mem(nc, ctx, "out")
        wo_hl = m.sb("wo_hl", [P, 2, DT, H], F32R)
        wo = m.sb("wo", [P, 2, H])
        y = m.sb("y", [P, 2, DT, P])
        g = m.sb("g", [P, DT, P])
        y_hl = m.sb("y_hl", [P, 2, DT, P], F32R)
        y_hl2 = m.sb("y_hl2", [P, 2, DT, P], F32R)
        h0 = m.sb("h0", [P, H])
        h1 = m.sb("h1", [P, H])
        ys = (y_hl, y_hl2)
        p_o = [m.ps(f"p_o{i}", [P, H]) for i in range(2)]
        bstat = m.sb("bstat", [P, 12])
        mv = m.sb("mv", [P, 2])

        wo_ld = m.sems("wo_ld", 2)
        whi_ok = m.sem("whi_ok")
        wlo_ok = m.sem("wlo_ok")
        y_ld = m.sems("y_ld", 2)
        g_ld = m.sem("g_ld")
        silu_ok = m.sem("silu_ok")
        yg_ok = m.sem("yg_ok")
        h0_ld = m.sem("h0_ld")
        hi_ok = m.sem("hi_ok")
        lo_ok = m.sem("lo_ok")
        o_mm = m.sem("o_mm")
        h1_ok = m.sem("h1_ok")
        h1_st = m.sem("h1_st")
        bn_ok = m.sem("bn_ok")
        bn_seen = m.sem("bn_seen")
        mv_ok = m.sem("mv_ok")
        st_ok = m.sem("st_ok")
        block = ctx.enter_context(nc.Block())

        def tile_of(ap, b, t):
            return (ap.rearrange("(b k) p l -> b p k l", b=BATCH)[bass.ds(b, 1), :, :, P * t:P * t + P]
                    .rearrange("o p k l -> p (o k) l"))

        @block.sync
        def _(sp):
            sp.sem_inc(h1_st, 16)

            def load(b, v):
                i = TT * b + v
                sp.wait_ge(yg_ok, i + 1)
                sp.dma_start(g[:], tile_of(scr["g"], b + v // TT, v % TT)).then_inc(g_ld, 16)
                sp.wait_ge(lo_ok, i + 1)
                sp.dma_start(y[:, v % 2], tile_of(scr["y"], b + v // TT, v % TT)).then_inc(y_ld[v % 2], 16)

            def tile(b, t, more):
                if more(t + 1):
                    load(b, t + 1)
                sp.wait_ge(h1_ok, TT * b + t + 2)
                sp.dma_start(h0[:], one(scr["h0"], TT * b + t)).then_inc(h0_ld, 16)

            load(0, 0)
            for k in range(DT):
                if k >= 2:
                    sp.wait_ge(wlo_ok, k - 1)
                sp.dma_start(wo[:, k % 2], io["wo"][:, k, :]).then_inc(wo_ld[k % 2], 16)
            run_tiles(sp, tile)
            sp.wait_ge(h1_st, 16 * (BATCH * TT + 1))

        @block.tensor
        def _(pe):
            pe.sem_inc(o_mm, 2)
            with pe.Fori(0, BATCH) as b:
                for t in range(TT):
                    i = TT * b + t
                    s = t % 2
                    pe.wait_ge(lo_ok, i + 3)
                    pe.wait_ge(h1_ok, i + 1)
                    for k in range(DT):
                        if t == 0:
                            pe.wait_ge(wlo_ok, k + 1)
                        for c in range(HC):
                            for n_, (a, e) in enumerate(((0, 0), (1, 0), (0, 1))):
                                mm = pe.matmul(p_o[s][:, 512 * c:512 * c + 512], ys[s][:, a, k, :],
                                               wo_hl[:, e, k, 512 * c:512 * c + 512],
                                               start=(k == 0 and n_ == 0), stop=(k == DT - 1 and n_ == 2))
                    mm.then_inc(o_mm, 1)

        @block.scalar
        def _(act):
            def high(i, b, t):
                s = t % 2
                act.wait_ge(g_ld, 16 * i + 16)
                nc.scalar.activation(g[:], g[:], ACT.Silu).then_inc(silu_ok, 1)
                act.wait_ge(yg_ok, i + 2)
                act.wait_ge(o_mm, i + 1)
                nc.scalar.copy(ys[s][:, 0], y[:, s]).then_inc(hi_ok, 1)

            def tiles(b, last=False):
                for t in range(TT):
                    i = TT * b + t
                    if t < TT - 1:
                        high(i + 1, b, t + 1)
                    elif not last:
                        high(i + 1, b + 1, 0)
                    act.wait_ge(h1_ok, i + 3)
                    act.dma_start(one(scr["h1"], i), h1[:]).then_inc(h1_st, 16)

            high(0, 0, 0)
            for k in range(DT):
                act.wait_ge(wo_ld[k % 2], 16 * (k // 2 + 1))
                nc.scalar.copy(wo_hl[:, 0, k, :], wo[:, k % 2]).then_inc(whi_ok, 1)
            with act.Fori(0, BATCH - 1) as b:
                tiles(b)
            tiles(BATCH - 1, last=True)

        @block.vector
        def _(dve):
            dve.sem_inc(lo_ok, 2)
            dve.sem_inc(yg_ok, 1)
            dve.sem_inc(h1_ok, 2)
            def low(i, b, t):
                s = t % 2
                dve.wait_ge(y_ld[s], 32 * b + 16 * (t // 2) + 16)
                dve.wait_ge(silu_ok, i + 1)
                dve.tensor_tensor(y[:, s], y[:, s], g[:], ALU.mult).then_inc(yg_ok, 1)
                dve.wait_ge(hi_ok, i + 1)
                dve.tensor_tensor(ys[s][:, 1], y[:, s], ys[s][:, 0], ALU.subtract).then_inc(lo_ok, 1)

            def tiles(b, last=False):
                for t in range(TT):
                    i = TT * b + t
                    s = t % 2
                    if t < TT - 1:
                        low(i + 1, b, t + 1)
                    elif not last:
                        low(i + 1, b + 1, 0)
                    dve.wait_ge(o_mm, i + 3)
                    dve.wait_ge(h0_ld, 16 * i + 16)
                    dve.wait_ge(h1_st, 16 * i + 16)
                    dve.tensor_tensor(h1[:], h0[:], p_o[s][:, :], ALU.add).then_inc(h1_ok, 1)
                    dve.wait_ge(h1_ok, i + 3)
                    for c in range(HC):
                        dve.bn_stats(bstat[:, 6 * c:6 * c + 6], h1[:, 512 * c:512 * c + 512]).then_inc(bn_ok, 1)
                    dve.wait_ge(bn_ok, 2 * i + 2)
                    dve.sem_inc(bn_seen, 1)
                    dve.bn_aggr(mv[:], bstat[:]).then_inc(mv_ok, 1)
                    dve.wait_ge(mv_ok, i + 1)
                    dve.tensor_scalar(stats[:, bass.ds(2 * i, 2)], mv[:], 1.0, None, ALU.mult).then_inc(st_ok, 1)

            low(0, 0, 0)
            for k in range(DT):
                dve.wait_ge(whi_ok, k + 1)
                dve.tensor_tensor(wo_hl[:, 1, k, :], wo[:, k % 2], wo_hl[:, 0, k, :], ALU.subtract).then_inc(wlo_ok, 1)
            with dve.Fori(0, BATCH - 1) as b:
                tiles(b)
            tiles(BATCH - 1, last=True)
            dve.wait_ge(st_ok, BATCH * TT)


def ffn_phase(nc, io, scr, stats, out):
    HC = H // 512
    with ExitStack() as ctx:
        m = Mem(nc, ctx, "ffn")
        wz_hl = m.sb("wz_hl", [P, 2, KH, BN], F32R)
        wb_hl = m.sb("wb_hl", [P, 2, KB, H], F32R)
        w_f = m.sb("w_f", [P, 2, KH * BN])
        wr = m.sb("wr", [P, KH, ROUTER])
        keys = m.sb("keys", [ROUTER, EXPERTS])
        ident = m.sb("ident", [P, P])
        rstd = m.sb("rstd", [P, BATCH * TT])
        std = m.sb("std", [P, BATCH * TT])
        eps = m.sb("eps", [P, 1])
        h1 = m.sb("h1", [P, TT, H])
        xln = m.sb("xln", [P, 2, H])
        x_f = m.sb("x_f", [P, KH, P])
        x_hl = m.sb("x_hl", [P, 2, KH, P], F32R)
        qt = m.sb("qt", [ROUTER, P])
        score = m.sb("score", [P, EXPERTS])
        rest = m.sb("rest", [P, 2, EXPERTS])
        top = m.sb("top", [P, 2, 8])
        neg_max = m.sb("neg_max", [P, 1])
        ex = m.sb("ex", [P, EXPERTS])
        chosen = m.sb("chosen", [P, EXPERTS])
        total = m.sb("total", [P, 1])
        inv = m.sb("inv", [P, 1])
        gate = m.sb("gate", [P, EXPERTS, 1])
        zg = m.sb("zg", [P, BN])
        z_hl = m.sb("z_hl", [P, 2, KB, P], F32R)
        res = m.sb("res", [P, 2, H])
        p_xt = m.ps("p_xt", [P, H])
        p_z = m.ps("p_z", [P, BN])
        p_q = m.ps("p_q", [P, 512])
        p_s = m.ps("p_s", [P, 512])
        p_zt = m.ps("p_zt", [P, KB * P])
        p_o = m.ps("p_o", [P, H])

        consts = m.sem("consts")
        w_ldz = m.sem("w_ldz")
        w_ldb = m.sem("w_ldb")
        whi_ok = m.sem("whi_ok")
        wlo_ok = m.sem("wlo_ok")
        eps_ok = m.sem("eps_ok")
        std_ok = m.sem("std_ok")
        rstd_ok = m.sem("rstd_ok")
        h1_ld = m.sems("h1_ld", TT)
        xln_ok = m.sem("xln_ok")
        xt_mm = m.sem("xt_mm")
        xf_ok = m.sem("xf_ok")
        hi_ok = m.sem("hi_ok")
        lo_ok = m.sem("lo_ok")
        q_mm = m.sem("q_mm")
        q_ok = m.sem("q_ok")
        s_mm = m.sem("s_mm")
        z_mm = m.sem("z_mm")
        score_ok = m.sem("score_ok")
        pick = m.sem("pick")
        PICKS = 8
        pick_seen = m.sem("pick_seen")
        inv_ok = m.sem("inv_ok")
        gate_ok = m.sem("gate_ok")
        ex_ok = m.sem("ex_ok")
        zg_ok = m.sem("zg_ok")
        zt_mm = m.sem("zt_mm")
        zhi_ok = m.sem("zhi_ok")
        zlo_ok = m.sem("zlo_ok")
        o_mm = m.sem("o_mm")
        res_ok = m.sem("res_ok")
        out_st = m.sems("out_st", 2)
        block = ctx.enter_context(nc.Block())

        @block.sync
        def _(sp):
            for dst, src in ((wr[:], io["wr"]), (keys[:], io["keys"]), (ident[:], io["ident"])):
                sp.dma_start(dst, src).then_inc(consts, 16)
            for s in range(2):
                sp.sem_inc(out_st[s], 16)

            def load(b, v):
                sp.wait_ge(res_ok, TT * b + v + 1)
                sp.dma_start(h1[:, v % TT], one(scr["h1"], TT * b + v)).then_inc(h1_ld[v % TT], 16)

            def tile(b, t, more):
                i = TT * b + t
                sp.wait_ge(res_ok, i + TT + 1)
                sp.dma_start(one(out, i), res[:, t % 2]).then_inc(out_st[t % 2], 16)
                if more(t + TT):
                    load(b, t + TT)

            load(0, 0)
            sp.dma_start(w_f[:, 0].rearrange("p (k n) -> p k n", k=KH), io["wz"]).then_inc(w_ldz, 16)
            sp.dma_start(w_f[:, 1].rearrange("p (k n) -> p k n", k=KB), io["wb"]).then_inc(w_ldb, 16)
            for v in range(1, TT):
                load(0, v)
            run_tiles(sp, tile)
            for s in range(2):
                sp.wait_ge(out_st[s], 16 * (2 * BATCH + 1))

        @block.tensor
        def _(pe):
            pe.sem_inc(o_mm, 1)
            pe.wait_ge(consts, 48)

            def turn(b, v):
                pe.wait_ge(xln_ok, TT * b + v + 1)
                for k in range(KH):
                    mm = pe.transpose(p_xt[:, P * k:P * k + P], xln[:, v % 2, P * k:P * k + P], ident[:, :])
                mm.then_inc(xt_mm, 1)

            def route(i):
                pe.wait_ge(xf_ok, i + 1)
                for k in range(KH):
                    mm = pe.matmul(p_q[0:ROUTER, 0:P], wr[:, k, :], x_f[:, k, :], start=(k == 0), stop=(k == KH - 1))
                mm.then_inc(q_mm, 1)
                pe.wait_ge(lo_ok, i + 1)
                for k in range(KH):
                    if k == 3:
                        pe.wait_ge(q_ok, i + 1)
                        pe.matmul(p_s[:, 0:EXPERTS], qt[:, :], keys[:, :], start=True, stop=True).then_inc(s_mm, 1)
                    for n_, (a, e) in enumerate(((0, 0), (1, 0), (0, 1))):
                        mm = pe.matmul(p_z[:], x_hl[:, a, k, :], wz_hl[:, e, k, :],
                                       start=(k == 0 and n_ == 0), stop=(k == KH - 1 and n_ == 2))
                mm.then_inc(z_mm, 1)

            def turn_z(i):
                pe.wait_ge(zg_ok, i + 1)
                for k in range(KB):
                    mm = pe.transpose(p_zt[:, P * k:P * k + P], zg[:, P * k:P * k + P], ident[:, :])
                mm.then_inc(zt_mm, 1)

            def combine(i):
                pe.wait_ge(zlo_ok, i + 1)
                pe.wait_ge(res_ok, i + TT)
                for k in range(KB):
                    for c in range(HC):
                        for n_, (a, e) in enumerate(((0, 0), (1, 0), (0, 1))):
                            mm = pe.matmul(p_o[:, 512 * c:512 * c + 512], z_hl[:, a, k, :],
                                           wb_hl[:, e, k, 512 * c:512 * c + 512],
                                           start=(k == 0 and n_ == 0), stop=(k == KB - 1 and n_ == 2))
                mm.then_inc(o_mm, 1)

            def tile(b, t, more):
                i = TT * b + t
                turn_z(i)
                if more(t + 1):
                    route(i + 1)
                if more(t + 2):
                    turn(b, t + 2)
                combine(i)

            turn(0, 0)
            pe.wait_ge(wlo_ok, 1)
            route(0)
            turn(0, 1)
            pe.wait_ge(wlo_ok, 2)
            run_tiles(pe, tile)

        @block.scalar
        def _(act):
            act.wait_ge(eps_ok, 1)
            nc.scalar.activation(std[:], stats[:].rearrange("p (i e) -> p i e", e=2)[:, :, 1], ACT.Sqrt,
                                 bias=eps[:, 0:1]).then_inc(std_ok, 1)
            act.wait_ge(w_ldz, 16)
            nc.scalar.copy(wz_hl[:, 0].rearrange("p k n -> p (k n)"), w_f[:, 0]).then_inc(whi_ok, 1)

            def split_x(i, begin=False):
                act.wait_ge(xt_mm, i + 1)
                if not begin:
                    act.wait_ge(z_mm, i)
                nc.scalar.copy(x_f[:].rearrange("p k n -> p (k n)"), p_xt[:]).then_inc(xf_ok, 1)
                act.wait_ge(xf_ok, i + 1)
                nc.scalar.copy(x_hl[:, 0], x_f[:]).then_inc(hi_ok, 1)

            def query(i):
                act.wait_ge(q_mm, i + 1)
                nc.scalar.copy(qt[:], p_q[0:ROUTER, 0:P]).then_inc(q_ok, 1)

            def weigh(i):
                act.wait_ge(pick, PICKS * i + 2)
                nc.scalar.activation(ex[:], score[:], ACT.Exp, bias=neg_max[:, 0:1]).then_inc(ex_ok, 1)

            def tile(b, t, more):
                i = TT * b + t
                if more(t + 1):
                    query(i + 1)
                act.wait_ge(zt_mm, i + 1)
                act.wait_ge(o_mm, i + 1)
                nc.scalar.copy(z_hl[:, 0].rearrange("p k n -> p (k n)"), p_zt[:]).then_inc(zhi_ok, 1)
                if more(t + 1):
                    weigh(i + 1)
                if more(t + 2):
                    split_x(i + 2)

            split_x(0, begin=True)
            act.wait_ge(w_ldb, 16)
            nc.scalar.copy(wb_hl[:, 0].rearrange("p k n -> p (k n)"), w_f[:, 1]).then_inc(whi_ok, 1)
            query(0)
            weigh(0)
            split_x(1)
            run_tiles(act, tile)

        @block.vector
        def _(dve):
            dve.memset(eps[:], LN_EPS).then_inc(eps_ok, 1)
            dve.sem_inc(res_ok, TT)

            def low_w(hl, f):
                dve.wait_ge(whi_ok, f + 1)
                dve.tensor_tensor(hl[:, 1].rearrange("p k n -> p (k n)"), w_f[:, f],
                                  hl[:, 0].rearrange("p k n -> p (k n)"), ALU.subtract).then_inc(wlo_ok, 1)

            dve.wait_ge(std_ok, 1)
            dve.reciprocal(rstd[:], std[:]).then_inc(rstd_ok, 1)
            dve.wait_ge(rstd_ok, 1)

            def norm(b, v, begin=False):
                i = TT * b + v
                dve.wait_ge(h1_ld[v % TT], 16 * (b + v // TT) + 16)
                if not begin:
                    dve.wait_ge(xt_mm, i - 1)
                dve.tensor_scalar(xln[:, v % 2], h1[:, v % TT], stats[:, bass.ds(2 * i, 1)],
                                  rstd[:, bass.ds(i, 1)], ALU.subtract, ALU.mult).then_inc(xln_ok, 1)

            def low_x(i):
                dve.wait_ge(hi_ok, i + 1)
                dve.tensor_tensor(x_hl[:, 1], x_f[:], x_hl[:, 0], ALU.subtract).then_inc(lo_ok, 1)

            def choose(i):
                def picked(k):
                    dve.wait_ge(pick, PICKS * i + k)
                    dve.sem_inc(pick_seen, 1)

                dve.wait_ge(s_mm, i + 1)
                dve.tensor_copy(score[:], p_s[:, 0:EXPERTS]).then_inc(score_ok, 1)
                dve.wait_ge(score_ok, i + 1)
                dve.sem_inc(pick_seen, 1)
                dve.max(top[:, 0], score[:]).then_inc(pick, 1)
                picked(1)
                dve.tensor_scalar(neg_max[:], top[:, 0, 0:1], -1.0, None, ALU.mult).then_inc(pick, 1)
                picked(2)
                dve.match_replace(rest[:, 0], top[:, 0], score[:], NEG).then_inc(pick, 1)
                picked(3)
                dve.max(top[:, 1], rest[:, 0]).then_inc(pick, 1)
                picked(4)
                dve.match_replace(rest[:, 1], top[:, 1], rest[:, 0], NEG).then_inc(pick, 1)
                picked(5)
                dve.tensor_scalar(chosen[:], rest[:, 1], NEG, None, ALU.is_equal).then_inc(pick, 1)
                picked(6)
                dve.wait_ge(ex_ok, i + 1)
                dve.tensor_tensor(chosen[:], chosen[:], ex[:], ALU.mult).then_inc(pick, 1)
                picked(7)
                dve.tensor_reduce(total[:], chosen[:], AX_X, ALU.add).then_inc(pick, 1)
                picked(8)
                dve.reciprocal(inv[:], total[:]).then_inc(inv_ok, 1)
                dve.wait_ge(inv_ok, i + 1)
                dve.tensor_scalar(gate[:].rearrange("p e o -> p (e o)"), chosen[:], inv[:, 0:1], SCALING,
                                  ALU.mult, ALU.mult).then_inc(gate_ok, 1)
                dve.wait_ge(gate_ok, i + 1)
                dve.wait_ge(z_mm, i + 1)
                dve.tensor_tensor(zg[:].rearrange("p (e r) -> p e r", r=RANK),
                                  p_z[:].rearrange("p (e r) -> p e r", r=RANK),
                                  gate[:].to_broadcast([P, EXPERTS, RANK]), ALU.mult).then_inc(zg_ok, 1)

            def tile(b, t, more):
                i = TT * b + t
                dve.wait_ge(zhi_ok, i + 1)
                dve.tensor_tensor(z_hl[:, 1].rearrange("p k n -> p (k n)"), p_zt[:],
                                  z_hl[:, 0].rearrange("p k n -> p (k n)"), ALU.subtract).then_inc(zlo_ok, 1)
                if more(t + 1):
                    choose(i + 1)
                if more(t + 3):
                    norm(b, t + 3)
                if more(t + 2):
                    low_x(i + 2)
                dve.wait_ge(o_mm, i + 2)
                dve.wait_ge(out_st[t % 2], 32 * b + 16 * (t // 2) + 16)
                dve.tensor_tensor(res[:, t % 2], h1[:, t % TT], p_o[:], ALU.add).then_inc(res_ok, 1)

            norm(0, 0, begin=True)
            low_w(wz_hl, 0)
            low_x(0)
            norm(0, 1, begin=True)
            low_w(wb_hl, 1)
            choose(0)
            norm(0, 2)
            low_x(1)
            run_tiles(dve, tile)


_IN = ["orig_w", "tok_row", "tok_col", "ids_row", "ids_col", "lower", "tw", "aw", "ab", "bw", "bb", "ident",
       "wpack", "par", "rms_w", "rms_mean", "wo", "wz", "wr", "keys", "wb"]


def lay_out(np, a):
    f = np.ascontiguousarray
    win = a["L0_attn_W_in"].reshape(2, DT, P, KH, P).transpose(1, 4, 3, 0, 2).reshape(DT, P, WU)
    wx = a["L0_attn_Wx"].reshape(XP, DT, P).transpose(1, 2, 0)
    wdt = np.zeros((DT, P, P), np.float32)
    wdt[:, 0:R, :] = a["L0_attn_Wdt"].reshape(DT, P, R).transpose(0, 2, 1)
    par = np.concatenate([a["L0_attn_A"], a["L0_attn_conv_w"], a["L0_attn_conv_b"][:, None],
                          a["L0_attn_dt_bias"][:, None], a["L0_attn_D_param"][:, None]], axis=1)
    mean = np.zeros((XP, XP), np.float32)
    for lo, hi in ((0, R), (R, R + N), (R + N, XP)):
        mean[lo:hi, lo:hi] = 1.0 / (hi - lo)
    return {
        "orig_w": f(a["L0_tok_orig_W"]),
        "tok_row": f(a["x"].reshape(1, BATCH * L)),
        "tok_col": f(a["x"].reshape(BATCH * TT, P).T),
        "ids_row": f(a["L0_tok_ids"].reshape(1, N_IDS)),
        "ids_col": f(a["L0_tok_ids"].reshape(N_IDS, 1)),
        "lower": np.tril(np.ones((N_IDS, N_IDS), np.float32), -1),
        "tw": f(a["L0_tok_trainable_W"].reshape(N_IDS, KH, P).transpose(2, 1, 0)),
        "aw": f(a["L0_tok_A_w"].reshape(INNER, KH, P).transpose(2, 1, 0)),
        "ab": f(a["L0_tok_A_b"].reshape(INNER, 1)),
        "bw": f(a["L0_tok_B_w"].T),
        "bb": f(a["L0_tok_B_b"].reshape(1, H)),
        "ident": np.eye(P, dtype=np.float32),
        "wpack": f(np.concatenate([win, wx, wdt], axis=2)),
        "par": f(par.reshape(DT, P, PAR)),
        "rms_w": f(np.concatenate([a["L0_attn_dt_ln_w"], a["L0_attn_b_ln_w"], a["L0_attn_c_ln_w"]]).reshape(XP, 1)),
        "rms_mean": mean,
        "wo": f(a["L0_attn_W_out"].reshape(H, DT, P).transpose(2, 1, 0)),
        "wz": f(a["L0_ffn_A_w"].reshape(BN, KH, P).transpose(2, 1, 0)),
        "wr": f(a["L0_ffn_Wq_w"].reshape(ROUTER, KH, P).transpose(2, 1, 0)),
        "keys": f(a["L0_ffn_keys"].T),
        "wb": f(a["L0_ffn_B_w"].reshape(H, KB, P).transpose(2, 1, 0)),
    }


def build(nc, io, out):
    scr = {
        "h0": nc.dram_tensor("h0_scratch", (BATCH * TT, P, H), F32).ap(),
        "xln": nc.dram_tensor("xln_scratch", (BATCH, P, 2, KH, L), F32).ap(),
        "w": nc.dram_tensor("w_scratch", (DT, P, 2, WP), F32).ap(),
        "bc": nc.dram_tensor("bc_scratch", (BATCH, 2 * N, L), F32).ap(),
        "u": nc.dram_tensor("u_scratch", (BATCH * DT, P, L), F32).ap(),
        "g": nc.dram_tensor("g_scratch", (BATCH * DT, P, L), F32).ap(),
        "y": nc.dram_tensor("y_scratch", (BATCH * DT, P, L), F32).ap(),
        "h1": nc.dram_tensor("h1_scratch", (BATCH * TT, P, H), F32).ap(),
    }
    embed_phase(nc, io, scr)
    mamba_phase(nc, io, scr)
    with nc.sbuf_tensor("stats", [P, 2 * BATCH * TT], F32) as stats:
        out_phase(nc, io, scr, stats)
        ffn_phase(nc, io, scr, stats, out)


def kernel(**inputs):
    import numpy as _np
    import concourse.bacc as _bacc
    from concourse import mybir as _mybir
    from concourse.bass_utils import run_bass_kernel_spmd as _run

    nc = _bacc.Bacc("TRN2", target_bir_lowering=False, num_devices=1)
    laid = lay_out(_np, {k: _np.asarray(v) for k, v in inputs.items()})
    arrays, io = {}, {}
    for name in _IN:
        a = laid[name]
        arrays[f"in_{name}"] = a
        io[name] = nc.dram_tensor(f"in_{name}", a.shape, _mybir.dt.from_np(a.dtype), kind="ExternalInput").ap()
    out = nc.dram_tensor("out_h", (BATCH * TT, P, H), F32, kind="ExternalOutput").ap()
    build(nc, io, out)
    r = _run(nc, [arrays], core_ids=[0])
    return r.results[0]["out_h"].reshape(BATCH, L, H)
```
